# Optimizing a Trainium2 kernel written in Bass

```python
import numpy as np
import jax
import jax.numpy as jnp

def _softmax(x, axis=-1):
    return jax.nn.softmax(x, axis=axis)

def _gelu(x):
    return jax.nn.gelu(x, approximate=True)

def _silu(x):
    return jax.nn.silu(x)

def _sigmoid(x):
    return jax.nn.sigmoid(x)

def _layernorm(x, axis=-1, eps=1e-05):
    m = jnp.mean(x, axis=axis, keepdims=True)
    v = jnp.var(x, axis=axis, keepdims=True)
    return (x - m) / jnp.sqrt(v + eps)

def _scatter_add(tgt, idx, src, axis=0):
    return tgt.at[idx].add(src)

def _segment_sum(src, seg, n):
    return jax.ops.segment_sum(src, seg, n)
kernel_name = 'mk_gps_d1_gnn_r8_a3e3ab'

def setup_inputs(seed: int=0):
    np.random.seed(seed)
    _w = jnp.asarray

    def _rec_inputs():
        import jax
        import jax.numpy as jnp
        _gk = jax.random.key(seed)
        x = -8.776e-05 + 1 * jax.random.normal(jax.random.fold_in(_gk, 1), (6250, 256), jnp.float32)
        _s = jax.random.randint(jax.random.fold_in(_gk, 2), (100000,), 0, 6250, jnp.int32)
        _d = jax.random.randint(jax.random.fold_in(_gk, 3), (100000,), 0, 6250, jnp.int32)
        _loop = jnp.arange(6250, dtype=jnp.int32)
        src = jnp.concatenate([_s, _d, _loop])
        dst = jnp.concatenate([_d, _s, _loop])
        _o = jnp.argsort(dst, stable=True)
        src = src[_o]
        dst = dst[_o]
        return (x, src, dst)
    x, src, dst = _rec_inputs()

    def _L0_gnn_setup():
        import jax, jax.numpy as jnp
        import numpy as np
        N_NODES = 2500
        N_EDGES = 40000
        D_FEAT = 256
        MID = 256
        OUT = 256

        def _coo_sum(rows, cols, msg_in, msg_out):
            msg_vect = jax.nn.relu(msg_in[rows] + msg_out[cols])
            return jnp.zeros_like(msg_out).at[rows].add(msg_vect)
        key = jax.random.key(seed)
        ks = jax.random.split(key, 16)
        s_in = 1.0 / np.sqrt(D_FEAT)
        s_mid = 1.0 / np.sqrt(2 * MID)
        inp = {'features': jax.random.normal(ks[0], (N_NODES, D_FEAT), jnp.float32), 'rows': jax.random.randint(ks[1], (N_EDGES,), 0, N_NODES, jnp.int32), 'cols': jax.random.randint(ks[2], (N_EDGES,), 0, N_NODES, jnp.int32), 'W1_1': jax.random.normal(ks[3], (D_FEAT, MID), jnp.float32) * s_in, 'b1_1': jnp.zeros((MID,), jnp.float32), 'W2_1': jax.random.normal(ks[4], (D_FEAT, MID), jnp.float32) * s_in, 'b2_1': jnp.zeros((MID,), jnp.float32), 'W1_2': jax.random.normal(ks[5], (D_FEAT, MID), jnp.float32) * s_in, 'b1_2': jnp.zeros((MID,), jnp.float32), 'W2_2': jax.random.normal(ks[6], (D_FEAT, MID), jnp.float32) * s_in, 'b2_2': jnp.zeros((MID,), jnp.float32), 'Wo': jax.random.normal(ks[7], (2 * MID, OUT), jnp.float32) * s_mid, 'bo': jnp.zeros((OUT,), jnp.float32), 'Wr': jax.random.normal(ks[8], (D_FEAT, OUT), jnp.float32) * s_in, 'br': jnp.zeros((OUT,), jnp.float32)}
        return inp
    _L0_gnn_all = _L0_gnn_setup()
    _L0_gnn_in = {k: v for k, v in _L0_gnn_all.items() if k in ('W1_1', 'b1_1', 'W2_1', 'b2_1', 'W1_2', 'b1_2', 'W2_2', 'b2_2', 'Wo', 'bo', 'Wr', 'br')}
    del _L0_gnn_all

    def _L0_mix_setup():
        import jax, jax.numpy as jnp
        import numpy as np
        import math
        EMBED = 256
        HEADS = 4
        HEAD_DIM = EMBED // HEADS
        OUT_DIM = 256
        LN_EPS = 1e-05

        def _qkv_init(key):
            spread = math.sqrt(3.0 / EMBED)
            gain, delta = (0.01, 0.01)
            w = jax.random.uniform(key, (EMBED, EMBED), minval=-spread, maxval=spread) * gain
            return w + delta * jnp.eye(EMBED, dtype=w.dtype)

        def _layer_norm(x, g, b):
            mu = jnp.mean(x, axis=-1, keepdims=True)
            var = jnp.mean(jnp.square(x - mu), axis=-1, keepdims=True)
            return (x - mu) * jax.lax.rsqrt(var + LN_EPS) * g + b

        def _split_heads(x, B, S):
            return x.reshape(B, S, HEADS, HEAD_DIM).transpose(0, 2, 1, 3)
        key = jax.random.key(seed)
        ks = jax.random.split(key, 6)
        seq = jax.random.normal(ks[0], (4, 1024, EMBED), dtype=jnp.float32)
        wq = _qkv_init(ks[1])
        wk = _qkv_init(ks[2])
        wv = _qkv_init(ks[3])
        bound = 1.0 / math.sqrt(EMBED)
        wo = jax.random.uniform(ks[4], (OUT_DIM, EMBED), minval=-bound, maxval=bound)
        bo = jax.random.uniform(ks[5], (OUT_DIM,), minval=-bound, maxval=bound)
        ln_k_g = jnp.ones((HEAD_DIM,), jnp.float32)
        ln_k_b = jnp.zeros((HEAD_DIM,), jnp.float32)
        ln_v_g = jnp.ones((HEAD_DIM,), jnp.float32)
        ln_v_b = jnp.zeros((HEAD_DIM,), jnp.float32)
        return {'seq': seq, 'wq': wq, 'wk': wk, 'wv': wv, 'wo': wo, 'bo': bo, 'ln_k_g': ln_k_g, 'ln_k_b': ln_k_b, 'ln_v_g': ln_v_g, 'ln_v_b': ln_v_b}
    _L0_mix_all = _L0_mix_setup()
    _L0_mix_in = {k: v for k, v in _L0_mix_all.items() if k in ('wq', 'wk', 'wv', 'wo', 'bo', 'ln_k_g', 'ln_k_b', 'ln_v_g', 'ln_v_b')}
    del _L0_mix_all

    def _L0_ffn_setup():
        import math
        import jax, jax.numpy as jnp
        import numpy as np
        CAPACITY_FACTOR = 1.25
        key = jax.random.key(seed)
        ks = jax.random.split(key, 5)
        B, L, D, F, E = (8, 1024, 256, 1024, 8)
        h = jax.random.normal(ks[0], (B, L, D), dtype=jnp.float32)
        gate_w = jax.random.normal(ks[1], (D, E), dtype=jnp.float32) * 0.02
        gate_b = jnp.zeros((E,), dtype=jnp.float32)
        w1 = jax.random.normal(ks[2], (E, D, F), dtype=jnp.float32) * (1.0 / math.sqrt(D))
        b1 = jnp.zeros((E, F), dtype=jnp.float32)
        w2 = jax.random.normal(ks[3], (E, F, D), dtype=jnp.float32) * (1.0 / math.sqrt(F))
        b2 = jnp.zeros((E, D), dtype=jnp.float32)
        return {'h': h, 'gate_w': gate_w, 'gate_b': gate_b, 'w1': w1, 'b1': b1, 'w2': w2, 'b2': b2}
    _L0_ffn_all = _L0_ffn_setup()
    _L0_ffn_in = {k: v for k, v in _L0_ffn_all.items() if k in ('gate_w', 'gate_b', 'w1', 'b1', 'w2', 'b2')}
    del _L0_ffn_all
    return {'x': x, 'src': src, 'dst': dst, 'L0_gnn_W1_1': _L0_gnn_in['W1_1'], 'L0_gnn_b1_1': _L0_gnn_in['b1_1'], 'L0_gnn_W2_1': _L0_gnn_in['W2_1'], 'L0_gnn_b2_1': _L0_gnn_in['b2_1'], 'L0_gnn_W1_2': _L0_gnn_in['W1_2'], 'L0_gnn_b1_2': _L0_gnn_in['b1_2'], 'L0_gnn_W2_2': _L0_gnn_in['W2_2'], 'L0_gnn_b2_2': _L0_gnn_in['b2_2'], 'L0_gnn_Wo': _L0_gnn_in['Wo'], 'L0_gnn_bo': _L0_gnn_in['bo'], 'L0_gnn_Wr': _L0_gnn_in['Wr'], 'L0_gnn_br': _L0_gnn_in['br'], 'L0_mix_wq': _L0_mix_in['wq'], 'L0_mix_wk': _L0_mix_in['wk'], 'L0_mix_wv': _L0_mix_in['wv'], 'L0_mix_wo': _L0_mix_in['wo'], 'L0_mix_bo': _L0_mix_in['bo'], 'L0_mix_ln_k_g': _L0_mix_in['ln_k_g'], 'L0_mix_ln_k_b': _L0_mix_in['ln_k_b'], 'L0_mix_ln_v_g': _L0_mix_in['ln_v_g'], 'L0_mix_ln_v_b': _L0_mix_in['ln_v_b'], 'L0_ffn_gate_w': _L0_ffn_in['gate_w'], 'L0_ffn_gate_b': _L0_ffn_in['gate_b'], 'L0_ffn_w1': _L0_ffn_in['w1'], 'L0_ffn_b1': _L0_ffn_in['b1'], 'L0_ffn_w2': _L0_ffn_in['w2'], 'L0_ffn_b2': _L0_ffn_in['b2']}

def reference(x, src, dst, L0_gnn_W1_1, L0_gnn_b1_1, L0_gnn_W2_1, L0_gnn_b2_1, L0_gnn_W1_2, L0_gnn_b1_2, L0_gnn_W2_2, L0_gnn_b2_2, L0_gnn_Wo, L0_gnn_bo, L0_gnn_Wr, L0_gnn_br, L0_mix_wq, L0_mix_wk, L0_mix_wv, L0_mix_wo, L0_mix_bo, L0_mix_ln_k_g, L0_mix_ln_k_b, L0_mix_ln_v_g, L0_mix_ln_v_b, L0_ffn_gate_w, L0_ffn_gate_b, L0_ffn_w1, L0_ffn_b1, L0_ffn_w2, L0_ffn_b2):
    import jax
    import jax.numpy as jnp

    def _L0_gnn_ref(features, rows, cols, W1_1, b1_1, W2_1, b2_1, W1_2, b1_2, W2_2, b2_2, Wo, bo, Wr, br):
        import jax, jax.numpy as jnp
        import numpy as np
        N_NODES = 2500
        N_EDGES = 40000
        D_FEAT = 256
        MID = 256
        OUT = 256

        def _coo_sum(rows, cols, msg_in, msg_out):
            msg_vect = jax.nn.relu(msg_in[rows] + msg_out[cols])
            return jnp.zeros_like(msg_out).at[rows].add(msg_vect)
        msg_1_1 = features @ W1_1 + b1_1
        msg_2_1 = features @ W2_1 + b2_1
        msg_1_2 = features @ W1_2 + b1_2
        msg_2_2 = features @ W2_2 + b2_2
        msgs_1 = _coo_sum(rows, cols, msg_1_1, msg_2_1)
        msgs_2 = _coo_sum(cols, rows, msg_1_2, msg_2_2)
        msgs = jnp.concatenate([msgs_1, msgs_2], axis=-1)
        h_2 = msgs @ Wo + bo
        h_1 = features @ Wr + br
        return jax.nn.relu(h_1 + h_2)

    def _L0_mix_ref(seq, wq, wk, wv, wo, bo, ln_k_g, ln_k_b, ln_v_g, ln_v_b):
        import jax, jax.numpy as jnp
        import numpy as np
        import math
        EMBED = 256
        HEADS = 4
        HEAD_DIM = EMBED // HEADS
        OUT_DIM = 256
        LN_EPS = 1e-05

        def _qkv_init(key):
            spread = math.sqrt(3.0 / EMBED)
            gain, delta = (0.01, 0.01)
            w = jax.random.uniform(key, (EMBED, EMBED), minval=-spread, maxval=spread) * gain
            return w + delta * jnp.eye(EMBED, dtype=w.dtype)

        def _layer_norm(x, g, b):
            mu = jnp.mean(x, axis=-1, keepdims=True)
            var = jnp.mean(jnp.square(x - mu), axis=-1, keepdims=True)
            return (x - mu) * jax.lax.rsqrt(var + LN_EPS) * g + b

        def _split_heads(x, B, S):
            return x.reshape(B, S, HEADS, HEAD_DIM).transpose(0, 2, 1, 3)
        B, S, _ = seq.shape
        q = _split_heads(seq @ wq.T, B, S)
        k = _split_heads(seq @ wk.T, B, S)
        v = _split_heads(seq @ wv.T, B, S)
        k = _layer_norm(k, ln_k_g, ln_k_b)
        v = _layer_norm(v, ln_v_g, ln_v_b)
        kv = jnp.einsum('bhsd,bhse->bhde', k, v) / S
        ga = jnp.einsum('bhsd,bhde->bhse', q, kv)
        ga = ga.transpose(0, 2, 1, 3).reshape(B, S, EMBED)
        return ga @ wo.T + bo

    def _L0_ffn_ref(h, gate_w, gate_b, w1, b1, w2, b2):
        import math
        import jax, jax.numpy as jnp
        import numpy as np
        CAPACITY_FACTOR = 1.25
        B, L, D = h.shape
        E = gate_w.shape[1]
        T = B * L
        C = max(1, math.ceil(CAPACITY_FACTOR * T / E))
        x = h.reshape(T, D)
        logits = x @ gate_w + gate_b
        probs = jax.nn.softmax(logits, axis=-1)
        idx = jnp.argmax(probs, axis=-1)
        prb = jnp.take_along_axis(probs, idx[:, None], axis=1)[:, 0]
        one_hot = jax.nn.one_hot(idx, E, dtype=jnp.float32)
        pos = (jnp.cumsum(one_hot, axis=0) * one_hot).sum(-1).astype(jnp.int32) - 1
        kept = pos < C
        pos_safe = jnp.where(kept, pos, C)
        buf = jnp.zeros((E, C, D), dtype=h.dtype).at[idx, pos_safe].set(x, mode='drop')
        hmid = jax.nn.relu(jnp.einsum('ecd,edf->ecf', buf, w1) + b1[:, None, :])
        ybuf = jnp.einsum('ecf,efd->ecd', hmid, w2) + b2[:, None, :]
        pos_g = jnp.minimum(pos, C - 1)
        y_tok = ybuf[idx, pos_g] * (prb * kept)[:, None]
        y = y_tok.reshape(B, L, D)
        y = jnp.nan_to_num(y, nan=0.0, posinf=10000.0, neginf=-10000.0)
        return y
    xn = _layernorm(x, axis=-1)
    x = x + _L0_gnn_ref(xn, src, dst, L0_gnn_W1_1, L0_gnn_b1_1, L0_gnn_W2_1, L0_gnn_b2_1, L0_gnn_W1_2, L0_gnn_b1_2, L0_gnn_W2_2, L0_gnn_b2_2, L0_gnn_Wo, L0_gnn_bo, L0_gnn_Wr, L0_gnn_br) + _L0_mix_ref(xn[None], L0_mix_wq, L0_mix_wk, L0_mix_wv, L0_mix_wo, L0_mix_bo, L0_mix_ln_k_g, L0_mix_ln_k_b, L0_mix_ln_v_g, L0_mix_ln_v_b)[0]
    x = x + _L0_ffn_ref(_layernorm(x, axis=-1)[None], L0_ffn_gate_w, L0_ffn_gate_b, L0_ffn_w1, L0_ffn_b1, L0_ffn_w2, L0_ffn_b2)[0]
    return x

_drawn_inputs = setup_inputs


def setup_inputs(seed=0):
    import zlib

    import numpy as np

    out = dict(_drawn_inputs(seed))
    spreads = {'L0_gnn_b1_1': (0.0, 0.1),
     'L0_gnn_b2_1': (0.0, 0.1),
     'L0_gnn_b1_2': (0.0, 0.1),
     'L0_gnn_b2_2': (0.0, 0.1),
     'L0_gnn_bo': (0.0, 0.8),
     'L0_gnn_br': (0.0, 0.8),
     'L0_mix_ln_k_g': (1.0, 0.6),
     'L0_mix_ln_k_b': (0.0, 0.8),
     'L0_mix_ln_v_g': (1.0, 0.6),
     'L0_mix_ln_v_b': (0.0, 0.8),
     'L0_ffn_gate_b': (0.0, 0.8),
     'L0_ffn_b1': (0.0, 0.8),
     'L0_ffn_b2': (0.0, 2.0)}
    factors = {'L0_mix_wq': 8.0,
     'L0_mix_wk': 8.0,
     'L0_mix_wv': 8.0,
     'L0_mix_wo': 8.0,
     'L0_mix_bo': 8.0,
     'L0_ffn_gate_w': 8.0,
     'L0_ffn_w1': 8.0,
     'L0_ffn_w2': 8.0}
    for name, (base, spread) in spreads.items():
        noise = np.random.default_rng([zlib.crc32(name.encode()), seed]).standard_normal(out[name].shape)
        drawn = base * np.exp(spread * noise) if base else spread * noise
        out[name] = jnp.asarray(drawn.astype(out[name].dtype))
    for name, factor in factors.items():
        out[name] = (out[name] * factor).astype(out[name].dtype)
    return out
```

```python
import concourse.bass as bass
from concourse import mybir
from contextlib import ExitStack

F32 = mybir.dt.float32
I32 = mybir.dt.int32
ALU = mybir.AluOpType
ACT = mybir.ActivationFunctionType
AXX = mybir.AxisListType.X

N = 6250
D = 256
P = 125
TT = N // P
E = 206250
NJ = N
TROWS = 6272
AROWS = TROWS + 128
U = 4
NT = 1616
NG2 = NT // (2 * U)
H, HD = 4, 64
NE, C = 8, 977
CP = 1024
JUNK = 640 + 128
NF = 1024
EPS = 1e-5


def graph_moe_kernel(nc, a, out):
    ctx = ExitStack()
    with ctx:
        def sem(name):
            return ctx.enter_context(nc.semaphore(name))

        def sb(scope, name, shape, dt=F32):
            return scope.enter_context(nc.sbuf_tensor(name, shape, dt))

        def ps(scope, name, shape):
            return scope.enter_context(nc.psum_tensor(name, shape, F32))

        def dram(name, shape):
            return nc.dram_tensor(name, shape, F32, kind="Internal").ap()

        tab_ad = dram("tab_ad", [TROWS, 2 * D])
        tab_bc = dram("tab_bc", [TROWS, 2 * D])
        acc = dram("acc", [2 * U * AROWS, D])
        buf = dram("buf", [NE * CP + JUNK, D])
        ybuf = dram("ybuf", [NE * CP, D])

        ident = sb(ctx, "ident", [128, 128])
        upper = sb(ctx, "upper", [128, 128])
        pcol_i = sb(ctx, "pcol_i", [128, 1], I32)
        pcol = sb(ctx, "pcol", [128, 1])
        x_sb = sb(ctx, "x_sb", [128, TT, D])
        keep = sb(ctx, "keep", [128, TT, D])
        mixw = sb(ctx, "mixw", [128, 2, D])
        slot_g = sb(ctx, "slot_g", [128, TT], I32)
        gate_p = sb(ctx, "gate_p", [128, TT])

        project(nc, a, sem, sb, ps, tab_ad, tab_bc, acc, buf, ident, upper, pcol_i, pcol,
                x_sb, keep, mixw)
        edges(nc, a, sem, sb, ps, tab_ad, tab_bc, acc, ident, upper, pcol)
        logits = sb(ctx, "logits", [128, TT, NE])
        nodes(nc, a, sem, sb, ps, acc, ident, x_sb, keep, mixw, logits)
        route(nc, sem, sb, ps, buf, upper, pcol, keep, logits, slot_g, gate_p)
        experts(nc, a, sem, sb, ps, buf, ybuf, ident)
        finish(nc, sem, sb, ybuf, x_sb, slot_g, gate_p, out)


def chain(eng, s, base=0):
    done = [0]

    def link(ins):
        done[0] += 1
        ins.then_inc(s, 1)
        eng.wait_ge(s, base + done[0])
    return link


def project(nc, a, sem, sb, ps, tab_ad, tab_bc, acc, buf, ident, upper, pcol_i, pcol, x_sb,
            keep, mixw):
    ZR = 5
    with ExitStack() as st:
        w = sb(st, "w", [128, 2, 6 * D])
        wq = sb(st, "wq", [128, 2, D])
        wot = sb(st, "wot", [128, 2, D])
        bias4 = sb(st, "bias4", [128, 2, 2 * D])
        lng = sb(st, "lng", [128, 2, HD])
        lnb = sb(st, "lnb", [128, 2, HD])
        zero = sb(st, "zero", [128, ZR * D])
        eps = sb(st, "eps", [128, 1])
        stats = sb(st, "stats", [128, TT, 6])
        mv = sb(st, "mv", [128, TT, 2])
        rstd = sb(st, "rstd", [128, TT])
        xn = sb(st, "xn", [128, 2, D])
        xT = sb(st, "xT", [128, 2, 2, P])
        ad = sb(st, "ad", [128, 2, 2 * D])
        bc = sb(st, "bc", [128, 2, 2 * D])
        cen = sb(st, "cen", [128, 2, 2 * D])
        sq = sb(st, "sq", [128, 2, 2 * D])
        hs = sb(st, "hs", [128, 2, 3, 8])
        kvg = sb(st, "kvg", [128, 2, 2 * D])
        kvT = sb(st, "kvT", [128, 2, 128])
        t1 = sb(st, "t1", [128, 2, D])
        p_T = ps(st, "p_T", [128, 512])
        p_ad = ps(st, "p_ad", [128, 2, 512])
        p_bc = ps(st, "p_bc", [128, 2, 512])
        p_kv = ps(st, "p_kv", [128, 2, 512])
        p_sum = ps(st, "p_sum", [128, 512])

        s_x = sem("a_x")
        s_w = sem("a_w")
        s_w2 = sem("a_w2")
        s_zst = sem("a_zst")
        s_const = sem("a_const")
        s_memset = sem("a_memset")
        s_dv = sem("a_dv")
        s_stats = sem("a_stats")
        s_std0 = sem("a_std0")
        s_norm = sem("a_norm")
        s_rstd0 = sem("a_rstd0")
        s_T = sem("a_T")
        s_xT = sem("a_xT")
        s_kept = sem("a_kept")
        s_mad = sem("a_mad")
        s_mbc = sem("a_mbc")
        s_mkv = sem("a_mkv")
        s_adc = sem("a_adc")
        s_bcc = sem("a_bcc")
        s_mean = sem("a_mean")
        s_cen = sem("a_cen")
        s_sq = sem("a_sq")
        s_var = sem("a_var")
        s_std = sem("a_std")
        s_rs = sem("a_rs")
        s_kvn = sem("a_kvn")
        s_gain = sem("a_gain")
        s_kvg = sem("a_kvg")
        s_msum = sem("a_msum")
        s_fold = sem("a_fold")
        s_foldc = sem("a_foldc")
        s_stad = [sem(f"a_stad{b}") for b in range(2)]
        s_stbc = [sem(f"a_stbc{b}") for b in range(2)]

        rows_ad = tab_ad[0:N, :].rearrange("(p t) d -> p t d", t=TT)
        rows_bc = tab_bc[0:N, :].rearrange("(p t) d -> p t d", t=TT)
        parts = [("L0_gnn_W1_1", 0), ("L0_gnn_W2_2", 1), ("L0_gnn_W2_1", 2), ("L0_gnn_W1_2", 3),
                 ("wkT", 4), ("wvT", 5)]

        block = st.enter_context(nc.Block())

        @block.sync
        def _(sp):
            sp.dma_start(x_sb[0:P, :, :], a["x"].rearrange("(p t) d -> p t d", t=TT)).then_inc(s_x, 16)
            for name, c in parts:
                sp.dma_start(w[:, :, c * D:(c + 1) * D],
                             a[name].rearrange("(k p) n -> p k n", p=128)).then_inc(s_w, 16)
            for k, name in enumerate(("L0_gnn_b2_1", "L0_gnn_b1_2", "L0_gnn_b1_1", "L0_gnn_b2_2")):
                sp.dma_start(bias4[:, k // 2, (k % 2) * D:(k % 2 + 1) * D],
                             a[name].unsqueeze(0).to_broadcast([128, D])).then_inc(s_w2, 16)
            for k, name in enumerate(("L0_mix_ln_k", "L0_mix_ln_v")):
                sp.dma_start(lng[:, k, :], a[name + "_g"].unsqueeze(0).to_broadcast([128, HD])).then_inc(s_w2, 16)
                sp.dma_start(lnb[:, k, :], a[name + "_b"].unsqueeze(0).to_broadcast([128, HD])).then_inc(s_w2, 16)
            sp.dma_start(wq[:, :, :], a["L0_mix_wq"].rearrange("(k p) n -> p k n", p=128)).then_inc(s_w2, 16)
            sp.dma_start(wot[:, :, :], a["woT"].rearrange("(k p) n -> p k n", p=128)).then_inc(s_w2, 16)

            def store(i, first):
                for b in range(2):
                    sp.wait_ge(s_adc, 2 * i + b + 1)
                    sp.dma_start(rows_ad[:, bass.ds(2 * i + b, 1), :],
                                 ad[0:P, b:b + 1, :]).then_inc(s_stad[b], 16)
                    sp.wait_ge(s_bcc, 2 * i + b + 1)
                    sp.dma_start(rows_bc[:, bass.ds(2 * i + b, 1), :],
                                 bc[0:P, b:b + 1, :]).then_inc(s_stbc[b], 16)
            store(0, True)
            with sp.Fori(1, TT // 2) as i:
                store(i, False)
            for b in range(2):
                sp.wait_ge(s_stad[b], 16 * (TT // 2))
                sp.wait_ge(s_stbc[b], 16 * (TT // 2))

        @block.gpsimd
        def _(pool):
            pool.memset(ident[:, :], 1.0).then_inc(s_memset, 1)
            pool.memset(upper[:, :], 1.0).then_inc(s_memset, 1)
            pool.iota(pcol_i[:, :], pattern=[[0, 1]], base=0, channel_multiplier=1).then_inc(s_memset, 1)
            pool.wait_ge(s_memset, 3)
            pool.affine_select(out=ident[:, :], in_=ident[:, :], compare_op=ALU.is_equal, fill=0.0, base=0,
                               pattern=[[-1, 128]], channel_multiplier=1).then_inc(s_const, 1)
            pool.affine_select(out=upper[:, :], in_=upper[:, :], compare_op=ALU.is_gt, fill=0.0, base=0,
                               pattern=[[1, 128]], channel_multiplier=-1).then_inc(s_const, 1)
            pool.tensor_copy(pcol[:, :], pcol_i[:, :]).then_inc(s_const, 1)
            pool.wait_ge(s_w2, 16 * 10)

            def tile(t, b, first):
                pool.wait_ge(s_xT, t + 1)
                pool.tensor_copy(keep[:, bass.ds(t, 1), 0:2 * P],
                                 xT[:, b, :, :].rearrange("p k n -> p (k n)").unsqueeze(1)).then_inc(s_kept, 1)

            def gains(t, b):
                kv4 = kvg[0:P, b, :].rearrange("p (w h d) -> p w h d", w=2, h=H)
                pool.wait_ge(s_kvn, t + 1)
                pool.tensor_tensor(kv4, kv4, lng[0:P, :, :].unsqueeze(2).to_broadcast([P, 2, H, HD]),
                                   ALU.mult).then_inc(s_gain, 1)
                pool.wait_ge(s_gain, t + 1)
                pool.tensor_tensor(kv4, kv4, lnb[0:P, :, :].unsqueeze(2).to_broadcast([P, 2, H, HD]),
                                   ALU.add).then_inc(s_kvg, 1)
            tile(0, 0, True)
            tile(1, 1, True)
            gains(0, 0)
            with pool.Fori(1, TT // 2) as i:
                for b in range(2):
                    tile(2 * i + b, b, False)
                    gains(2 * i + b - 1, 1 - b)
            gains(TT - 1, 1)

        @block.scalar
        def _(act):
            act.wait_ge(s_dv, 1)
            acc_z = acc.rearrange("(p k r) d -> p k (r d)", p=128, r=ZR)
            nz = acc_z.shape[1] // (2 * U)
            for c in range(2 * U):
                act.dma_start(acc_z[:, c * nz:(c + 1) * nz, :], zero[:, :].unsqueeze(1).to_broadcast([128, nz, ZR * D])
                              ).then_inc(s_zst, 16)
            act.dma_start(buf.rearrange("(p k r) d -> p k (r d)", p=128, r=ZR),
                          zero[:, :].unsqueeze(1).to_broadcast([128, (NE * CP + JUNK) // 128 // ZR, ZR * D])
                          ).then_inc(s_zst, 16)
            for t in (tab_ad, tab_bc):
                act.dma_start(t[N:TROWS, :], zero[0:TROWS - N, 0:2 * D]).then_inc(s_zst, 16)
            act.wait_ge(s_stats, 6)
            nc.scalar.activation(rstd[0:P, :], mv[0:P, :, 1], ACT.Sqrt, bias=eps[0:P, :]).then_inc(s_std0, 1)

            def transposed(t, b, first):
                act.wait_ge(s_T, t + 1)
                if not first:
                    act.wait_ge(s_mkv, t - 1)
                    act.wait_ge(s_kept, t - 1)
                nc.scalar.copy(xT[:, b, :, :].rearrange("p k n -> p (k n)"), p_T[:, 0:2 * P]).then_inc(s_xT, 1)

            def evacuate(t, b, first):
                act.wait_ge(s_mad, t + 1)
                if not first:
                    act.wait_ge(s_stad[b], 8 * t - 8 * b)
                nc.scalar.copy(ad[0:P, b, :], p_ad[0:P, b, :]).then_inc(s_adc, 1)
                act.wait_ge(s_cen, t + 1)
                nc.scalar.activation(sq[0:P, b, :], cen[0:P, b, :], ACT.Square).then_inc(s_sq, 1)
                act.wait_ge(s_var, t + 1)
                nc.scalar.activation(hs[0:P, b, 2, :], hs[0:P, b, 1, :], ACT.Sqrt, bias=eps[0:P, :],
                                     scale=1.0 / HD).then_inc(s_std, 1)
            transposed(0, 0, True)
            transposed(1, 1, True)
            evacuate(0, 0, True)
            transposed(2, 0, False)
            evacuate(1, 1, True)
            transposed(3, 1, False)
            with act.Fori(1, TT // 2 - 1) as i:
                for b in range(2):
                    evacuate(2 * i + b, b, False)
                    transposed(2 * i + b + 2, b, False)
            evacuate(TT - 2, 0, False)
            evacuate(TT - 1, 1, False)
            act.wait_ge(s_zst, 16 * (2 * U + 3))

        @block.vector
        def _(dve):
            nc.vector.memset(zero[:, :], 0.0).then_inc(s_dv, 1)
            nc.vector.memset(eps[:, :], EPS).then_inc(s_dv, 1)
            dve.wait_ge(s_x, 16)
            with dve.Fori(0, TT) as t:
                nc.vector.bn_stats(stats[0:P, bass.ds(t, 1), :], x_sb[0:P, bass.ds(t, 1), :]).then_inc(s_rstd0, 1)
            dve.wait_ge(s_rstd0, TT)
            even, odd = stats[0:P, :, 0:3], stats[0:P, :, 3:6]
            nc.vector.tensor_tensor(mv[0:P, :, :], even[:, :, 1:3], odd[:, :, 1:3], ALU.add).then_inc(s_stats, 1)
            nc.vector.tensor_tensor(rstd[0:P, :], even[:, :, 1], odd[:, :, 1], ALU.subtract).then_inc(s_stats, 1)
            dve.wait_ge(s_stats, 2)
            nc.vector.tensor_tensor(rstd[0:P, :], rstd[0:P, :], rstd[0:P, :], ALU.mult).then_inc(s_stats, 1)
            nc.vector.tensor_scalar_mul(mv[0:P, :, 0], mv[0:P, :, 0], 0.5).then_inc(s_stats, 1)
            dve.wait_ge(s_stats, 4)
            nc.vector.tensor_scalar_mul(mv[0:P, :, 1], mv[0:P, :, 1], 1.0 / D).then_inc(s_stats, 1)
            dve.wait_ge(s_stats, 5)
            nc.vector.scalar_tensor_tensor(mv[0:P, :, 1], rstd[0:P, :], 0.25, mv[0:P, :, 1], ALU.mult, ALU.add
                                           ).then_inc(s_stats, 1)
            dve.wait_ge(s_std0, 1)
            nc.vector.reciprocal(rstd[0:P, :], rstd[0:P, :]).then_inc(s_rstd0, 1)
            dve.wait_ge(s_rstd0, TT + 1)
            dve.wait_ge(s_w2, 16 * 10)
            nc.vector.tensor_tensor(bias4[:, 0, :], bias4[:, 0, :], bias4[:, 1, :], ALU.add).then_inc(s_rstd0, 1)
            dve.wait_ge(s_rstd0, TT + 2)

            def normalise(t, b, first):
                if not first:
                    dve.wait_ge(s_T, t - 1)
                nc.vector.tensor_scalar(xn[0:P, b:b + 1, :], x_sb[0:P, bass.ds(t, 1), :],
                                        mv[0:P, bass.ds(t, 1), 0], rstd[0:P, bass.ds(t, 1)],
                                        ALU.subtract, ALU.mult).then_inc(s_norm, 1)

            def heads(t, b, first):
                kv8 = p_kv[0:P, b, :].rearrange("p (g d) -> p g d", d=HD)
                cen8 = cen[0:P, b, :].rearrange("p (g d) -> p g d", d=HD)
                sq8 = sq[0:P, b, :].rearrange("p (g d) -> p g d", d=HD)
                out8 = kvg[0:P, b, :].rearrange("p (g d) -> p g d", d=HD)

                def wide(v):
                    return v.unsqueeze(2).to_broadcast([P, 8, HD])
                dve.wait_ge(s_mkv, t + 1)
                nc.vector.tensor_reduce(hs[0:P, b, 0, :], kv8, AXX, ALU.add).then_inc(s_mean, 1)
                dve.wait_ge(s_mean, 2 * t + 1)
                nc.vector.tensor_scalar_mul(hs[0:P, b, 0, :], hs[0:P, b, 0, :], 1.0 / HD).then_inc(s_mean, 1)
                dve.wait_ge(s_mean, 2 * t + 2)
                nc.vector.tensor_tensor(cen8, kv8, wide(hs[0:P, b, 0, :]), ALU.subtract).then_inc(s_cen, 1)
                dve.wait_ge(s_mbc, t + 1)
                if not first:
                    dve.wait_ge(s_stbc[b], 8 * t - 8 * b)
                nc.vector.tensor_tensor(bc[0:P, b, :], p_bc[0:P, b, :], bias4[0:P, 0, :], ALU.add).then_inc(s_bcc, 1)
                dve.wait_ge(s_sq, t + 1)
                nc.vector.tensor_reduce(hs[0:P, b, 1, :], sq8, AXX, ALU.add).then_inc(s_var, 1)
                dve.wait_ge(s_std, t + 1)
                nc.vector.reciprocal(hs[0:P, b, 2, :], hs[0:P, b, 2, :]).then_inc(s_rs, 1)
                dve.wait_ge(s_rs, t + 1)
                if not first:
                    dve.wait_ge(s_msum, t - 1)
                nc.vector.tensor_tensor(out8, cen8, wide(hs[0:P, b, 2, :]), ALU.mult).then_inc(s_kvn, 1)
            normalise(0, 0, True)
            normalise(1, 1, True)
            normalise(2, 0, False)
            heads(0, 0, True)
            normalise(3, 1, False)
            heads(1, 1, True)
            with dve.Fori(1, TT // 2 - 1) as i:
                for b in range(2):
                    normalise(2 * i + b + 2, b, False)
                    heads(2 * i + b, b, False)
            heads(TT - 2, 0, False)
            heads(TT - 1, 1, False)

            nc.vector.memset(kvT[:, :, :], 0.0).then_inc(s_dv, 1)
            dve.wait_ge(s_dv, 3)
            dve.wait_ge(s_msum, TT + 1)
            for hp in range(2):
                for h in range(2):
                    r = slice(h * HD, (h + 1) * HD)
                    nc.vector.tensor_scalar_mul(kvT[r, hp, r], p_sum[r, hp * 128 + h * HD:hp * 128 + (h + 1) * HD],
                                                1.0 / N).then_inc(s_foldc, 1)
            dve.wait_ge(s_fold, 1)
            nc.vector.tensor_copy(t1[:, :, :].rearrange("p k n -> p (k n)"), p_ad[:, 0, :]).then_inc(s_foldc, 1)
            dve.wait_ge(s_fold, 2)
            nc.vector.tensor_copy(mixw[:, :, :].rearrange("p k n -> p (k n)"), p_bc[:, 0, :]).then_inc(s_foldc, 1)

        @block.tensor
        def _(pe):
            pe.wait_ge(s_const, 3)
            pe.wait_ge(s_w, 16 * 6)
            pe.wait_ge(s_dv, 1)
            nc.tensor.matmul(p_sum[:, 0:256], zero[:, 0:128], zero[:, 0:256], start=True, stop=False)

            def transposes(t, b, first):
                pe.wait_ge(s_norm, t + 1)
                if not (first and t == 0):
                    pe.wait_ge(s_xT, t)
                for k in range(2):
                    last = nc.tensor.transpose(p_T[:, k * P:(k + 1) * P], xn[0:P, b, k * 128:(k + 1) * 128],
                                               ident[0:P, 0:P])
                last.then_inc(s_T, 1)

            def products(t, b, first):
                pe.wait_ge(s_xT, t + 1)
                for pt, c, done, free in ((p_ad, 0, s_mad, s_adc), (p_bc, 2, s_mbc, s_bcc), (p_kv, 4, s_mkv, s_cen)):
                    if not first:
                        pe.wait_ge(free, t - 1)
                    for k in range(2):
                        last = nc.tensor.matmul(pt[0:P, b, :], xT[:, b, k, :], w[:, k, c * D:(c + 2) * D],
                                                start=(k == 0), stop=(k == 1))
                    last.then_inc(done, 1)

            def sums(t, b, stop=False):
                pe.wait_ge(s_kvg, t + 1)
                for hp in range(2):
                    last = nc.tensor.matmul(p_sum[:, hp * 128:(hp + 1) * 128],
                                            kvg[0:P, b, D + hp * 128:D + (hp + 1) * 128],
                                            kvg[0:P, b, hp * 128:(hp + 1) * 128], start=False, stop=False)
                last.then_inc(s_msum, 1)
            transposes(0, 0, True)
            transposes(1, 1, True)
            products(0, 0, True)
            transposes(2, 0, False)
            products(1, 1, True)
            sums(0, 0)
            transposes(3, 1, False)
            with pe.Fori(1, TT // 2 - 1) as i:
                for b in range(2):
                    products(2 * i + b, b, False)
                    sums(2 * i + b - 1, 1 - b)
                    transposes(2 * i + b + 2, b, False)
            products(TT - 2, 0, False)
            sums(TT - 3, 1)
            products(TT - 1, 1, False)
            sums(TT - 2, 0)
            sums(TT - 1, 1)
            nc.tensor.matmul(p_sum[:, 0:256], zero[:, 0:128], zero[:, 0:256], start=False, stop=True).then_inc(s_msum, 1)
            pe.wait_ge(s_foldc, 4)
            pe.wait_ge(s_adc, TT)
            pe.wait_ge(s_bcc, TT)
            pe.wait_ge(s_w2, 16 * 10)
            for hp in range(2):
                last = nc.tensor.matmul(p_ad[:, 0, hp * D:(hp + 1) * D], kvT[:, hp, :], wot[:, hp, :],
                                        start=True, stop=True)
            last.then_inc(s_fold, 1)
            pe.wait_ge(s_foldc, 5)
            for m in range(2):
                for k in range(2):
                    last = nc.tensor.matmul(p_bc[:, 0, m * D:(m + 1) * D], wq[:, k, m * 128:(m + 1) * 128],
                                            t1[:, k, :], start=(k == 0), stop=(k == 1))
            last.then_inc(s_fold, 1)


def edges(nc, a, sem, sb, ps, tab_ad, tab_bc, acc, ident, upper, pcol):
    G = 2 * U
    RG = (NT + 127) // 128
    full = E // 128
    with ExitStack() as st:
        ids = sb(st, "ids", [128, NT, 2])
        raw = sb(st, "raw", [128, 2, 128], I32)
        rawf = sb(st, "rawf", [128, 2, 128])
        idf = sb(st, "idf", [128, 2, G])
        gidx = sb(st, "gidx", [128, 2, G], I32)
        sidx = sb(st, "sidx", [128, 2, G], I32)
        same = sb(st, "same", [128, 2, G, 128])
        later = sb(st, "later", [128, G, 128])
        small = sb(st, "small", [128, 2, 2, G])
        copy_row = sb(st, "copy_row", [128, G])
        junk = sb(st, "junk", [128, G])
        g_ad = sb(st, "g_ad", [128, 2, U, 2 * D])
        g_bc = sb(st, "g_bc", [128, U, 2 * D])
        res = sb(st, "res", [128, 2 * U, 2, D])
        p_row = ps(st, "p_row", [128, G, 128])
        p_res = ps(st, "p_res", [128, U, 512])

        s_raw = sem("e_raw")
        s_rawm = sem("e_rawm")
        s_rawf = sem("e_rawf")
        s_rawT = sem("e_rawT")
        s_ids = sem("e_ids")
        s_idx = sem("e_idx")
        s_turn = sem("e_turn")
        s_row = sem("e_row")
        s_same = sem("e_same")
        s_small = sem("e_small")
        s_sidx = sem("e_sidx")
        s_gad = [sem(f"e_gad{b}") for b in range(2)]
        s_gbc = [sem(f"e_gbc{b}") for b in range(2)]
        s_add = sem("e_add")
        s_relu = sem("e_relu")
        s_sum = sem("e_sum")
        s_res = sem("e_res")
        s_scat = [sem(f"e_scat{b}") for b in range(2)]

        block = st.enter_context(nc.Block())

        @block.sync
        def _(sp):
            for g in range(RG):
                r0, r1 = g * 128, min((g + 1) * 128, full)
                if g == 0:
                    sp.wait_ge(s_rawm, 1)
                else:
                    sp.wait_ge(s_rawm, g + 1)
                for k, name in enumerate(("src", "dst")):
                    sp.dma_start(raw[0:r1 - r0, k, :],
                                 a[name][r0 * 128:r1 * 128].rearrange("(r e) -> r e", e=128)).then_inc(s_raw, 16)
                    if g == RG - 1:
                        sp.dma_start(raw[r1 - r0:r1 - r0 + 1, k, 0:E - full * 128],
                                     a[name][full * 128:E].unsqueeze(0)).then_inc(s_raw, 16)

        @block.gpsimd
        def _(pool):
            def gathers(q, b, first):
                pool.wait_ge(s_idx, q + 1)
                if first != 0:
                    pool.wait_ge(s_add, q)
                if first == 2:
                    pool.wait_ge(s_sum, U * (q - 1))
                pool.sem_inc(s_turn)
                for u in range(U):
                    pool.indirect_dma_start(g_ad[:, b, u, :], None, tab_ad,
                                            bass.IndirectOffsetOnAxis(gidx[:, b, 2 * u:2 * u + 1], 0)
                                            ).then_inc(s_gad[b], 16)
                    pool.indirect_dma_start(g_bc[:, u, :], None, tab_bc,
                                            bass.IndirectOffsetOnAxis(gidx[:, b, 2 * u + 1:2 * u + 2], 0)
                                            ).then_inc(s_gbc[b], 16)

            def scatters(q, b, h, first):
                pool.wait_ge(s_sidx, q + 1)
                pool.wait_ge(s_res, U * (q + 1))
                if not first:
                    pool.wait_ge(s_scat[1 - b], h)
                pool.sem_inc(s_turn)
                for u in range(U):
                    pool.indirect_dma_start(acc, bass.IndirectOffsetOnAxis(sidx[:, b, 2 * u:2 * u + 1], 0),
                                            res[:, b * U + u, 0, :], None, compute_op=ALU.add
                                            ).then_inc(s_scat[b], 16)
                    pool.indirect_dma_start(acc, bass.IndirectOffsetOnAxis(sidx[:, b, 2 * u + 1:2 * u + 2], 0),
                                            res[:, b * U + u, 1, :], None, compute_op=ALU.add
                                            ).then_inc(s_scat[b], 16)
            per = 16 * G
            gathers(0, 0, 0)
            gathers(1, 1, 1)
            scatters(0, 0, 0, True)
            with pool.Fori(1, NG2) as i:
                gathers(2 * i, 0, 2)
                scatters(2 * i - 1, 1, per * i, False)
                gathers(2 * i + 1, 1, 2)
                scatters(2 * i, 0, per * i, False)
            scatters(2 * NG2 - 1, 1, per * NG2, False)
            pool.wait_ge(s_scat[0], per * NG2)
            pool.wait_ge(s_scat[1], per * NG2)

        @block.vector
        def _(dve):
            nc.vector.memset(raw[:, :, :], NJ).then_inc(s_rawm, 1)
            for g in range(RG):
                dve.wait_ge(s_raw, 32 * (g + 1) + (32 if g == RG - 1 else 0))
                if g:
                    dve.wait_ge(s_rawT, g)
                nc.vector.tensor_copy(rawf[:, :, :], raw[:, :, :]).then_inc(s_rawf, 1)
                dve.wait_ge(s_rawf, g + 1)
                if g < RG - 1:
                    nc.vector.memset(raw[:, :, :], NJ).then_inc(s_rawm, 1)
                w = min(128, NT - g * 128)
                dve.wait_ge(s_rawT, g + 1)
                nc.vector.tensor_copy(ids[:, g * 128:g * 128 + w, :].rearrange("p t k -> p k t"),
                                      p_row[:, 0:2, 0:w]).then_inc(s_ids, 1)
            dve.wait_ge(s_ids, RG)

            def indices(q, b, first):
                if not first:
                    dve.wait_ge(s_row, q - 1)
                    dve.wait_ge(s_add, q - 1)
                src = ids[:, bass.ds(U * q, U), :].rearrange("p t k -> p (t k)")
                nc.vector.tensor_copy(gidx[:, b, :], src)
                nc.vector.tensor_tensor(idf[:, b, :], src, copy_row[:, :], ALU.add).then_inc(s_idx, 1)

            def duplicates(q, b, h, first):
                def wide(v):
                    return v.unsqueeze(2).to_broadcast([128, G, 128])
                dve.wait_ge(s_idx, q + 1)
                dve.wait_ge(s_row, q + 1)
                if not first:
                    dve.wait_ge(s_sum, U * (q - 1))
                nc.vector.tensor_tensor(same[:, b, :, :], p_row[:, :, :], wide(idf[:, b, :]), ALU.is_equal
                                        ).then_inc(s_same, 1)
                dve.wait_ge(s_same, q + 1)
                link = chain(dve, s_small, 4 * q)
                link(nc.vector.tensor_tensor(later[:, :, :], same[:, b, :, :],
                                             upper[:, :].unsqueeze(1).to_broadcast([128, G, 128]), ALU.mult))
                link(nc.vector.tensor_reduce(small[:, b, 0, :], later[:, :, :], AXX, ALU.add))
                link(nc.vector.scalar_tensor_tensor(small[:, b, 1, :], junk[:, :], 1.0, idf[:, b, :], ALU.mult, ALU.subtract))
                link(nc.vector.scalar_tensor_tensor(small[:, b, 1, :], small[:, b, 0, :], 0.0, small[:, b, 1, :],
                                                    ALU.is_gt, ALU.mult))
                if not first:
                    dve.wait_ge(s_scat[b], h)
                nc.vector.tensor_tensor(sidx[:, b, :], small[:, b, 1, :], idf[:, b, :], ALU.add).then_inc(s_sidx, 1)

            def add(q, b, h):
                dve.wait_ge(s_gad[b], h)
                dve.wait_ge(s_gbc[b], h)
                nc.vector.tensor_tensor(g_ad[:, b, :, :], g_ad[:, b, :, :], g_bc[:, :, :], ALU.add).then_inc(s_add, 1)

            for c in range(G):
                nc.vector.memset(copy_row[:, c:c + 1], float(c * AROWS)).then_inc(s_ids, 1)
            dve.wait_ge(s_ids, RG + G)
            nc.vector.tensor_scalar(junk[:, :], copy_row[:, :], pcol[:, :], float(TROWS), ALU.add, ALU.add
                                    ).then_inc(s_ids, 1)
            dve.wait_ge(s_ids, RG + G + 1)
            one = 16 * U
            indices(0, 0, True)
            indices(1, 1, True)
            duplicates(0, 0, 0, True)
            add(0, 0, one)
            indices(2, 0, False)
            duplicates(1, 1, 0, True)
            add(1, 1, one)
            indices(3, 1, False)
            with dve.Fori(1, NG2 - 1) as i:
                for b in range(2):
                    duplicates(2 * i + b, b, 16 * G * i, False)
                    add(2 * i + b, b, one * (i + 1))
                    indices(2 * i + b + 2, b, False)
            for b in range(2):
                duplicates(2 * (NG2 - 1) + b, b, 16 * G * (NG2 - 1), False)
                add(2 * (NG2 - 1) + b, b, one * NG2)

        @block.scalar
        def _(act):
            def group(q, b, first):
                act.wait_ge(s_add, q + 1)
                nc.scalar.activation(g_ad[:, b, :, :], g_ad[:, b, :, :], ACT.Relu).then_inc(s_relu, 1)

            def copy(q, b, h, first):
                if not first:
                    act.wait_ge(s_scat[b], h)
                for u in range(U):
                    act.wait_ge(s_sum, U * q + u + 1)
                    nc.scalar.copy(res[:, b * U + u, :, :].rearrange("p k n -> p (k n)"), p_res[:, u, :]
                                   ).then_inc(s_res, 1)
            group(0, 0, True)
            copy(0, 0, 0, True)
            group(1, 1, True)
            copy(1, 1, 0, True)
            with act.Fori(1, NG2) as i:
                for b in range(2):
                    group(2 * i + b, b, False)
                    copy(2 * i + b, b, 16 * G * i, False)

        @block.tensor
        def _(pe):
            for g in range(RG):
                pe.wait_ge(s_rawf, g + 1)
                if g:
                    pe.wait_ge(s_ids, g)
                for k in range(2):
                    last = nc.tensor.transpose(p_row[:, k, :], rawf[:, k, :], ident[:, :])
                last.then_inc(s_rawT, 1)
            pe.wait_ge(s_ids, RG)

            def rows(q, b, first):
                pe.wait_ge(s_idx, q + 1)
                if not first:
                    pe.wait_ge(s_same, q)
                for c in range(G):
                    last = nc.tensor.transpose(p_row[:, c, :], idf[:, b, c:c + 1].to_broadcast([128, 128]),
                                               ident[:, :])
                last.then_inc(s_row, 1)

            def sums(q, b, first):
                pe.wait_ge(s_same, q + 1)
                pe.wait_ge(s_relu, q + 1)
                for u in range(U):
                    if not first:
                        pe.wait_ge(s_res, U * (q - 1) + u + 1)
                    for k in range(2):
                        last = nc.tensor.matmul(p_res[:, u, k * D:(k + 1) * D], same[:, b, 2 * u + k, :],
                                                g_ad[:, b, u, k * D:(k + 1) * D], start=True, stop=True)
                    last.then_inc(s_sum, 1)
            rows(0, 0, True)
            rows(1, 1, False)
            sums(0, 0, True)
            rows(2, 0, False)
            sums(1, 1, False)
            rows(3, 1, False)
            with pe.Fori(1, NG2 - 1) as i:
                for b in range(2):
                    sums(2 * i + b, b, False)
                    rows(2 * i + b + 2, b, False)
            sums(2 * NG2 - 2, 0, False)
            sums(2 * NG2 - 1, 1, False)


def live(t):
    return not isinstance(t, int) or 0 <= t < TT


def again(t):
    return not isinstance(t, int) or t >= 2


def landed(t, b):
    return 8 * (t - b) + 16


def pipeline(eng, step):
    for s in (-1, 0, 1):
        step(s, s % 2)
    with eng.Fori(1, TT // 2 - 1) as i:
        for b in range(2):
            step(2 * i + b, b)
    for s in (TT - 2, TT - 1, TT):
        step(s, s % 2)


def nodes(nc, a, sem, sb, ps, acc, ident, x_sb, keep, mixw, logits):
    with ExitStack() as st:
        wo = sb(st, "wo", [128, 4, D])
        wr = sb(st, "wr", [128, 2, D])
        gw = sb(st, "gw", [128, 2, NE])
        bh = sb(st, "bh", [128, 2, D])
        bm = sb(st, "bm", [128, D])
        bg = sb(st, "bg", [128, NE])
        eps = sb(st, "eps2", [128, 1])
        part = sb(st, "part", [128, 2, U, 2 * D])
        xc = sb(st, "xc", [128, 2, 2, P])
        mT = sb(st, "mT", [128, 2, 4, P])
        hb = sb(st, "hb", [128, 2, D])
        mb = sb(st, "mb", [128, 2, D])
        stats = sb(st, "stats2", [128, 2, 6])
        mv = sb(st, "mv2", [128, 2, 2])
        std = sb(st, "std2", [128, 2])
        x2T = sb(st, "x2T", [128, 2, 2, P])
        p_mT = ps(st, "p_mT", [128, 2, 512])
        p_h = ps(st, "p_h", [128, 2, 512])
        p_xT = ps(st, "p_xT", [128, 2, 512])
        p_g = ps(st, "p_g", [128, 2, 512])

        s_w = sem("n_w")
        s_ld = [sem(f"n_ld{b}") for b in range(2)]
        s_const = sem("n_const")
        s_half = sem("n_half")
        s_msg = sem("n_msg")
        s_xc = sem("n_xc")
        s_xb = sem("n_xb")
        s_mT = sem("n_mT")
        s_mTc = sem("n_mTc")
        s_h = sem("n_h")
        s_hb = sem("n_hb")
        s_ln = sem("n_ln")
        s_var = sem("n_var")
        s_std = sem("n_std")
        s_xn2 = sem("n_xn2")
        s_xT = sem("n_xT")
        s_xTc = sem("n_xTc")
        s_gate = sem("n_gate")
        s_lg = sem("n_lg")
        rows = acc.rearrange("(c r) d -> r c d", r=AROWS)[0:N, :, :].rearrange("(p t) c d -> p t c d", t=TT)

        block = st.enter_context(nc.Block())

        @block.sync
        def _(sp):
            sp.dma_start(wo[:, :, :], a["L0_gnn_Wo"].rearrange("(k p) n -> p k n", p=128)).then_inc(s_w, 16)
            sp.dma_start(wr[:, :, :], a["L0_gnn_Wr"].rearrange("(k p) n -> p k n", p=128)).then_inc(s_w, 16)
            sp.dma_start(gw[:, :, :], a["L0_ffn_gate_w"].rearrange("(k p) n -> p k n", p=128)).then_inc(s_w, 16)
            for dst, name, n in ((bh[:, 0, :], "L0_gnn_bo", D), (bh[:, 1, :], "L0_gnn_br", D),
                                 (bm[:, :], "L0_mix_bo", D), (bg[:, :], "L0_ffn_gate_b", NE)):
                sp.dma_start(dst, a[name].unsqueeze(0).to_broadcast([128, n])).then_inc(s_w, 16)

            def step(s, b):
                t = s + 1
                if live(t):
                    if again(t):
                        sp.wait_ge(s_mT, t - 1)
                    sp.dma_start(part[0:P, 1 - b, :, :].rearrange("p u (k d) -> p (u k) d", k=2),
                                 rows[:, bass.ds(t, 1), :, :].rearrange("p t c d -> p (t c) d")
                                 ).then_inc(s_ld[1 - b], 16)
            pipeline(sp, step)

        @block.gpsimd
        def _(pool):
            pool.wait_ge(s_w, 16 * 7)

            def step(s, b):
                if live(s):
                    if again(s):
                        pool.wait_ge(s_h, s - 1)
                    pool.tensor_copy(xc[:, b, :, :].rearrange("p k n -> p (k n)").unsqueeze(1),
                                     keep[:, bass.ds(s, 1), 0:2 * P]).then_inc(s_xc, 1)
                    pool.tensor_tensor(x_sb[0:P, bass.ds(s, 1), :], x_sb[0:P, bass.ds(s, 1), :],
                                       bm[0:P, :].unsqueeze(1), ALU.add).then_inc(s_xb, 1)
            pipeline(pool, step)

        @block.vector
        def _(dve):
            nc.vector.memset(eps[:, :], EPS).then_inc(s_const, 1)
            dve.wait_ge(s_w, 16 * 7)
            nc.vector.tensor_tensor(bh[:, 0, :], bh[:, 0, :], bh[:, 1, :], ALU.add).then_inc(s_const, 1)
            dve.wait_ge(s_const, 2)

            def message_sums(t, b):
                dve.wait_ge(s_ld[b], landed(t, b))
                nc.vector.tensor_tensor(part[0:P, b, 0:2, :], part[0:P, b, 0:2, :], part[0:P, b, 2:4, :],
                                        ALU.add).then_inc(s_half, 1)
                dve.wait_ge(s_half, t + 1)
                nc.vector.tensor_tensor(part[0:P, b, 0, :], part[0:P, b, 0, :], part[0:P, b, 1, :],
                                        ALU.add).then_inc(s_msg, 1)

            def finish_layer(t, b):
                dve.wait_ge(s_h, t + 1)
                link = chain(dve, s_ln, 5 * t)
                nc.vector.tensor_tensor(hb[0:P, b, :], p_h[0:P, b, 0:D], bh[0:P, 0, :], ALU.add).then_inc(s_hb, 1)
                dve.wait_ge(s_xb, t + 1)
                link(nc.vector.tensor_tensor(mb[0:P, b:b + 1, :], p_h[0:P, b:b + 1, D:2 * D],
                                             x_sb[0:P, bass.ds(t, 1), :], ALU.add))
                dve.wait_ge(s_hb, 2 * t + 1)
                link(nc.vector.scalar_tensor_tensor(mb[0:P, b, :], hb[0:P, b, :], 0.0, mb[0:P, b, :],
                                                    ALU.max, ALU.add))
                link(nc.vector.bn_stats(stats[0:P, b, :], mb[0:P, b, :]))
                nc.vector.tensor_scalar_mul(x_sb[0:P, bass.ds(t, 1), :], mb[0:P, b:b + 1, :], 1.0).then_inc(s_hb, 1)
                nc.vector.bn_aggr(mv[0:P, b, :], stats[0:P, b, :]).then_inc(s_var, 1)
                dve.wait_ge(s_std, t + 1)
                link(nc.vector.reciprocal(std[0:P, b:b + 1], std[0:P, b:b + 1]))
                link(nc.vector.tensor_scalar(mb[0:P, b, :], mb[0:P, b, :], mv[0:P, b, 0:1], std[0:P, b:b + 1],
                                             ALU.subtract, ALU.mult))
                dve.wait_ge(s_xc, t + 1)
                nc.vector.tensor_scalar_mul(keep[0:P, bass.ds(t, 1), :], mb[0:P, b:b + 1, :], 1.0).then_inc(s_xn2, 1)

            def step(s, b):
                if live(s + 1):
                    message_sums(s + 1, 1 - b)
                if live(s - 1):
                    dve.wait_ge(s_gate, s)
                    nc.vector.tensor_tensor(logits[0:P, bass.ds(s - 1, 1), :], p_g[0:P, 1 - b:2 - b, 0:NE],
                                            bg[0:P, :].unsqueeze(1), ALU.add).then_inc(s_lg, 1)
                if live(s):
                    if again(s):
                        dve.wait_ge(s_xT, s - 1)
                    finish_layer(s, b)
            pipeline(dve, step)

        @block.scalar
        def _(act):
            def step(s, b):
                t = s + 1
                if live(t):
                    act.wait_ge(s_mT, t + 1)
                    if again(t):
                        act.wait_ge(s_h, t - 1)
                    nc.scalar.copy(mT[:, 1 - b, :, :].rearrange("p k n -> p (k n)"), p_mT[:, 1 - b, 0:4 * P]
                                   ).then_inc(s_mTc, 1)
                t = s - 1
                if live(t):
                    act.wait_ge(s_xT, t + 1)
                    if again(t):
                        act.wait_ge(s_gate, t - 1)
                    nc.scalar.copy(x2T[:, 1 - b, :, :].rearrange("p k n -> p (k n)"), p_xT[:, 1 - b, 0:2 * P]
                                   ).then_inc(s_xTc, 1)
                if live(s):
                    act.wait_ge(s_var, s + 1)
                    nc.scalar.activation(std[0:P, b:b + 1], mv[0:P, b, 1:2], ACT.Sqrt, bias=eps[0:P, :]
                                         ).then_inc(s_std, 1)
            act.wait_ge(s_const, 2)
            pipeline(act, step)

        @block.tensor
        def _(pe):
            pe.wait_ge(s_w, 16 * 7)

            def step(s, b):
                t = s + 1
                if live(t):
                    pe.wait_ge(s_msg, t + 1)
                    if again(t):
                        pe.wait_ge(s_mTc, t - 1)
                    for k in range(4):
                        last = nc.tensor.transpose(p_mT[:, 1 - b, k * P:(k + 1) * P],
                                                   part[0:P, 1 - b, 0, k * 128:(k + 1) * 128], ident[0:P, 0:P])
                    last.then_inc(s_mT, 1)
                t = s - 1
                if live(t):
                    pe.wait_ge(s_xn2, t + 1)
                    if again(t):
                        pe.wait_ge(s_xTc, t - 1)
                    for k in range(2):
                        last = nc.tensor.transpose(p_xT[:, 1 - b, k * P:(k + 1) * P],
                                                   mb[0:P, 1 - b, k * 128:(k + 1) * 128], ident[0:P, 0:P])
                    last.then_inc(s_xT, 1)
                if live(s):
                    pe.wait_ge(s_mTc, s + 1)
                    pe.wait_ge(s_xc, s + 1)
                    if again(s):
                        pe.wait_ge(s_hb, 2 * s - 2)
                        pe.wait_ge(s_ln, 5 * s - 9)
                    for k in range(6):
                        nc.tensor.matmul(p_h[0:P, b, 0:D], mT[:, b, k, :] if k < 4 else xc[:, b, k - 4, :],
                                         wo[:, k, :] if k < 4 else wr[:, k - 4, :], start=(k == 0), stop=(k == 5))
                    for k in range(2):
                        last = nc.tensor.matmul(p_h[0:P, b, D:2 * D], xc[:, b, k, :], mixw[:, k, :],
                                                start=(k == 0), stop=(k == 1))
                    last.then_inc(s_h, 1)
                if live(t):
                    pe.wait_ge(s_xTc, t + 1)
                    if again(t):
                        pe.wait_ge(s_lg, t - 1)
                    for k in range(2):
                        last = nc.tensor.matmul(p_g[0:P, 1 - b, 0:NE], x2T[:, 1 - b, k, :], gw[:, k, :],
                                                start=(k == 0), stop=(k == 1))
                    last.then_inc(s_gate, 1)
            pipeline(pe, step)


def route(nc, sem, sb, ps, buf, upper, pcol, keep, logits, slot_g, gate_p):
    with ExitStack() as st:
        probs = sb(st, "probs", [128, TT, NE])
        hot = sb(st, "hot", [128, TT, NE])
        before = sb(st, "before", [128, TT, NE])
        tmp = sb(st, "tmp", [128, TT, NE])
        ones = sb(st, "ones", [128, TT])
        rank = sb(st, "rank", [128, 2, NE])
        col = sb(st, "col", [128, 5, TT])
        junk = sb(st, "junk2", [128, TT])
        offs = sb(st, "offs", [128, NE])
        dest = sb(st, "dest", [128, TT])
        dslot = sb(st, "dslot", [128, 2], I32)
        rowst = sb(st, "rowst", [128, 2, D])
        p_off = ps(st, "p_off", [128, 512])
        s_c = sem("r_chain")
        s_shift = sem("r_shift")
        s_exp = sem("r_exp")
        s_tot = sem("r_tot")
        s_off = sem("r_off")
        s_stage = sem("r_stage")
        s_turn = sem("r_turn")
        s_sc = [sem(f"r_sc{b}") for b in range(2)]

        block = st.enter_context(nc.Block())

        @block.scalar
        def _(act):
            act.wait_ge(s_shift, 1)
            nc.scalar.activation(probs[0:P, :, :], tmp[0:P, :, :], ACT.Exp).then_inc(s_exp, 1)

        @block.tensor
        def _(pe):
            pe.wait_ge(s_tot, 1)
            nc.tensor.matmul(p_off[0:P, 0:NE], upper[0:P, 0:P], before[0:P, TT - 1, :], start=True, stop=True
                             ).then_inc(s_off, 1)

        @block.vector
        def _(dve):
            link = chain(dve, s_c)
            V = nc.vector
            top, total, pos, base, kept = (col[0:P, k, :] for k in range(5))
            lg, pr, ht, bf, tm = (x[0:P, :, :] for x in (logits, probs, hot, before, tmp))

            def wide(v):
                return v.unsqueeze(2).to_broadcast([P, TT, NE])
            for e in range(NE):
                link(V.memset(rank[:, 0, e:e + 1], float(NE - e)))
                link(V.memset(rank[:, 1, e:e + 1], float(e * CP)))
            link(V.memset(ones[:, :], 1.0))
            for b in range(2):
                link(V.memset(junk[:, b::2], float(NE * CP + 128 * b)))
            link(V.tensor_scalar_add(junk[:, :], junk[:, :], pcol[:, :]))
            link(V.tensor_reduce(top, lg, AXX, ALU.max))
            V.tensor_tensor(tm, lg, wide(top), ALU.subtract).then_inc(s_shift, 1)
            dve.wait_ge(s_exp, 1)
            link(V.tensor_reduce(total, pr, AXX, ALU.add))
            link(V.reciprocal(total, total))
            link(V.tensor_tensor(pr, pr, wide(total), ALU.mult))
            link(V.tensor_reduce(top, pr, AXX, ALU.max))
            link(V.tensor_tensor(tm, pr, wide(top), ALU.is_equal))
            link(V.tensor_tensor(tm, tm, rank[0:P, 0:1, :].to_broadcast([P, TT, NE]), ALU.mult))
            link(V.tensor_reduce(pos, tm, AXX, ALU.max))
            link(V.tensor_tensor(ht, tm, wide(pos), ALU.is_equal))
            for e in range(NE):
                last = V.tensor_tensor_scan(before[0:P, :, e], ones[0:P, :], hot[0:P, :, e], 0.0, ALU.mult, ALU.add)
            last.then_inc(s_tot, 1)
            dve.wait_ge(s_off, 1)
            link(V.tensor_copy(offs[0:P, :], p_off[0:P, 0:NE]))
            link(V.tensor_tensor(tm, bf, offs[0:P, :].unsqueeze(1).to_broadcast([P, TT, NE]), ALU.add))
            link(V.tensor_tensor(tm, tm, ht, ALU.mult))
            link(V.tensor_reduce(pos, tm, AXX, ALU.add))
            link(V.tensor_tensor(tm, ht, rank[0:P, 1:2, :].to_broadcast([P, TT, NE]), ALU.mult))
            link(V.tensor_reduce(base, tm, AXX, ALU.add))
            link(V.tensor_scalar(kept, pos, float(C), None, ALU.is_le))
            link(V.tensor_tensor(gate_p[0:P, :], top, kept, ALU.mult))
            link(V.tensor_tensor(dest[0:P, :], base, pos, ALU.add))
            link(V.scalar_tensor_tensor(dest[0:P, :], dest[0:P, :], -1.0, junk[0:P, :], ALU.add, ALU.subtract))
            link(V.tensor_tensor(dest[0:P, :], dest[0:P, :], kept, ALU.mult))
            link(V.tensor_tensor(dest[0:P, :], dest[0:P, :], junk[0:P, :], ALU.add))
            link(V.tensor_scalar(pos, pos, float(C), -1.0, ALU.min, ALU.add))
            link(V.tensor_tensor(slot_g[0:P, :], base, pos, ALU.add))

            def stage(t, b, h):
                if again(t):
                    dve.wait_ge(s_sc[b], h)
                V.tensor_copy(dslot[0:P, b:b + 1], dest[0:P, bass.ds(t, 1)])
                V.tensor_copy(rowst[0:P, b:b + 1, :], keep[0:P, bass.ds(t, 1), :]).then_inc(s_stage, 1)
            stage(0, 0, 0)
            stage(1, 1, 0)
            with dve.Fori(1, TT // 2) as i:
                for b in range(2):
                    stage(2 * i + b, b, 16 * i)

        @block.gpsimd
        def _(pool):
            with pool.Fori(0, TT // 2) as i:
                for b in range(2):
                    pool.wait_ge(s_stage, 2 * i + b + 1)
                    pool.sem_inc(s_turn)
                    pool.indirect_dma_start(buf, bass.IndirectOffsetOnAxis(dslot[0:P, b:b + 1], 0),
                                            rowst[0:P, b, :], None).then_inc(s_sc[b], 16)
            pool.wait_ge(s_sc[0], 16 * (TT // 2))
            pool.wait_ge(s_sc[1], 16 * (TT // 2))


def experts(nc, a, sem, sb, ps, buf, ybuf, ident):
    J = CP // 128
    F = NF // 128
    with ExitStack() as st:
        w1 = sb(st, "w1", [128, 2, 2, NF])
        w2 = sb(st, "w2", [128, 2, F, D])
        b2 = sb(st, "b2", [128, 2, D])
        tok = sb(st, "tok", [128, J, D])
        tokT = sb(st, "tokT", [128, 2, CP])
        hT = sb(st, "hT", [128, F, CP])
        y = sb(st, "y", [128, J, D])
        b1r = sb(st, "b1r", [NE * F, 128])
        b1T = sb(st, "b1T", [128, NE * F])
        b1c = sb(st, "b1c", [128, F])
        p_t = ps(st, "p_t", [128, 2, 512])
        p_h = ps(st, "p_hid", [128, 4, 512])
        p_y = ps(st, "p_y", [128, 2, 512])

        s_b1 = sem("x_b1")
        s_b1T = sem("x_b1T")
        s_b1c = sem("x_b1c")
        s_w = [sem(f"x_w{b}") for b in range(2)]
        s_tok = sem("x_tok")
        s_T = sem("x_T")
        s_Tc = sem("x_Tc")
        s_h = sem("x_h")
        s_hr = sem("x_hr")
        s_y = sem("x_y")
        s_yc = sem("x_yc")
        s_st = sem("x_st")
        tok_d = buf[0:NE * CP, :].rearrange("(e p j) d -> p e j d", p=128, j=J)
        y_d = ybuf.rearrange("(e p j) d -> p e j d", p=128, j=J)
        w1_d = a["L0_ffn_w1"].rearrange("e (k p) f -> p e k f", p=128)
        w2_d = a["L0_ffn_w2"].rearrange("e (f p) d -> p e f d", p=128)
        GH = 2 * F

        block = st.enter_context(nc.Block())

        @block.sync
        def _(sp):
            sp.dma_start(b1r[:, :], a["L0_ffn_b1"].rearrange("e (f p) -> (e f) p", p=128)).then_inc(s_b1, 16)

            def load(e, b, first):
                if not first:
                    sp.wait_ge(s_T, 4 * e)
                sp.dma_start(tok[:, :, :].unsqueeze(1), tok_d[:, bass.ds(e, 1), :, :]).then_inc(s_tok, 16)
                if not first:
                    sp.wait_ge(s_yc, J * (e - 1))
                sp.dma_start(w1[:, b:b + 1, :, :], w1_d[:, bass.ds(e, 1), :, :]).then_inc(s_w[b], 16)
                sp.dma_start(w2[:, b:b + 1, :, :], w2_d[:, bass.ds(e, 1), :, :]).then_inc(s_w[b], 16)
                sp.dma_start(b2[:, b:b + 1, :], a["L0_ffn_b2"][bass.ds(e, 1), :].unsqueeze(0).to_broadcast([128, 1, D])
                             ).then_inc(s_w[b], 16)
            load(0, 0, True)
            sp.wait_ge(s_T, 4)
            sp.dma_start(tok[:, :, :].unsqueeze(1), tok_d[:, 1:2, :, :]).then_inc(s_tok, 16)
            sp.dma_start(w1[:, 1:2, :, :], w1_d[:, 1:2, :, :]).then_inc(s_w[1], 16)
            sp.dma_start(w2[:, 1:2, :, :], w2_d[:, 1:2, :, :]).then_inc(s_w[1], 16)
            sp.dma_start(b2[:, 1:2, :], a["L0_ffn_b2"][1:2, :].unsqueeze(0).to_broadcast([128, 1, D])
                         ).then_inc(s_w[1], 16)
            with sp.Fori(1, NE // 2) as i:
                for b in range(2):
                    load(2 * i + b, b, False)

        @block.gpsimd
        def _(pool):
            with pool.Fori(0, NE) as e:
                pool.wait_ge(s_yc, J * e + J)
                pool.dma_start(y_d[:, bass.ds(e, 1), :, :], y[:, :, :].unsqueeze(1)).then_inc(s_st, 16)
            pool.wait_ge(s_st, 16 * NE)

        @block.scalar
        def _(act):
            act.wait_ge(s_b1T, 2)

            def hidden(e, b, first):
                act.wait_ge(s_b1c, e + 1)
                if not first:
                    act.wait_ge(s_y, J * e)
                for g in range(GH):
                    f, half = g // 2, g % 2
                    act.wait_ge(s_h, GH * e + g + 1)
                    nc.scalar.activation(hT[:, f, half * 512:(half + 1) * 512], p_h[:, g % 4, :], ACT.Relu,
                                         bias=b1c[:, f:f + 1]).then_inc(s_hr, 1)
            hidden(0, 0, True)
            with act.Fori(1, NE) as e:
                hidden(e, 0, False)

        @block.vector
        def _(dve):
            dve.wait_ge(s_b1T, 1)
            nc.vector.tensor_copy(b1T[:, :], p_t[:, 0, 0:NE * F]).then_inc(s_b1T, 1)
            dve.wait_ge(s_b1T, 2)

            def expert(e, b, h, first):
                if not first:
                    dve.wait_ge(s_hr, GH * e)
                nc.vector.tensor_copy(b1c[:, :], b1T[:, bass.ds(F * e, F)]).then_inc(s_b1c, 1)
                for q in range(4):
                    dve.wait_ge(s_T, 4 * e + q + 1)
                    if q == 0 and not first:
                        dve.wait_ge(s_h, GH * e)
                    nc.vector.tensor_copy(tokT[:, q // 2, (q % 2) * 512:(q % 2 + 1) * 512], p_t[:, q % 2, :]
                                          ).then_inc(s_Tc, 1)
                if not first:
                    dve.wait_ge(s_st, 16 * e)
                dve.wait_ge(s_w[b], h)
                for j in range(J):
                    dve.wait_ge(s_y, J * e + j + 1)
                    nc.vector.tensor_tensor(y[:, j, :], p_y[:, j % 2, 0:D], b2[:, b, :], ALU.add).then_inc(s_yc, 1)
            expert(0, 0, 48, True)
            expert(1, 1, 48, False)
            with dve.Fori(1, NE // 2) as i:
                for b in range(2):
                    expert(2 * i + b, b, 48 * i + 48, False)

        @block.tensor
        def _(pe):
            pe.wait_ge(s_b1, 16)
            nc.tensor.transpose(p_t[:, 0, 0:NE * F], b1r[:, :], ident[0:NE * F, 0:NE * F]).then_inc(s_b1T, 1)
            pe.wait_ge(s_b1T, 2)

            def expert(e, b, h, first):
                pe.wait_ge(s_tok, 16 * e + 16)
                for q in range(4):
                    if q >= 2:
                        pe.wait_ge(s_Tc, 4 * e + q - 1)
                    elif not first:
                        pe.wait_ge(s_Tc, 4 * e + q - 1)
                    for r in range(4):
                        last = nc.tensor.transpose(p_t[:, q % 2, r * 128:(r + 1) * 128],
                                                   tok[:, (q % 2) * 4 + r, (q // 2) * 128:(q // 2 + 1) * 128],
                                                   ident[:, :])
                    last.then_inc(s_T, 1)
                pe.wait_ge(s_w[b], h)
                pe.wait_ge(s_Tc, 4 * e + 4)
                for g in range(GH):
                    f, half = g // 2, g % 2
                    if g >= 4:
                        pe.wait_ge(s_hr, GH * e + g - 3)
                    elif not first:
                        pe.wait_ge(s_hr, GH * e + g - 3)
                    for k in range(2):
                        last = nc.tensor.matmul(p_h[:, g % 4, :], w1[:, b, k, f * 128:(f + 1) * 128],
                                                tokT[:, k, half * 512:(half + 1) * 512],
                                                start=(k == 0), stop=(k == 1))
                    last.then_inc(s_h, 1)
                pe.wait_ge(s_hr, GH * e + GH)
                for j in range(J):
                    if j >= 2:
                        pe.wait_ge(s_yc, J * e + j - 1)
                    elif not first:
                        pe.wait_ge(s_yc, J * e + j - 1)
                    for f in range(F):
                        last = nc.tensor.matmul(p_y[:, j % 2, 0:D], hT[:, f, j * 128:(j + 1) * 128], w2[:, b, f, :],
                                                start=(f == 0), stop=(f == F - 1))
                    last.then_inc(s_y, 1)
            expert(0, 0, 48, True)
            expert(1, 1, 48, False)
            with pe.Fori(1, NE // 2) as i:
                for b in range(2):
                    expert(2 * i + b, b, 48 * i + 48, False)


def finish(nc, sem, sb, ybuf, x_sb, slot_g, gate_p, out):
    Q = 5
    BIG = 3.4028234e38
    with ExitStack() as st:
        islot = sb(st, "islot", [128, 2], I32)
        yg = sb(st, "yg", [128, 2, D])
        sc = sb(st, "sc", [128, 2, D])
        odd = sb(st, "odd", [128, 2, D])
        sub = sb(st, "sub", [128, 2, 2, D])
        s_i = sem("f_i")
        s_turn = sem("f_turn")
        s_g = [sem(f"f_g{b}") for b in range(2)]
        s_y = sem("f_y")
        s_odd = sem("f_odd")
        s_a = sem("f_a")
        s_sub = sem("f_sub")
        s_fix = sem("f_fix")
        s_x = sem("f_x")
        s_out = sem("f_out")
        rows = out.rearrange("(p t) d -> p t d", t=TT)
        block = st.enter_context(nc.Block())

        @block.gpsimd
        def _(pool):
            def gather(t, b):
                pool.wait_ge(s_i, t + 1)
                pool.sem_inc(s_turn)
                pool.indirect_dma_start(yg[0:P, b, :], None, ybuf,
                                        bass.IndirectOffsetOnAxis(islot[0:P, b:b + 1], 0)).then_inc(s_g[b], 16)

            def substitute(t, b):
                pool.wait_ge(s_y, t + 1)
                if again(t):
                    pool.wait_ge(s_fix, t - 1)
                pool.sem_inc(s_turn)
                pool.tensor_scalar(sub[0:P, b, 0, :], sc[0:P, b, :], BIG, 1e4, ALU.is_gt, ALU.mult).then_inc(s_a, 1)
                pool.tensor_scalar(sub[0:P, b, 1, :], sc[0:P, b, :], -BIG, -1e4, ALU.is_lt, ALU.mult).then_inc(s_a, 1)
                pool.wait_ge(s_a, 2 * t + 2)
                pool.tensor_tensor(sub[0:P, b, 0, :], sub[0:P, b, 0, :], sub[0:P, b, 1, :], ALU.add).then_inc(s_sub, 1)

            def step(s, b):
                if live(s + 1):
                    gather(s + 1, 1 - b)
                if live(s):
                    substitute(s, b)
            pipeline(pool, step)

        @block.scalar
        def _(act):
            def step(s, b):
                if live(s):
                    act.wait_ge(s_y, s + 1)
                    if again(s):
                        act.wait_ge(s_fix, s - 1)
                    nc.scalar.activation(odd[0:P, b, :], sc[0:P, b, :], ACT.Square, scale=0.0).then_inc(s_odd, 1)
            pipeline(act, step)

        @block.vector
        def _(dve):
            def step(s, b):
                t = s + 1
                if live(t):
                    if again(t):
                        dve.wait_ge(s_y, t - 1)
                    nc.vector.tensor_copy(islot[0:P, 1 - b:2 - b], slot_g[0:P, bass.ds(t, 1)]).then_inc(s_i, 1)
                if live(s):
                    dve.wait_ge(s_g[b], landed(s, b))
                    if again(s):
                        dve.wait_ge(s_x, s - 1)
                    nc.vector.tensor_scalar(sc[0:P, b, :], yg[0:P, b, :], gate_p[0:P, bass.ds(s, 1)], None, ALU.mult
                                            ).then_inc(s_y, 1)
                t = s - 1
                if live(t):
                    dve.wait_ge(s_odd, t + 1)
                    dve.wait_ge(s_sub, t + 1)
                    dve.sem_inc(s_turn)
                    nc.vector.copy_predicated(sc[0:P, 1 - b, :], odd[0:P, 1 - b, :].bitcast(I32), sub[0:P, 1 - b, 0, :]
                                              ).then_inc(s_fix, 1)
                    dve.wait_ge(s_fix, t + 1)
                    nc.vector.tensor_tensor(x_sb[0:P, bass.ds(t, 1), :], x_sb[0:P, bass.ds(t, 1), :],
                                            sc[0:P, 1 - b:2 - b, :], ALU.add).then_inc(s_x, 1)
            pipeline(dve, step)

        @block.sync
        def _(sp):
            with sp.Fori(0, TT // Q) as i:
                sp.wait_ge(s_x, Q * i + Q)
                sp.dma_start(rows[:, bass.ds(Q * i, Q), :], x_sb[0:P, bass.ds(Q * i, Q), :]).then_inc(s_out, 16)
            sp.wait_ge(s_out, 16 * (TT // Q))


_NAMES = ["x", "src", "dst", "L0_gnn_W1_1", "L0_gnn_b1_1", "L0_gnn_W2_1", "L0_gnn_b2_1", "L0_gnn_W1_2",
          "L0_gnn_b1_2", "L0_gnn_W2_2", "L0_gnn_b2_2", "L0_gnn_Wo", "L0_gnn_bo", "L0_gnn_Wr", "L0_gnn_br",
          "L0_mix_wq", "L0_mix_bo", "L0_mix_ln_k_g", "L0_mix_ln_k_b", "L0_mix_ln_v_g", "L0_mix_ln_v_b",
          "L0_ffn_gate_w", "L0_ffn_gate_b", "L0_ffn_w1", "L0_ffn_b1", "L0_ffn_w2", "L0_ffn_b2"]
_TRANSPOSED = {"wkT": "L0_mix_wk", "wvT": "L0_mix_wv", "woT": "L0_mix_wo"}


def kernel(**inputs):
    import numpy as np
    import concourse.bacc as bacc
    from concourse.bass_utils import run_bass_kernel_spmd

    nc = bacc.Bacc("TRN2", target_bir_lowering=False, num_devices=1)
    arrays = {n: np.ascontiguousarray(inputs[n]) for n in _NAMES}
    arrays |= {n: np.ascontiguousarray(np.asarray(inputs[m]).T) for n, m in _TRANSPOSED.items()}
    a = {n: nc.dram_tensor("in_" + n, v.shape, mybir.dt.from_np(v.dtype), kind="ExternalInput").ap()
         for n, v in arrays.items()}
    out = nc.dram_tensor("out", (N, D), F32, kind="ExternalOutput").ap()
    graph_moe_kernel(nc, a, out)
    r = run_bass_kernel_spmd(nc, [{"in_" + n: v for n, v in arrays.items()}], core_ids=[0])
    return r.results[0]["out"]
```

```python
import concourse.bass as bass
from concourse import mybir
from contextlib import ExitStack

F32 = mybir.dt.float32
I32 = mybir.dt.int32
BF16 = mybir.dt.bfloat16
ALU = mybir.AluOpType
ACT = mybir.ActivationFunctionType
AXX = mybir.AxisListType.X

N = 6250
D = 256
P = 125
TT = N // P
E = 206250
NJ = N
TROWS = 6400
AROWS = 6400
U = 4
NT = 1616
NQ = NT // U
WT = 2 * U
NW = NT // WT
W = 42
NACC = U + 1
H, HD = 4, 64
NE, C = 8, 977
CP = 1024
JUNK = 640 + 128
NF = 1024
EPS = 1e-5


def graph_moe_kernel(nc, a, out):
    ctx = ExitStack()
    with ctx:
        def sem(name):
            return ctx.enter_context(nc.semaphore(name))

        def sb(scope, name, shape, dt=F32):
            return scope.enter_context(nc.sbuf_tensor(name, shape, dt))

        def ps(scope, name, shape):
            return scope.enter_context(nc.psum_tensor(name, shape, F32))

        def dram(name, shape):
            return nc.dram_tensor(name, shape, F32, kind="Internal").ap()

        tab_ad = dram("tab_ad", [TROWS, 2 * D])
        tab_bc = dram("tab_bc", [TROWS, 2 * D])
        acc = dram("acc", [NACC * AROWS, D])
        a["srow"] = nc.dram_tensor("srow", [NT, 2, 128], BF16, kind="Internal").ap()
        buf = dram("buf", [NE * CP + JUNK, D])
        ybuf = dram("ybuf", [NE * CP, D])

        ident = sb(ctx, "ident", [128, 128])
        upper = sb(ctx, "upper", [128, 128])
        pcol_i = sb(ctx, "pcol_i", [128, 1], I32)
        pcol = sb(ctx, "pcol", [128, 1])
        x_sb = sb(ctx, "x_sb", [128, TT, D])
        keep = sb(ctx, "keep", [128, TT, D])
        mixw = sb(ctx, "mixw", [128, 2, D])
        slot_g = sb(ctx, "slot_g", [128, TT], I32)
        gate_p = sb(ctx, "gate_p", [128, TT])

        project(nc, a, sem, sb, ps, tab_ad, tab_bc, acc, buf, ident, upper, pcol_i, pcol,
                x_sb, keep, mixw)
        edges(nc, a, sem, sb, ps, tab_ad, tab_bc, acc, ident, upper, pcol)
        logits = sb(ctx, "logits", [128, TT, NE])
        nodes(nc, a, sem, sb, ps, acc, ident, x_sb, keep, mixw, logits)
        route(nc, sem, sb, ps, buf, upper, pcol, keep, logits, slot_g, gate_p)
        experts(nc, a, sem, sb, ps, buf, ybuf, ident)
        finish(nc, sem, sb, ybuf, x_sb, slot_g, gate_p, out)


def chain(eng, s, base=0):
    done = [0]

    def link(ins):
        done[0] += 1
        ins.then_inc(s, 1)
        eng.wait_ge(s, base + done[0])
    return link


def project(nc, a, sem, sb, ps, tab_ad, tab_bc, acc, buf, ident, upper, pcol_i, pcol, x_sb,
            keep, mixw):
    ZR = 5
    with ExitStack() as st:
        w = sb(st, "w", [128, 2, 6 * D])
        wq = sb(st, "wq", [128, 2, D])
        wot = sb(st, "wot", [128, 2, D])
        bias4 = sb(st, "bias4", [128, 2, 2 * D])
        lng = sb(st, "lng", [128, 2, HD])
        lnb = sb(st, "lnb", [128, 2, HD])
        zero = sb(st, "zero", [128, ZR * D])
        eps = sb(st, "eps", [128, 1])
        stats = sb(st, "stats", [128, TT, 6])
        mv = sb(st, "mv", [128, TT, 2])
        rstd = sb(st, "rstd", [128, TT])
        xn = sb(st, "xn", [128, 2, D])
        xT = sb(st, "xT", [128, 2, 2, P])
        ad = sb(st, "ad", [128, 2, 2 * D])
        bc = sb(st, "bc", [128, 2, 2 * D])
        cen = sb(st, "cen", [128, 2, 2 * D])
        sq = sb(st, "sq", [128, 2, 2 * D])
        hs = sb(st, "hs", [128, 2, 3, 8])
        kvg = sb(st, "kvg", [128, 2, 2 * D])
        kvT = sb(st, "kvT", [128, 2, 128])
        t1 = sb(st, "t1", [128, 2, D])
        p_T = ps(st, "p_T", [128, 512])
        p_ad = ps(st, "p_ad", [128, 2, 512])
        p_bc = ps(st, "p_bc", [128, 2, 512])
        p_kv = ps(st, "p_kv", [128, 2, 512])
        p_sum = ps(st, "p_sum", [128, 512])

        s_x = sem("a_x")
        s_w = sem("a_w")
        s_w2 = sem("a_w2")
        s_zst = sem("a_zst")
        s_const = sem("a_const")
        s_memset = sem("a_memset")
        s_dv = sem("a_dv")
        s_stats = sem("a_stats")
        s_std0 = sem("a_std0")
        s_norm = sem("a_norm")
        s_rstd0 = sem("a_rstd0")
        s_T = sem("a_T")
        s_xT = sem("a_xT")
        s_kept = sem("a_kept")
        s_mad = sem("a_mad")
        s_mbc = sem("a_mbc")
        s_mkv = sem("a_mkv")
        s_adc = sem("a_adc")
        s_bcc = sem("a_bcc")
        s_mean = sem("a_mean")
        s_cen = sem("a_cen")
        s_sq = sem("a_sq")
        s_var = sem("a_var")
        s_std = sem("a_std")
        s_rs = sem("a_rs")
        s_kvn = sem("a_kvn")
        s_gain = sem("a_gain")
        s_kvg = sem("a_kvg")
        s_msum = sem("a_msum")
        s_fold = sem("a_fold")
        s_foldc = sem("a_foldc")
        s_stad = [sem(f"a_stad{b}") for b in range(2)]
        s_stbc = [sem(f"a_stbc{b}") for b in range(2)]

        rows_ad = tab_ad[0:N, :].rearrange("(p t) d -> p t d", t=TT)
        rows_bc = tab_bc[0:N, :].rearrange("(p t) d -> p t d", t=TT)
        parts = [("L0_gnn_W1_1", 0), ("L0_gnn_W2_2", 1), ("L0_gnn_W2_1", 2), ("L0_gnn_W1_2", 3),
                 ("wkT", 4), ("wvT", 5)]

        block = st.enter_context(nc.Block())

        @block.sync
        def _(sp):
            sp.dma_start(x_sb[0:P, :, :], a["x"].rearrange("(p t) d -> p t d", t=TT)).then_inc(s_x, 16)
            for name, c in parts:
                sp.dma_start(w[:, :, c * D:(c + 1) * D],
                             a[name].rearrange("(k p) n -> p k n", p=128)).then_inc(s_w, 16)
            for k, name in enumerate(("L0_gnn_b2_1", "L0_gnn_b1_2", "L0_gnn_b1_1", "L0_gnn_b2_2")):
                sp.dma_start(bias4[:, k // 2, (k % 2) * D:(k % 2 + 1) * D],
                             a[name].unsqueeze(0).to_broadcast([128, D])).then_inc(s_w2, 16)
            for k, name in enumerate(("L0_mix_ln_k", "L0_mix_ln_v")):
                sp.dma_start(lng[:, k, :], a[name + "_g"].unsqueeze(0).to_broadcast([128, HD])).then_inc(s_w2, 16)
                sp.dma_start(lnb[:, k, :], a[name + "_b"].unsqueeze(0).to_broadcast([128, HD])).then_inc(s_w2, 16)
            sp.dma_start(wq[:, :, :], a["L0_mix_wq"].rearrange("(k p) n -> p k n", p=128)).then_inc(s_w2, 16)
            sp.dma_start(wot[:, :, :], a["woT"].rearrange("(k p) n -> p k n", p=128)).then_inc(s_w2, 16)

            def store(i, first):
                for b in range(2):
                    sp.wait_ge(s_adc, 2 * i + b + 1)
                    sp.dma_start(rows_ad[:, bass.ds(2 * i + b, 1), :],
                                 ad[0:P, b:b + 1, :]).then_inc(s_stad[b], 16)
                    sp.wait_ge(s_bcc, 2 * i + b + 1)
                    sp.dma_start(rows_bc[:, bass.ds(2 * i + b, 1), :],
                                 bc[0:P, b:b + 1, :]).then_inc(s_stbc[b], 16)
            store(0, True)
            with sp.Fori(1, TT // 2) as i:
                store(i, False)
            for b in range(2):
                sp.wait_ge(s_stad[b], 16 * (TT // 2))
                sp.wait_ge(s_stbc[b], 16 * (TT // 2))

        @block.gpsimd
        def _(pool):
            pool.memset(ident[:, :], 1.0).then_inc(s_memset, 1)
            pool.memset(upper[:, :], 1.0).then_inc(s_memset, 1)
            pool.iota(pcol_i[:, :], pattern=[[0, 1]], base=0, channel_multiplier=1).then_inc(s_memset, 1)
            pool.wait_ge(s_memset, 3)
            pool.affine_select(out=ident[:, :], in_=ident[:, :], compare_op=ALU.is_equal, fill=0.0, base=0,
                               pattern=[[-1, 128]], channel_multiplier=1).then_inc(s_const, 1)
            pool.affine_select(out=upper[:, :], in_=upper[:, :], compare_op=ALU.is_gt, fill=0.0, base=0,
                               pattern=[[1, 128]], channel_multiplier=-1).then_inc(s_const, 1)
            pool.tensor_copy(pcol[:, :], pcol_i[:, :]).then_inc(s_const, 1)
            pool.wait_ge(s_w2, 16 * 10)

            def tile(t, b, first):
                pool.wait_ge(s_xT, t + 1)
                pool.tensor_copy(keep[:, bass.ds(t, 1), 0:2 * P],
                                 xT[:, b, :, :].rearrange("p k n -> p (k n)").unsqueeze(1)).then_inc(s_kept, 1)

            def gains(t, b):
                kv4 = kvg[0:P, b, :].rearrange("p (w h d) -> p w h d", w=2, h=H)
                pool.wait_ge(s_kvn, t + 1)
                pool.tensor_tensor(kv4, kv4, lng[0:P, :, :].unsqueeze(2).to_broadcast([P, 2, H, HD]),
                                   ALU.mult).then_inc(s_gain, 1)
                pool.wait_ge(s_gain, t + 1)
                pool.tensor_tensor(kv4, kv4, lnb[0:P, :, :].unsqueeze(2).to_broadcast([P, 2, H, HD]),
                                   ALU.add).then_inc(s_kvg, 1)
            tile(0, 0, True)
            tile(1, 1, True)
            gains(0, 0)
            with pool.Fori(1, TT // 2) as i:
                for b in range(2):
                    tile(2 * i + b, b, False)
                    gains(2 * i + b - 1, 1 - b)
            gains(TT - 1, 1)

        @block.scalar
        def _(act):
            act.wait_ge(s_dv, 1)
            acc_z = acc.rearrange("(p k r) d -> p k (r d)", p=128, r=ZR)
            nz = acc_z.shape[1] // NACC
            for c in range(NACC):
                act.dma_start(acc_z[:, c * nz:(c + 1) * nz, :], zero[:, :].unsqueeze(1).to_broadcast([128, nz, ZR * D])
                              ).then_inc(s_zst, 16)
            act.dma_start(buf.rearrange("(p k r) d -> p k (r d)", p=128, r=ZR),
                          zero[:, :].unsqueeze(1).to_broadcast([128, (NE * CP + JUNK) // 128 // ZR, ZR * D])
                          ).then_inc(s_zst, 16)
            for t in (tab_ad, tab_bc):
                act.dma_start(t[N:N + 75, :], zero[0:75, 0:2 * D]).then_inc(s_zst, 16)
                act.dma_start(t[N + 75:TROWS, :], zero[0:75, 0:2 * D]).then_inc(s_zst, 16)
            act.wait_ge(s_stats, 6)
            nc.scalar.activation(rstd[0:P, :], mv[0:P, :, 1], ACT.Sqrt, bias=eps[0:P, :]).then_inc(s_std0, 1)

            def transposed(t, b, first):
                act.wait_ge(s_T, t + 1)
                if not first:
                    act.wait_ge(s_mkv, t - 1)
                    act.wait_ge(s_kept, t - 1)
                nc.scalar.copy(xT[:, b, :, :].rearrange("p k n -> p (k n)"), p_T[:, 0:2 * P]).then_inc(s_xT, 1)

            def evacuate(t, b, first):
                act.wait_ge(s_mad, t + 1)
                if not first:
                    act.wait_ge(s_stad[b], 8 * t - 8 * b)
                nc.scalar.copy(ad[0:P, b, :], p_ad[0:P, b, :]).then_inc(s_adc, 1)
                act.wait_ge(s_cen, t + 1)
                nc.scalar.activation(sq[0:P, b, :], cen[0:P, b, :], ACT.Square).then_inc(s_sq, 1)
                act.wait_ge(s_var, t + 1)
                nc.scalar.activation(hs[0:P, b, 2, :], hs[0:P, b, 1, :], ACT.Sqrt, bias=eps[0:P, :],
                                     scale=1.0 / HD).then_inc(s_std, 1)
            transposed(0, 0, True)
            transposed(1, 1, True)
            evacuate(0, 0, True)
            transposed(2, 0, False)
            evacuate(1, 1, True)
            transposed(3, 1, False)
            with act.Fori(1, TT // 2 - 1) as i:
                for b in range(2):
                    evacuate(2 * i + b, b, False)
                    transposed(2 * i + b + 2, b, False)
            evacuate(TT - 2, 0, False)
            evacuate(TT - 1, 1, False)
            act.wait_ge(s_zst, 16 * (NACC + 5))

        @block.vector
        def _(dve):
            nc.vector.memset(zero[:, :], 0.0).then_inc(s_dv, 1)
            nc.vector.memset(eps[:, :], EPS).then_inc(s_dv, 1)
            dve.wait_ge(s_x, 16)
            with dve.Fori(0, TT) as t:
                nc.vector.bn_stats(stats[0:P, bass.ds(t, 1), :], x_sb[0:P, bass.ds(t, 1), :]).then_inc(s_rstd0, 1)
            dve.wait_ge(s_rstd0, TT)
            even, odd = stats[0:P, :, 0:3], stats[0:P, :, 3:6]
            nc.vector.tensor_tensor(mv[0:P, :, :], even[:, :, 1:3], odd[:, :, 1:3], ALU.add).then_inc(s_stats, 1)
            nc.vector.tensor_tensor(rstd[0:P, :], even[:, :, 1], odd[:, :, 1], ALU.subtract).then_inc(s_stats, 1)
            dve.wait_ge(s_stats, 2)
            nc.vector.tensor_tensor(rstd[0:P, :], rstd[0:P, :], rstd[0:P, :], ALU.mult).then_inc(s_stats, 1)
            nc.vector.tensor_scalar_mul(mv[0:P, :, 0], mv[0:P, :, 0], 0.5).then_inc(s_stats, 1)
            dve.wait_ge(s_stats, 4)
            nc.vector.tensor_scalar_mul(mv[0:P, :, 1], mv[0:P, :, 1], 1.0 / D).then_inc(s_stats, 1)
            dve.wait_ge(s_stats, 5)
            nc.vector.scalar_tensor_tensor(mv[0:P, :, 1], rstd[0:P, :], 0.25, mv[0:P, :, 1], ALU.mult, ALU.add
                                           ).then_inc(s_stats, 1)
            dve.wait_ge(s_std0, 1)
            nc.vector.reciprocal(rstd[0:P, :], rstd[0:P, :]).then_inc(s_rstd0, 1)
            dve.wait_ge(s_rstd0, TT + 1)
            dve.wait_ge(s_w2, 16 * 10)
            nc.vector.tensor_tensor(bias4[:, 0, :], bias4[:, 0, :], bias4[:, 1, :], ALU.add).then_inc(s_rstd0, 1)
            dve.wait_ge(s_rstd0, TT + 2)

            def normalise(t, b, first):
                if not first:
                    dve.wait_ge(s_T, t - 1)
                nc.vector.tensor_scalar(xn[0:P, b:b + 1, :], x_sb[0:P, bass.ds(t, 1), :],
                                        mv[0:P, bass.ds(t, 1), 0], rstd[0:P, bass.ds(t, 1)],
                                        ALU.subtract, ALU.mult).then_inc(s_norm, 1)

            def heads(t, b, first):
                kv8 = p_kv[0:P, b, :].rearrange("p (g d) -> p g d", d=HD)
                cen8 = cen[0:P, b, :].rearrange("p (g d) -> p g d", d=HD)
                sq8 = sq[0:P, b, :].rearrange("p (g d) -> p g d", d=HD)
                out8 = kvg[0:P, b, :].rearrange("p (g d) -> p g d", d=HD)

                def wide(v):
                    return v.unsqueeze(2).to_broadcast([P, 8, HD])
                dve.wait_ge(s_mkv, t + 1)
                nc.vector.tensor_reduce(hs[0:P, b, 0, :], kv8, AXX, ALU.add).then_inc(s_mean, 1)
                dve.wait_ge(s_mean, 2 * t + 1)
                nc.vector.tensor_scalar_mul(hs[0:P, b, 0, :], hs[0:P, b, 0, :], 1.0 / HD).then_inc(s_mean, 1)
                dve.wait_ge(s_mean, 2 * t + 2)
                nc.vector.tensor_tensor(cen8, kv8, wide(hs[0:P, b, 0, :]), ALU.subtract).then_inc(s_cen, 1)
                dve.wait_ge(s_mbc, t + 1)
                if not first:
                    dve.wait_ge(s_stbc[b], 8 * t - 8 * b)
                nc.vector.tensor_tensor(bc[0:P, b, :], p_bc[0:P, b, :], bias4[0:P, 0, :], ALU.add).then_inc(s_bcc, 1)
                dve.wait_ge(s_sq, t + 1)
                nc.vector.tensor_reduce(hs[0:P, b, 1, :], sq8, AXX, ALU.add).then_inc(s_var, 1)
                dve.wait_ge(s_std, t + 1)
                nc.vector.reciprocal(hs[0:P, b, 2, :], hs[0:P, b, 2, :]).then_inc(s_rs, 1)
                dve.wait_ge(s_rs, t + 1)
                if not first:
                    dve.wait_ge(s_msum, t - 1)
                nc.vector.tensor_tensor(out8, cen8, wide(hs[0:P, b, 2, :]), ALU.mult).then_inc(s_kvn, 1)
            normalise(0, 0, True)
            normalise(1, 1, True)
            normalise(2, 0, False)
            heads(0, 0, True)
            normalise(3, 1, False)
            heads(1, 1, True)
            with dve.Fori(1, TT // 2 - 1) as i:
                for b in range(2):
                    normalise(2 * i + b + 2, b, False)
                    heads(2 * i + b, b, False)
            heads(TT - 2, 0, False)
            heads(TT - 1, 1, False)

            nc.vector.memset(kvT[:, :, :], 0.0).then_inc(s_dv, 1)
            dve.wait_ge(s_dv, 3)
            dve.wait_ge(s_msum, TT + 1)
            for hp in range(2):
                for h in range(2):
                    r = slice(h * HD, (h + 1) * HD)
                    nc.vector.tensor_scalar_mul(kvT[r, hp, r], p_sum[r, hp * 128 + h * HD:hp * 128 + (h + 1) * HD],
                                                1.0 / N).then_inc(s_foldc, 1)
            dve.wait_ge(s_fold, 1)
            nc.vector.tensor_copy(t1[:, :, :].rearrange("p k n -> p (k n)"), p_ad[:, 0, :]).then_inc(s_foldc, 1)
            dve.wait_ge(s_fold, 2)
            nc.vector.tensor_copy(mixw[:, :, :].rearrange("p k n -> p (k n)"), p_bc[:, 0, :]).then_inc(s_foldc, 1)

        @block.tensor
        def _(pe):
            pe.wait_ge(s_const, 3)
            pe.wait_ge(s_w, 16 * 6)
            pe.wait_ge(s_dv, 1)
            nc.tensor.matmul(p_sum[:, 0:256], zero[:, 0:128], zero[:, 0:256], start=True, stop=False)

            def transposes(t, b, first):
                pe.wait_ge(s_norm, t + 1)
                if not (first and t == 0):
                    pe.wait_ge(s_xT, t)
                for k in range(2):
                    last = nc.tensor.transpose(p_T[:, k * P:(k + 1) * P], xn[0:P, b, k * 128:(k + 1) * 128],
                                               ident[0:P, 0:P])
                last.then_inc(s_T, 1)

            def products(t, b, first):
                pe.wait_ge(s_xT, t + 1)
                for pt, c, done, free in ((p_ad, 0, s_mad, s_adc), (p_bc, 2, s_mbc, s_bcc), (p_kv, 4, s_mkv, s_cen)):
                    if not first:
                        pe.wait_ge(free, t - 1)
                    for k in range(2):
                        last = nc.tensor.matmul(pt[0:P, b, :], xT[:, b, k, :], w[:, k, c * D:(c + 2) * D],
                                                start=(k == 0), stop=(k == 1))
                    last.then_inc(done, 1)

            def sums(t, b, stop=False):
                pe.wait_ge(s_kvg, t + 1)
                for hp in range(2):
                    last = nc.tensor.matmul(p_sum[:, hp * 128:(hp + 1) * 128],
                                            kvg[0:P, b, D + hp * 128:D + (hp + 1) * 128],
                                            kvg[0:P, b, hp * 128:(hp + 1) * 128], start=False, stop=False)
                last.then_inc(s_msum, 1)
            transposes(0, 0, True)
            transposes(1, 1, True)
            products(0, 0, True)
            transposes(2, 0, False)
            products(1, 1, True)
            sums(0, 0)
            transposes(3, 1, False)
            with pe.Fori(1, TT // 2 - 1) as i:
                for b in range(2):
                    products(2 * i + b, b, False)
                    sums(2 * i + b - 1, 1 - b)
                    transposes(2 * i + b + 2, b, False)
            products(TT - 2, 0, False)
            sums(TT - 3, 1)
            products(TT - 1, 1, False)
            sums(TT - 2, 0)
            sums(TT - 1, 1)
            nc.tensor.matmul(p_sum[:, 0:256], zero[:, 0:128], zero[:, 0:256], start=False, stop=True).then_inc(s_msum, 1)
            pe.wait_ge(s_foldc, 4)
            pe.wait_ge(s_adc, TT)
            pe.wait_ge(s_bcc, TT)
            pe.wait_ge(s_w2, 16 * 10)
            for hp in range(2):
                last = nc.tensor.matmul(p_ad[:, 0, hp * D:(hp + 1) * D], kvT[:, hp, :], wot[:, hp, :],
                                        start=True, stop=True)
            last.then_inc(s_fold, 1)
            pe.wait_ge(s_foldc, 5)
            for m in range(2):
                for k in range(2):
                    last = nc.tensor.matmul(p_bc[:, 0, m * D:(m + 1) * D], wq[:, k, m * 128:(m + 1) * 128],
                                            t1[:, k, :], start=(k == 0), stop=(k == 1))
            last.then_inc(s_fold, 1)


def edges(nc, a, sem, sb, ps, tab_ad, tab_bc, acc, ident, upper, pcol):
    RG = (NT + 127) // 128
    full = E // 128
    with ExitStack() as st:
        ids = sb(st, "ids", [128, NT, 2])
        raw = sb(st, "raw", [128, 2, 128], I32)
        rawf = sb(st, "rawf", [128, 2, 128])
        rowi = sb(st, "rowi", [128, 2, 128], I32)
        rowb = sb(st, "rowb", [128, 2, 128], BF16)
        small = sb(st, "small", [128, 2, 2, 2 * U])
        copy_row = sb(st, "copy_row", [128, 2 * U])
        junk = sb(st, "junk", [128, 2 * U])
        gidx = sb(st, "gidx", [128, 2, 2 * U], I32)
        sidx = sb(st, "sidx", [128, 2, 2 * U], I32)
        g_ad = sb(st, "g_ad", [128, 2, U, 2 * D])
        later = sb(st, "later", [128, 2 * U, 128])
        rel = sb(st, "rel", [128, NW, WT])
        base_f = sb(st, "base_f", [128, NW])
        base_i = sb(st, "base_i", [128, NW], I32)
        row0 = sb(st, "row0", [128, 128])
        worst = sb(st, "worst", [128, 2])
        narrow_i = sb(st, "narrow_i", [1, 1], I32)
        wide_f = sb(st, "wide_f", [1, 1])
        scol = sb(st, "scol", [128, NQ, U])
        tojunk = sb(st, "tojunk", [128, NT])
        iota_i = sb(st, "iota_i", [128, 3, W], I32)
        iota3 = sb(st, "iota3", [128, 3 * W])
        part = sb(st, "part", [128, 2])
        self32 = sb(st, "self32", [2 * WT, WT, 128])
        sel = sb(st, "sel", [2 * WT, WT, 128], BF16)

        s_raw = sem("e_raw")
        s_rawm = sem("e_rawm")
        s_rawf = sem("e_rawf")
        s_rawT = sem("e_rawT")
        s_ids = sem("e_ids")
        s_rowb = sem("e_rowb")
        s_rowd = sem("e_rowd")
        s_base = sem("e_base")
        s_prep = sem("e_prep")
        s_worst = sem("e_worst")
        s_wide = sem("e_wide")
        s_cst = sem("e_cst")
        s_idx = sem("e_idx")
        s_turn = sem("e_turn")
        s_row = sem("e_row")
        s_same = sem("e_same")
        s_small = sem("e_small")
        s_sidx = sem("e_sidx")
        s_gad = [sem(f"e_gad{b}") for b in range(2)]
        s_gbc = [sem(f"e_gbc{b}") for b in range(2)]
        s_add = sem("e_add")
        s_relu = sem("e_relu")
        s_sum = sem("e_sum")
        s_res = sem("e_res")
        s_scat = [sem(f"e_scat{b}") for b in range(2)]
        s_dst = sem("e_dst")
        s_srow = sem("e_srow")
        s_win = sem("e_win")
        s_h = sem("e_h")
        s_t1 = sem("e_t1")
        s_m1 = sem("e_m1")
        s_wout = sem("e_wout")
        s_hot = sem("e_hot")
        s_T = sem("e_T")
        s_hotT = sem("e_hotT")
        s_exp = sem("e_exp")
        s_dd = sem("e_dd")
        s_wev = sem("e_wev")
        s_rank = sem("e_rank")

        with ExitStack() as s1:
            p_row = ps(s1, "p_ids", [128, 2, 128])
            p_base = ps(s1, "p_base", [128, 512])
            block = s1.enter_context(nc.Block())

            @block.sync
            def _(sp):
                for g in range(RG):
                    r0, r1 = g * 128, min((g + 1) * 128, full)
                    sp.wait_ge(s_rawm, g + 1)
                    for k, name in enumerate(("src", "dst")):
                        sp.dma_start(raw[0:r1 - r0, k, :],
                                     a[name][r0 * 128:r1 * 128].rearrange("(r e) -> r e", e=128)
                                     ).then_inc(s_raw, 16)
                        if g == RG - 1:
                            sp.dma_start(raw[r1 - r0:r1 - r0 + 1, k, 0:E - full * 128],
                                         a[name][full * 128:E].unsqueeze(0)).then_inc(s_raw, 16)
                    w = min(128, NT - r0)
                    sp.wait_ge(s_rowb, g + 1)
                    sp.dma_start(a["srow"][r0:r0 + w, :, :], rowb[0:w, :, :]).then_inc(s_rowd, 16)
                sp.wait_ge(s_rowd, 16 * RG)

            @block.vector
            def _(dve):
                V = nc.vector
                V.memset(raw[:, :, :], NJ).then_inc(s_rawm, 1)
                for g in range(RG):
                    dve.wait_ge(s_raw, 32 * (g + 1) + (32 if g == RG - 1 else 0))
                    if g:
                        dve.wait_ge(s_rawT, g)
                        dve.wait_ge(s_rowd, 16 * g)
                    V.tensor_copy(rawf[:, :, :], raw[:, :, :]).then_inc(s_rawf, 1)
                    V.tensor_single_scalar(rowi[:, 0, :], raw[:, 0, :], 7, ALU.logical_shift_right
                                           ).then_inc(s_prep, 1)
                    V.tensor_single_scalar(rowi[:, 1, :], raw[:, 0, :], 127, ALU.bitwise_and).then_inc(s_prep, 1)
                    dve.wait_ge(s_prep, 2 * g + 2)
                    V.tensor_copy(rowb[:, :, :], rowi[:, :, :]).then_inc(s_rowb, 1)
                    dve.wait_ge(s_rawf, g + 1)
                    dve.wait_ge(s_rowb, g + 1)
                    if g < RG - 1:
                        V.memset(raw[:, :, :], NJ).then_inc(s_rawm, 1)
                    w = min(128, NT - g * 128)
                    dve.wait_ge(s_rawT, g + 1)
                    V.tensor_copy(ids[:, g * 128:g * 128 + w, :].rearrange("p t k -> p k t"),
                                  p_row[:, :, 0:w]).then_inc(s_ids, 1)
                V.memset(row0[:, :], 0.0).then_inc(s_cst, 1)
                dve.wait_ge(s_cst, 1)
                V.memset(row0[0:1, :], 1.0).then_inc(s_cst, 1)
                for c in range(2 * U):
                    V.memset(copy_row[:, c:c + 1], float((U if c % 2 else c // 2) * AROWS)).then_inc(s_cst, 1)
                dve.wait_ge(s_cst, 2 + 2 * U)
                dve.wait_ge(s_ids, RG)
                done = 2 * RG
                link = chain(dve, s_prep, done)
                link(V.tensor_scalar(junk[:, :], copy_row[:, :], pcol[:, :], float(N + 22), ALU.add, ALU.add))
                link(V.tensor_scalar(tojunk[:, :], ids[:, :, 0], -1.0, junk[:, 0:1], ALU.mult, ALU.add))
                link(V.tensor_tensor(scol[:, :, :], ids[:, :, 0].rearrange("p (q u) -> p q u", u=U),
                                     copy_row[:, ::2].unsqueeze(1).to_broadcast([128, NQ, U]), ALU.add))
                link(V.tensor_scalar(part[:, 0:1], pcol[:, :], float(W), -1.0, ALU.is_ge, ALU.mult))
                link(V.tensor_scalar(part[:, 1:2], pcol[:, :], float(2 * W), -1.0, ALU.is_ge, ALU.mult))
                dve.wait_ge(s_base, 1)
                link(V.tensor_copy(base_f[:, :], p_base[:, 0:NW]))
                link(V.tensor_copy(base_i[:, :], base_f[:, :]))
                link(V.tensor_tensor(rel[:, :, :], ids[:, :, 1].rearrange("p (w t) -> p w t", t=WT),
                                     base_f[:, :].unsqueeze(2).to_broadcast([128, NW, WT]), ALU.subtract))
                flat = rel[:, :, :].rearrange("p w t -> p (w t)")
                link(V.tensor_reduce(worst[:, 0:1], flat, AXX, ALU.max))
                link(V.tensor_reduce(worst[:, 1:2], flat, AXX, ALU.min))
                link(V.tensor_scalar_add(worst[:, 0:1], worst[:, 0:1], float(1 - W)))
                link(V.scalar_tensor_tensor(worst[:, 0:1], worst[:, 1:2], -1.0, worst[:, 0:1], ALU.mult, ALU.max))
                dve.sem_inc(s_worst)
                dve.wait_ge(s_worst, 2)
                link(V.tensor_reduce(wide_f[:, :], p_base[0:1, 256:384], AXX, ALU.max))
                link(V.tensor_scalar(narrow_i[:, :], wide_f[:, :], 0.0, None, ALU.is_le))
                dve.wait_ge(s_wide, 3)
                V.tensor_copy(iota3[:, :], iota_i[:, :, :].rearrange("p c w -> p (c w)")).then_inc(s_cst, 1)
                V.tensor_copy(sel[:, :, :], self32[:, :, :]).then_inc(s_cst, 1)
                dve.wait_ge(s_cst, 4 + 2 * U)

            @block.tensor
            def _(pe):
                for g in range(RG):
                    pe.wait_ge(s_rawf, g + 1)
                    if g:
                        pe.wait_ge(s_ids, g)
                    for k in range(2):
                        last = nc.tensor.transpose(p_row[:, k, :], rawf[:, k, :], ident[:, :])
                    last.then_inc(s_rawT, 1)
                pe.wait_ge(s_ids, RG)
                pe.wait_ge(s_cst, 2)
                nc.tensor.matmul(p_base[:, 0:NW], row0[:, :], ids[:, ::WT, 1], start=True, stop=True
                                 ).then_inc(s_base, 1)
                pe.wait_ge(s_worst, 1)
                nc.tensor.transpose(p_base[0:1, 256:384], worst[:, 0:1], ident[:, :]).then_inc(s_worst, 1)

            @block.gpsimd
            def _(pool):
                pool.iota(iota_i[:, :, :], pattern=[[0, 3], [1, W]], base=0, channel_multiplier=0
                          ).then_inc(s_wide, 1)
                pool.memset(self32[:, :, :], 0.0).then_inc(s_turn, 1)
                for k, v in ((0, 128.0), (1, 1.0)):
                    pool.wait_ge(s_turn, k + 1)
                    ins = pool.affine_select(out=self32[:, :, :], in_=self32[:, :, :], compare_op=ALU.not_equal,
                                             fill=v, base=-k, pattern=[[-2, WT], [0, 128]], channel_multiplier=1)
                    ins.then_inc(s_wide if k else s_turn, 1 + k)

        with ExitStack() as s2:
            same = sb(s2, "same", [128, 2, U, 128])
            hot = sb(s2, "e_hot1", [128, 2, U, 3 * W])
            hotT = sb(s2, "hotT", [3 * W, U, 128], BF16)
            win = sb(s2, "win", [3 * W, 2 * D])
            hi = sb(s2, "hi", [3 * W, 2 * D], BF16)
            t1 = sb(s2, "rest1", [3 * W, 2 * D])
            m1 = sb(s2, "rest1b", [3 * W, 2 * D], BF16)
            winb = sb(s2, "winb", [3 * W, 2 * D], BF16)
            srow = sb(s2, "srow_sb", [2 * WT, 128], BF16)
            res = sb(s2, "res", [128, 2, 2, 2 * D])
            wres = sb(s2, "wres", [W, D])
            p_x = ps(s2, "p_x", [128, U, 128])
            p_bc = ps(s2, "p_bc2", [128, U, 512])
            p_res = ps(s2, "p_res", [128, 2, 512])
            p_win = ps(s2, "p_win", [128, 512])
            idf = sb(s2, "idf", [128, 2 * U])
            sG = same[:, :, :, :].rearrange("p b u e -> p (b u) e")
            gres = res[:, :, :, :].rearrange("p b r n -> p (b r) n")
            g_bc = g_ad[:, 1, :, :]
            PER = 16 * U
            LAST = NQ // 2

            block = s2.enter_context(nc.Block())

            def past(q, n):
                return not isinstance(q, int) or q >= n

            def ok(q, n=NQ):
                return not isinstance(q, int) or 0 <= q < n

            def pipe(eng, step):
                for i in (-1, 0, 1):
                    for b in range(2):
                        step(i, b)
                with eng.Fori(2, LAST - 1) as i:
                    for b in range(2):
                        step(i, b)
                for i in (LAST - 1, LAST):
                    for b in range(2):
                        step(i, b)

            @block.sync
            def _(sp):
                narrow = sp.value_load(narrow_i[0:1, 0:1], min_val=0, max_val=1)
                with sp.If(narrow):
                    def load(w):
                        if past(w, 1):
                            sp.wait_ge(s_row, 2 * w)
                        sp.dma_start(srow[:, :], a["srow"][bass.ds(WT * w, WT), :, :].rearrange("t k e -> (t k) e")
                                     ).then_inc(s_srow, 16)
                        first = sp.value_load(base_i[0:1, bass.ds(w, 1)], min_val=0, max_val=NJ)
                        if past(w, 1):
                            sp.wait_ge(s_t1, w)
                            sp.wait_ge(s_h, w)
                        for c in range(3):
                            sp.dma_start(win[c * W:(c + 1) * W, :], tab_bc[bass.ds(first, W), :]).then_inc(s_win, 16)
                    load(0)
                    with sp.Fori(1, NW) as w:
                        load(w)

            @block.gpsimd
            def _(pool):
                def gather(q, b):
                    pool.wait_ge(s_idx, q + 1)
                    if past(q, 2):
                        pool.wait_ge(s_sum, q - 1)
                    pool.sem_inc(s_turn)
                    for u in range(U):
                        pool.indirect_dma_start(g_ad[:, b, u, :], None, tab_ad,
                                                bass.IndirectOffsetOnAxis(gidx[:, b, u:u + 1], 0)
                                                ).then_inc(s_gad[b], 16)

                def scatter(q, b, w):
                    pool.wait_ge(s_sidx, q + 1)
                    pool.wait_ge(s_res, 2 * q + 2)
                    if past(q, 1):
                        pool.wait_ge(s_scat[1 - b], PER * (w + b))
                    pool.sem_inc(s_turn)
                    for u in range(U):
                        pool.indirect_dma_start(acc, bass.IndirectOffsetOnAxis(sidx[:, b, u:u + 1], 0),
                                                res[:, b, u // 2, (u % 2) * D:(u % 2 + 1) * D], None,
                                                compute_op=ALU.add).then_inc(s_scat[b], 16)

                def add_window(w):
                    first = pool.value_load(base_i[0:1, bass.ds(w, 1)], min_val=0, max_val=NJ)
                    pool.wait_ge(s_wev, w + 1)
                    pool.sem_inc(s_turn)
                    pool.dma_start(acc[bass.ds(U * AROWS + first, W), :], wres[:, :], accum_op=ALU.add
                                   ).then_inc(s_dst, 16)

                def step(i, b):
                    s = 2 * i + b
                    if ok(s):
                        gather(s, b)
                    if ok(s - 2):
                        scatter(s - 2, b, i - 1)
                    if b == 1 and ok(i - 1, NW):
                        add_window(i - 1)
                narrow = pool.value_load(narrow_i[0:1, 0:1], min_val=0, max_val=1)
                with pool.If(narrow):
                    pipe(pool, step)
                    for b in range(2):
                        pool.wait_ge(s_scat[b], PER * (NQ // 2))
                    pool.wait_ge(s_dst, 16 * NW)
                with pool.Else():
                    def tiles(q, first):
                        pool.wait_ge(s_idx, q + 1)
                        pool.sem_inc(s_turn)
                        for u in range(U):
                            pool.indirect_dma_start(g_ad[:, 0, u, :], None, tab_ad,
                                                    bass.IndirectOffsetOnAxis(gidx[:, 0, 2 * u:2 * u + 1], 0)
                                                    ).then_inc(s_gad[0], 16)
                            pool.indirect_dma_start(g_bc[:, u, :], None, tab_bc,
                                                    bass.IndirectOffsetOnAxis(gidx[:, 0, 2 * u + 1:2 * u + 2], 0)
                                                    ).then_inc(s_gbc[0], 16)
                        pool.wait_ge(s_sidx, q + 1)
                        pool.wait_ge(s_res, U * (q + 1))
                        pool.sem_inc(s_turn)
                        for u in range(U):
                            pool.indirect_dma_start(acc, bass.IndirectOffsetOnAxis(sidx[:, 0, 2 * u:2 * u + 1], 0),
                                                    gres[:, u, 0:D], None, compute_op=ALU.add
                                                    ).then_inc(s_scat[0], 16)
                            if u or not first:
                                pool.wait_ge(s_dst, 16 * U * q + 16 * u)
                                pool.sem_inc(s_turn)
                            pool.indirect_dma_start(acc, bass.IndirectOffsetOnAxis(sidx[:, 0, 2 * u + 1:2 * u + 2], 0),
                                                    gres[:, u, D:2 * D], None, compute_op=ALU.add
                                                    ).then_inc(s_dst, 16)
                    tiles(0, True)
                    with pool.Fori(1, NQ) as q:
                        tiles(q, False)
                    pool.wait_ge(s_scat[0], PER * NQ)
                    pool.wait_ge(s_dst, PER * NQ)

            @block.vector
            def _(dve):
                V = nc.vector

                def indices(q, b):
                    V.tensor_copy(gidx[:, b, 0:U], ids[:, bass.ds(U * q, U), 0]).then_inc(s_idx, 1)

                def onehot(q, b):
                    if past(q, 2):
                        dve.wait_ge(s_sum, q - 1)
                    r = rel[:, :, :].rearrange("p w t -> p (w t)")[:, bass.ds(U * q, U)]
                    V.tensor_tensor(hot[:, b, :, :], iota3[:, :].unsqueeze(1).to_broadcast([128, U, 3 * W]),
                                    r.unsqueeze(2).to_broadcast([128, U, 3 * W]), ALU.is_equal).then_inc(s_hot, 1)

                def duplicates(q, b):
                    dve.wait_ge(s_row, q + 1)
                    V.tensor_tensor(same[:, b, :, :], p_x[:, :, :],
                                    ids[:, bass.ds(U * q, U), 0].unsqueeze(2).to_broadcast([128, U, 128]),
                                    ALU.is_equal).then_inc(s_same, 1)
                    dve.wait_ge(s_same, q + 1)
                    if past(q, 1):
                        dve.wait_ge(s_rank, 3 * q)
                    V.tensor_tensor(later[:, 0:U, :], same[:, b, :, :],
                                    upper[:, :].unsqueeze(1).to_broadcast([128, U, 128]), ALU.mult
                                    ).then_inc(s_rank, 1)
                    dve.wait_ge(s_rank, 3 * q + 1)
                    V.tensor_reduce(small[:, b, 0, 0:U], later[:, 0:U, :], AXX, ALU.add).then_inc(s_rank, 1)
                    dve.wait_ge(s_rank, 3 * q + 2)
                    V.scalar_tensor_tensor(small[:, b, 1, 0:U], small[:, b, 0, 0:U], 0.0,
                                           tojunk[:, bass.ds(U * q, U)], ALU.is_gt, ALU.mult).then_inc(s_rank, 1)

                def targets(q, b, w):
                    dve.wait_ge(s_rank, 3 * q + 3)
                    if past(q, 2):
                        dve.wait_ge(s_scat[b], PER * w)
                    V.tensor_tensor(sidx[:, b, 0:U].unsqueeze(1), small[:, b, 1, 0:U].unsqueeze(1),
                                    scol[:, bass.ds(q, 1), :], ALU.add).then_inc(s_sidx, 1)

                def add(q, b, w):
                    dve.wait_ge(s_gad[b], PER * (w + 1))
                    dve.wait_ge(s_exp, q + 1)
                    V.tensor_tensor(g_ad[:, b, :, :], g_ad[:, b, :, :], p_bc[:, :, :], ALU.add).then_inc(s_add, 1)

                def rest(w):
                    dve.wait_ge(s_win, 48 * (w + 1))
                    dve.wait_ge(s_h, w + 1)
                    if past(w, 1):
                        dve.wait_ge(s_m1, w)
                        dve.wait_ge(s_wout, w)
                    V.scalar_tensor_tensor(t1[:, :], hi[:, :], part[0:3 * W, 0:1], win[:, :], ALU.mult, ALU.add
                                           ).then_inc(s_t1, 1)

                def thirds(w):
                    dve.wait_ge(s_m1, w + 1)
                    dve.wait_ge(s_t1, w + 1)
                    if past(w, 1):
                        dve.wait_ge(s_exp, 2 * w)
                    V.scalar_tensor_tensor(winb[:, :], m1[:, :], part[0:3 * W, 1:2], t1[:, :], ALU.mult, ALU.add
                                           ).then_inc(s_wout, 1)

                def step(i, b):
                    s = 2 * i + b
                    if ok(s - 1):
                        targets(s - 1, 1 - b, i - 1 + b)
                    if ok(s):
                        add(s, b, i)
                    if b == 1 and ok(i + 1, NW):
                        thirds(i + 1)
                    if ok(s + 1):
                        onehot(s + 1, 1 - b)
                        duplicates(s + 1, 1 - b)
                    if ok(s + 2):
                        indices(s + 2, b)
                    if b == 0 and ok(i + 1, NW):
                        rest(i + 1)
                narrow = dve.value_load(narrow_i[0:1, 0:1], min_val=0, max_val=1)
                with dve.If(narrow):
                    pipe(dve, step)
                with dve.Else():
                    def group(q, first):
                        def wide(v):
                            return v.unsqueeze(2).to_broadcast([128, 2 * U, 128])
                        src = ids[:, bass.ds(U * q, U), :].rearrange("p t k -> p (t k)")
                        if not first:
                            dve.wait_ge(s_scat[0], PER * q)
                            dve.wait_ge(s_dst, PER * q)
                        V.tensor_copy(idf[:, :], src).then_inc(s_small, 1)
                        V.tensor_copy(gidx[:, 0, :], src).then_inc(s_idx, 1)
                        dve.wait_ge(s_small, 6 * q + 1)
                        for half in range(2):
                            dve.wait_ge(s_row, 2 * q + half + 1)
                            V.tensor_tensor(sG[:, half * U:(half + 1) * U, :], p_x[:, :, :],
                                            idf[:, half * U:(half + 1) * U].unsqueeze(2).to_broadcast([128, U, 128]),
                                            ALU.is_equal).then_inc(s_same, 1)
                        dve.wait_ge(s_same, 2 * q + 2)
                        link = chain(dve, s_small, 6 * q + 1)
                        link(V.tensor_tensor(later[:, :, :], sG[:, :, :],
                                             upper[:, :].unsqueeze(1).to_broadcast([128, 2 * U, 128]), ALU.mult))
                        link(V.tensor_reduce(small[:, 0, 0, :], later[:, :, :], AXX, ALU.add))
                        link(V.tensor_tensor(idf[:, :], idf[:, :], copy_row[:, :], ALU.add))
                        link(V.tensor_tensor(small[:, 0, 1, :], junk[:, :], idf[:, :], ALU.subtract))
                        link(V.scalar_tensor_tensor(small[:, 0, 1, :], small[:, 0, 0, :], 0.0, small[:, 0, 1, :],
                                                    ALU.is_gt, ALU.mult))
                        V.tensor_tensor(sidx[:, 0, :], small[:, 0, 1, :], idf[:, :], ALU.add).then_inc(s_sidx, 1)
                        dve.wait_ge(s_sidx, q + 1)
                        dve.wait_ge(s_gad[0], PER * (q + 1))
                        dve.wait_ge(s_gbc[0], PER * (q + 1))
                        V.tensor_tensor(g_ad[:, 0, :, :], g_ad[:, 0, :, :], g_bc[:, :, :], ALU.add).then_inc(s_add, 1)
                    group(0, True)
                    with dve.Fori(1, NQ) as q:
                        group(q, False)

            @block.scalar
            def _(act):
                S = nc.scalar

                def results(q, b, w):
                    if past(q, 2):
                        act.wait_ge(s_scat[b], PER * w)
                    for r in range(2):
                        act.wait_ge(s_dd, 2 * q + r + 1)
                        S.copy(res[:, b, r, :], p_res[:, r, :]).then_inc(s_res, 1)

                def relu(q, b):
                    act.wait_ge(s_add, q + 1)
                    S.activation(g_ad[:, b, :, :], g_ad[:, b, :, :], ACT.Relu).then_inc(s_relu, 1)

                def window_sums(w):
                    act.wait_ge(s_sum, 2 * w + 2)
                    if past(w, 1):
                        act.wait_ge(s_dst, 16 * w)
                    S.copy(wres[:, :], p_win[0:W, 0:D]).then_inc(s_wev, 1)

                def transposed(q):
                    act.wait_ge(s_T, q + 1)
                    S.copy(hotT[:, :, :], p_x[0:3 * W, :, :]).then_inc(s_hotT, 1)

                def high(w):
                    act.wait_ge(s_win, 48 * (w + 1))
                    if past(w, 1):
                        act.wait_ge(s_t1, w)
                    S.copy(hi[:, :], win[:, :]).then_inc(s_h, 1)

                def middle(w):
                    act.wait_ge(s_t1, w + 1)
                    if past(w, 1):
                        act.wait_ge(s_wout, w)
                    S.copy(m1[:, :], t1[:, :]).then_inc(s_m1, 1)

                def step(i, b):
                    s = 2 * i + b
                    if b == 1 and ok(i + 1, NW):
                        middle(i + 1)
                    if ok(s - 1):
                        results(s - 1, 1 - b, i - 1 + b)
                    if b == 0 and ok(i - 1, NW):
                        window_sums(i - 1)
                    if ok(s):
                        relu(s, b)
                    if b == 0 and ok(i + 1, NW):
                        high(i + 1)
                    if ok(s + 1):
                        transposed(s + 1)
                narrow = act.value_load(narrow_i[0:1, 0:1], min_val=0, max_val=1)
                with act.If(narrow):
                    pipe(act, step)
                with act.Else():
                    with act.Fori(0, NQ) as q:
                        act.wait_ge(s_add, q + 1)
                        S.activation(g_ad[:, 0, :, :], g_ad[:, 0, :, :], ACT.Relu).then_inc(s_relu, 1)
                        for u in range(U):
                            act.wait_ge(s_sum, U * q + u + 1)
                            S.copy(gres[:, u, :], p_bc[:, u, :]).then_inc(s_res, 1)

            @block.tensor
            def _(pe):
                T = nc.tensor

                def rows(q, b, w):
                    pe.wait_ge(s_srow, 16 * (w + 1))
                    if past(q, 1):
                        pe.wait_ge(s_hotT, q)
                    for u in range(U):
                        last = T.matmul(p_x[:, u, :], sel[:, U * b + u, :], srow[:, :], start=True, stop=True)
                    last.then_inc(s_row, 1)

                def spread(q, b, w):
                    pe.wait_ge(s_hotT, q + 1)
                    pe.wait_ge(s_wout, w + 1)
                    if past(q, 1):
                        pe.wait_ge(s_add, q)
                    for u in range(U):
                        last = T.matmul(p_bc[:, u, :], hotT[:, u, :], winb[:, :], start=True, stop=True)
                    last.then_inc(s_exp, 1)

                def sums(q, b, w):
                    pe.wait_ge(s_relu, q + 1)
                    for r in range(2):
                        if past(q, 1):
                            pe.wait_ge(s_res, 2 * q - 1 + r)
                        for u in (2 * r, 2 * r + 1):
                            last = T.matmul(p_res[:, r, (u % 2) * D:(u % 2 + 1) * D], same[:, b, u, :],
                                            g_ad[:, b, u, 0:D], start=True, stop=True)
                        last.then_inc(s_dd, 1)
                    if b == 0 and past(w, 1):
                        pe.wait_ge(s_wev, w)
                    for u in range(U):
                        last = T.matmul(p_win[0:W, 0:D], hot[:, b, u, 0:W], g_ad[:, b, u, D:2 * D],
                                        start=(b == 0 and u == 0), stop=(b == 1 and u == U - 1))
                    last.then_inc(s_sum, 1)

                def transposes(q, b):
                    pe.wait_ge(s_hot, q + 1)
                    pe.wait_ge(s_same, q + 1)
                    for u in range(U):
                        last = T.transpose(p_x[0:3 * W, u, :], hot[:, b, u, :], ident[:, :])
                    last.then_inc(s_T, 1)

                def step(i, b):
                    s = 2 * i + b
                    if ok(s + 1):
                        rows(s + 1, 1 - b, i + b)
                    if ok(s):
                        spread(s, b, i)
                    if ok(s - 1):
                        sums(s - 1, 1 - b, i - 1 + b)
                    if ok(s + 1):
                        transposes(s + 1, 1 - b)
                narrow = pe.value_load(narrow_i[0:1, 0:1], min_val=0, max_val=1)
                with pe.If(narrow):
                    pipe(pe, step)
                with pe.Else():
                    def group(q, first):
                        pe.wait_ge(s_small, 6 * q + 1)
                        for half in range(2):
                            if half or not first:
                                pe.wait_ge(s_same, 2 * q + half)
                            for c in range(U):
                                last = T.transpose(p_x[:, c, :],
                                                   idf[:, half * U + c:half * U + c + 1].to_broadcast([128, 128]),
                                                   ident[:, :])
                            last.then_inc(s_row, 1)
                        pe.wait_ge(s_same, 2 * q + 2)
                        pe.wait_ge(s_relu, q + 1)
                        for u in range(U):
                            if not first:
                                pe.wait_ge(s_res, U * (q - 1) + u + 1)
                            for k in range(2):
                                last = T.matmul(p_bc[:, u, k * D:(k + 1) * D], sG[:, 2 * u + k, :],
                                                g_ad[:, 0, u, k * D:(k + 1) * D], start=True, stop=True)
                            last.then_inc(s_sum, 1)
                    group(0, True)
                    with pe.Fori(1, NQ) as q:
                        group(q, False)


def live(t):
    return not isinstance(t, int) or 0 <= t < TT


def again(t):
    return not isinstance(t, int) or t >= 2


def landed(t, b):
    return 8 * (t - b) + 16


def pipeline(eng, step):
    for s in (-1, 0, 1):
        step(s, s % 2)
    with eng.Fori(1, TT // 2 - 1) as i:
        for b in range(2):
            step(2 * i + b, b)
    for s in (TT - 2, TT - 1, TT):
        step(s, s % 2)


def nodes(nc, a, sem, sb, ps, acc, ident, x_sb, keep, mixw, logits):
    with ExitStack() as st:
        wo = sb(st, "wo", [128, 4, D])
        wr = sb(st, "wr", [128, 2, D])
        gw = sb(st, "gw", [128, 2, NE])
        bh = sb(st, "bh", [128, 2, D])
        bm = sb(st, "bm", [128, D])
        bg = sb(st, "bg", [128, NE])
        eps = sb(st, "eps2", [128, 1])
        part = sb(st, "nparts", [128, 2, NACC, D])
        xc = sb(st, "xc", [128, 2, 2, P])
        mT = sb(st, "mT", [128, 2, 4, P])
        hb = sb(st, "hb", [128, 2, D])
        mb = sb(st, "mb", [128, 2, D])
        stats = sb(st, "stats2", [128, 2, 6])
        mv = sb(st, "mv2", [128, 2, 2])
        std = sb(st, "std2", [128, 2])
        x2T = sb(st, "x2T", [128, 2, 2, P])
        p_mT = ps(st, "p_mT", [128, 2, 512])
        p_h = ps(st, "p_h", [128, 2, 512])
        p_xT = ps(st, "p_xT", [128, 2, 512])
        p_g = ps(st, "p_g", [128, 2, 512])

        s_w = sem("n_w")
        s_ld = [sem(f"n_ld{b}") for b in range(2)]
        s_const = sem("n_const")
        s_half = sem("n_half")
        s_msg = sem("n_msg")
        s_xc = sem("n_xc")
        s_xb = sem("n_xb")
        s_mT = sem("n_mT")
        s_mTc = sem("n_mTc")
        s_h = sem("n_h")
        s_hb = sem("n_hb")
        s_ln = sem("n_ln")
        s_var = sem("n_var")
        s_std = sem("n_std")
        s_xn2 = sem("n_xn2")
        s_xT = sem("n_xT")
        s_xTc = sem("n_xTc")
        s_gate = sem("n_gate")
        s_lg = sem("n_lg")
        rows = acc.rearrange("(c r) d -> r c d", r=AROWS)[0:N, :, :].rearrange("(p t) c d -> p t c d", t=TT)

        block = st.enter_context(nc.Block())

        @block.sync
        def _(sp):
            sp.dma_start(wo[:, :, :], a["L0_gnn_Wo"].rearrange("(k p) n -> p k n", p=128)).then_inc(s_w, 16)
            sp.dma_start(wr[:, :, :], a["L0_gnn_Wr"].rearrange("(k p) n -> p k n", p=128)).then_inc(s_w, 16)
            sp.dma_start(gw[:, :, :], a["L0_ffn_gate_w"].rearrange("(k p) n -> p k n", p=128)).then_inc(s_w, 16)
            for dst, name, n in ((bh[:, 0, :], "L0_gnn_bo", D), (bh[:, 1, :], "L0_gnn_br", D),
                                 (bm[:, :], "L0_mix_bo", D), (bg[:, :], "L0_ffn_gate_b", NE)):
                sp.dma_start(dst, a[name].unsqueeze(0).to_broadcast([128, n])).then_inc(s_w, 16)

            def step(s, b):
                t = s + 1
                if live(t):
                    if again(t):
                        sp.wait_ge(s_mT, t - 1)
                    sp.dma_start(part[0:P, 1 - b, :, :],
                                 rows[:, bass.ds(t, 1), :, :].rearrange("p t c d -> p (t c) d")
                                 ).then_inc(s_ld[1 - b], 16)
            pipeline(sp, step)

        @block.gpsimd
        def _(pool):
            pool.wait_ge(s_w, 16 * 7)

            def step(s, b):
                if live(s):
                    if again(s):
                        pool.wait_ge(s_h, s - 1)
                    pool.tensor_copy(xc[:, b, :, :].rearrange("p k n -> p (k n)").unsqueeze(1),
                                     keep[:, bass.ds(s, 1), 0:2 * P]).then_inc(s_xc, 1)
                    pool.tensor_tensor(x_sb[0:P, bass.ds(s, 1), :], x_sb[0:P, bass.ds(s, 1), :],
                                       bm[0:P, :].unsqueeze(1), ALU.add).then_inc(s_xb, 1)
            pipeline(pool, step)

        @block.vector
        def _(dve):
            nc.vector.memset(eps[:, :], EPS).then_inc(s_const, 1)
            dve.wait_ge(s_w, 16 * 7)
            nc.vector.tensor_tensor(bh[:, 0, :], bh[:, 0, :], bh[:, 1, :], ALU.add).then_inc(s_const, 1)
            dve.wait_ge(s_const, 2)

            def message_sums(t, b):
                dve.wait_ge(s_ld[b], landed(t, b))
                nc.vector.tensor_tensor(part[0:P, b, 0:2, :], part[0:P, b, 0:2, :], part[0:P, b, 2:4, :],
                                        ALU.add).then_inc(s_half, 1)
                dve.wait_ge(s_half, t + 1)
                nc.vector.tensor_tensor(part[0:P, b, 3, :], part[0:P, b, 0, :], part[0:P, b, 1, :],
                                        ALU.add).then_inc(s_msg, 1)

            def finish_layer(t, b):
                dve.wait_ge(s_h, t + 1)
                link = chain(dve, s_ln, 5 * t)
                nc.vector.tensor_tensor(hb[0:P, b, :], p_h[0:P, b, 0:D], bh[0:P, 0, :], ALU.add).then_inc(s_hb, 1)
                dve.wait_ge(s_xb, t + 1)
                link(nc.vector.tensor_tensor(mb[0:P, b:b + 1, :], p_h[0:P, b:b + 1, D:2 * D],
                                             x_sb[0:P, bass.ds(t, 1), :], ALU.add))
                dve.wait_ge(s_hb, 2 * t + 1)
                link(nc.vector.scalar_tensor_tensor(mb[0:P, b, :], hb[0:P, b, :], 0.0, mb[0:P, b, :],
                                                    ALU.max, ALU.add))
                link(nc.vector.bn_stats(stats[0:P, b, :], mb[0:P, b, :]))
                nc.vector.tensor_scalar_mul(x_sb[0:P, bass.ds(t, 1), :], mb[0:P, b:b + 1, :], 1.0).then_inc(s_hb, 1)
                nc.vector.bn_aggr(mv[0:P, b, :], stats[0:P, b, :]).then_inc(s_var, 1)
                dve.wait_ge(s_std, t + 1)
                link(nc.vector.reciprocal(std[0:P, b:b + 1], std[0:P, b:b + 1]))
                link(nc.vector.tensor_scalar(mb[0:P, b, :], mb[0:P, b, :], mv[0:P, b, 0:1], std[0:P, b:b + 1],
                                             ALU.subtract, ALU.mult))
                dve.wait_ge(s_xc, t + 1)
                nc.vector.tensor_scalar_mul(keep[0:P, bass.ds(t, 1), :], mb[0:P, b:b + 1, :], 1.0).then_inc(s_xn2, 1)

            def step(s, b):
                if live(s + 1):
                    message_sums(s + 1, 1 - b)
                if live(s - 1):
                    dve.wait_ge(s_gate, s)
                    nc.vector.tensor_tensor(logits[0:P, bass.ds(s - 1, 1), :], p_g[0:P, 1 - b:2 - b, 0:NE],
                                            bg[0:P, :].unsqueeze(1), ALU.add).then_inc(s_lg, 1)
                if live(s):
                    if again(s):
                        dve.wait_ge(s_xT, s - 1)
                    finish_layer(s, b)
            pipeline(dve, step)

        @block.scalar
        def _(act):
            def step(s, b):
                t = s + 1
                if live(t):
                    act.wait_ge(s_mT, t + 1)
                    if again(t):
                        act.wait_ge(s_h, t - 1)
                    nc.scalar.copy(mT[:, 1 - b, :, :].rearrange("p k n -> p (k n)"), p_mT[:, 1 - b, 0:4 * P]
                                   ).then_inc(s_mTc, 1)
                t = s - 1
                if live(t):
                    act.wait_ge(s_xT, t + 1)
                    if again(t):
                        act.wait_ge(s_gate, t - 1)
                    nc.scalar.copy(x2T[:, 1 - b, :, :].rearrange("p k n -> p (k n)"), p_xT[:, 1 - b, 0:2 * P]
                                   ).then_inc(s_xTc, 1)
                if live(s):
                    act.wait_ge(s_var, s + 1)
                    nc.scalar.activation(std[0:P, b:b + 1], mv[0:P, b, 1:2], ACT.Sqrt, bias=eps[0:P, :]
                                         ).then_inc(s_std, 1)
            act.wait_ge(s_const, 2)
            pipeline(act, step)

        @block.tensor
        def _(pe):
            pe.wait_ge(s_w, 16 * 7)

            def step(s, b):
                t = s + 1
                if live(t):
                    pe.wait_ge(s_msg, t + 1)
                    if again(t):
                        pe.wait_ge(s_mTc, t - 1)
                    for k in range(4):
                        last = nc.tensor.transpose(p_mT[:, 1 - b, k * P:(k + 1) * P],
                                                   part[0:P, 1 - b, 3 + k // 2, (k % 2) * 128:(k % 2 + 1) * 128], ident[0:P, 0:P])
                    last.then_inc(s_mT, 1)
                t = s - 1
                if live(t):
                    pe.wait_ge(s_xn2, t + 1)
                    if again(t):
                        pe.wait_ge(s_xTc, t - 1)
                    for k in range(2):
                        last = nc.tensor.transpose(p_xT[:, 1 - b, k * P:(k + 1) * P],
                                                   mb[0:P, 1 - b, k * 128:(k + 1) * 128], ident[0:P, 0:P])
                    last.then_inc(s_xT, 1)
                if live(s):
                    pe.wait_ge(s_mTc, s + 1)
                    pe.wait_ge(s_xc, s + 1)
                    if again(s):
                        pe.wait_ge(s_hb, 2 * s - 2)
                        pe.wait_ge(s_ln, 5 * s - 9)
                    for k in range(6):
                        nc.tensor.matmul(p_h[0:P, b, 0:D], mT[:, b, k, :] if k < 4 else xc[:, b, k - 4, :],
                                         wo[:, k, :] if k < 4 else wr[:, k - 4, :], start=(k == 0), stop=(k == 5))
                    for k in range(2):
                        last = nc.tensor.matmul(p_h[0:P, b, D:2 * D], xc[:, b, k, :], mixw[:, k, :],
                                                start=(k == 0), stop=(k == 1))
                    last.then_inc(s_h, 1)
                if live(t):
                    pe.wait_ge(s_xTc, t + 1)
                    if again(t):
                        pe.wait_ge(s_lg, t - 1)
                    for k in range(2):
                        last = nc.tensor.matmul(p_g[0:P, 1 - b, 0:NE], x2T[:, 1 - b, k, :], gw[:, k, :],
                                                start=(k == 0), stop=(k == 1))
                    last.then_inc(s_gate, 1)
            pipeline(pe, step)


def route(nc, sem, sb, ps, buf, upper, pcol, keep, logits, slot_g, gate_p):
    with ExitStack() as st:
        probs = sb(st, "probs", [128, TT, NE])
        hot = sb(st, "hot", [128, TT, NE])
        before = sb(st, "before", [128, TT, NE])
        tmp = sb(st, "tmp", [128, TT, NE])
        ones = sb(st, "ones", [128, TT])
        rank = sb(st, "rank", [128, 2, NE])
        col = sb(st, "col", [128, 5, TT])
        junk = sb(st, "junk2", [128, TT])
        offs = sb(st, "offs", [128, NE])
        dest = sb(st, "dest", [128, TT])
        dslot = sb(st, "dslot", [128, 2], I32)
        rowst = sb(st, "rowst", [128, 2, D])
        p_off = ps(st, "p_off", [128, 512])
        s_c = sem("r_chain")
        s_shift = sem("r_shift")
        s_exp = sem("r_exp")
        s_tot = sem("r_tot")
        s_off = sem("r_off")
        s_stage = sem("r_stage")
        s_turn = sem("r_turn")
        s_sc = [sem(f"r_sc{b}") for b in range(2)]

        block = st.enter_context(nc.Block())

        @block.scalar
        def _(act):
            act.wait_ge(s_shift, 1)
            nc.scalar.activation(probs[0:P, :, :], tmp[0:P, :, :], ACT.Exp).then_inc(s_exp, 1)

        @block.tensor
        def _(pe):
            pe.wait_ge(s_tot, 1)
            nc.tensor.matmul(p_off[0:P, 0:NE], upper[0:P, 0:P], before[0:P, TT - 1, :], start=True, stop=True
                             ).then_inc(s_off, 1)

        @block.vector
        def _(dve):
            link = chain(dve, s_c)
            V = nc.vector
            top, total, pos, base, kept = (col[0:P, k, :] for k in range(5))
            lg, pr, ht, bf, tm = (x[0:P, :, :] for x in (logits, probs, hot, before, tmp))

            def wide(v):
                return v.unsqueeze(2).to_broadcast([P, TT, NE])
            for e in range(NE):
                link(V.memset(rank[:, 0, e:e + 1], float(NE - e)))
                link(V.memset(rank[:, 1, e:e + 1], float(e * CP)))
            link(V.memset(ones[:, :], 1.0))
            for b in range(2):
                link(V.memset(junk[:, b::2], float(NE * CP + 128 * b)))
            link(V.tensor_scalar_add(junk[:, :], junk[:, :], pcol[:, :]))
            link(V.tensor_reduce(top, lg, AXX, ALU.max))
            V.tensor_tensor(tm, lg, wide(top), ALU.subtract).then_inc(s_shift, 1)
            dve.wait_ge(s_exp, 1)
            link(V.tensor_reduce(total, pr, AXX, ALU.add))
            link(V.reciprocal(total, total))
            link(V.tensor_tensor(pr, pr, wide(total), ALU.mult))
            link(V.tensor_reduce(top, pr, AXX, ALU.max))
            link(V.tensor_tensor(tm, pr, wide(top), ALU.is_equal))
            link(V.tensor_tensor(tm, tm, rank[0:P, 0:1, :].to_broadcast([P, TT, NE]), ALU.mult))
            link(V.tensor_reduce(pos, tm, AXX, ALU.max))
            link(V.tensor_tensor(ht, tm, wide(pos), ALU.is_equal))
            for e in range(NE):
                last = V.tensor_tensor_scan(before[0:P, :, e], ones[0:P, :], hot[0:P, :, e], 0.0, ALU.mult, ALU.add)
            last.then_inc(s_tot, 1)
            dve.wait_ge(s_off, 1)
            link(V.tensor_copy(offs[0:P, :], p_off[0:P, 0:NE]))
            link(V.tensor_tensor(tm, bf, offs[0:P, :].unsqueeze(1).to_broadcast([P, TT, NE]), ALU.add))
            link(V.tensor_tensor(tm, tm, ht, ALU.mult))
            link(V.tensor_reduce(pos, tm, AXX, ALU.add))
            link(V.tensor_tensor(tm, ht, rank[0:P, 1:2, :].to_broadcast([P, TT, NE]), ALU.mult))
            link(V.tensor_reduce(base, tm, AXX, ALU.add))
            link(V.tensor_scalar(kept, pos, float(C), None, ALU.is_le))
            link(V.tensor_tensor(gate_p[0:P, :], top, kept, ALU.mult))
            link(V.tensor_tensor(dest[0:P, :], base, pos, ALU.add))
            link(V.scalar_tensor_tensor(dest[0:P, :], dest[0:P, :], -1.0, junk[0:P, :], ALU.add, ALU.subtract))
            link(V.tensor_tensor(dest[0:P, :], dest[0:P, :], kept, ALU.mult))
            link(V.tensor_tensor(dest[0:P, :], dest[0:P, :], junk[0:P, :], ALU.add))
            link(V.tensor_scalar(pos, pos, float(C), -1.0, ALU.min, ALU.add))
            link(V.tensor_tensor(slot_g[0:P, :], base, pos, ALU.add))

            def stage(t, b, h):
                if again(t):
                    dve.wait_ge(s_sc[b], h)
                V.tensor_copy(dslot[0:P, b:b + 1], dest[0:P, bass.ds(t, 1)])
                V.tensor_copy(rowst[0:P, b:b + 1, :], keep[0:P, bass.ds(t, 1), :]).then_inc(s_stage, 1)
            stage(0, 0, 0)
            stage(1, 1, 0)
            with dve.Fori(1, TT // 2) as i:
                for b in range(2):
                    stage(2 * i + b, b, 16 * i)

        @block.gpsimd
        def _(pool):
            with pool.Fori(0, TT // 2) as i:
                for b in range(2):
                    pool.wait_ge(s_stage, 2 * i + b + 1)
                    pool.sem_inc(s_turn)
                    pool.indirect_dma_start(buf, bass.IndirectOffsetOnAxis(dslot[0:P, b:b + 1], 0),
                                            rowst[0:P, b, :], None).then_inc(s_sc[b], 16)
            pool.wait_ge(s_sc[0], 16 * (TT // 2))
            pool.wait_ge(s_sc[1], 16 * (TT // 2))


def experts(nc, a, sem, sb, ps, buf, ybuf, ident):
    J = CP // 128
    F = NF // 128
    with ExitStack() as st:
        w1 = sb(st, "w1", [128, 2, 2, NF])
        w2 = sb(st, "w2", [128, 2, F, D])
        b2 = sb(st, "b2", [128, 2, D])
        tok = sb(st, "tok", [128, J, D])
        tokT = sb(st, "tokT", [128, 2, CP])
        hT = sb(st, "hT", [128, F, CP])
        y = sb(st, "y", [128, J, D])
        b1r = sb(st, "b1r", [NE * F, 128])
        b1T = sb(st, "b1T", [128, NE * F])
        b1c = sb(st, "b1c", [128, F])
        p_t = ps(st, "p_t", [128, 2, 512])
        p_h = ps(st, "p_hid", [128, 4, 512])
        p_y = ps(st, "p_y", [128, 2, 512])

        s_b1 = sem("x_b1")
        s_b1T = sem("x_b1T")
        s_b1c = sem("x_b1c")
        s_w = [sem(f"x_w{b}") for b in range(2)]
        s_tok = sem("x_tok")
        s_T = sem("x_T")
        s_Tc = sem("x_Tc")
        s_h = sem("x_h")
        s_hr = sem("x_hr")
        s_y = sem("x_y")
        s_yc = sem("x_yc")
        s_st = sem("x_st")
        tok_d = buf[0:NE * CP, :].rearrange("(e p j) d -> p e j d", p=128, j=J)
        y_d = ybuf.rearrange("(e p j) d -> p e j d", p=128, j=J)
        w1_d = a["L0_ffn_w1"].rearrange("e (k p) f -> p e k f", p=128)
        w2_d = a["L0_ffn_w2"].rearrange("e (f p) d -> p e f d", p=128)
        GH = 2 * F

        block = st.enter_context(nc.Block())

        @block.sync
        def _(sp):
            sp.dma_start(b1r[:, :], a["L0_ffn_b1"].rearrange("e (f p) -> (e f) p", p=128)).then_inc(s_b1, 16)

            def load(e, b, first):
                if not first:
                    sp.wait_ge(s_T, 4 * e)
                sp.dma_start(tok[:, :, :].unsqueeze(1), tok_d[:, bass.ds(e, 1), :, :]).then_inc(s_tok, 16)
                if not first:
                    sp.wait_ge(s_yc, J * (e - 1))
                sp.dma_start(w1[:, b:b + 1, :, :], w1_d[:, bass.ds(e, 1), :, :]).then_inc(s_w[b], 16)
                sp.dma_start(w2[:, b:b + 1, :, :], w2_d[:, bass.ds(e, 1), :, :]).then_inc(s_w[b], 16)
                sp.dma_start(b2[:, b:b + 1, :], a["L0_ffn_b2"][bass.ds(e, 1), :].unsqueeze(0).to_broadcast([128, 1, D])
                             ).then_inc(s_w[b], 16)
            load(0, 0, True)
            sp.wait_ge(s_T, 4)
            sp.dma_start(tok[:, :, :].unsqueeze(1), tok_d[:, 1:2, :, :]).then_inc(s_tok, 16)
            sp.dma_start(w1[:, 1:2, :, :], w1_d[:, 1:2, :, :]).then_inc(s_w[1], 16)
            sp.dma_start(w2[:, 1:2, :, :], w2_d[:, 1:2, :, :]).then_inc(s_w[1], 16)
            sp.dma_start(b2[:, 1:2, :], a["L0_ffn_b2"][1:2, :].unsqueeze(0).to_broadcast([128, 1, D])
                         ).then_inc(s_w[1], 16)
            with sp.Fori(1, NE // 2) as i:
                for b in range(2):
                    load(2 * i + b, b, False)

        @block.gpsimd
        def _(pool):
            with pool.Fori(0, NE) as e:
                pool.wait_ge(s_yc, J * e + J)
                pool.dma_start(y_d[:, bass.ds(e, 1), :, :], y[:, :, :].unsqueeze(1)).then_inc(s_st, 16)
            pool.wait_ge(s_st, 16 * NE)

        @block.scalar
        def _(act):
            act.wait_ge(s_b1T, 2)

            def hidden(e, b, first):
                act.wait_ge(s_b1c, e + 1)
                if not first:
                    act.wait_ge(s_y, J * e)
                for g in range(GH):
                    f, half = g // 2, g % 2
                    act.wait_ge(s_h, GH * e + g + 1)
                    nc.scalar.activation(hT[:, f, half * 512:(half + 1) * 512], p_h[:, g % 4, :], ACT.Relu,
                                         bias=b1c[:, f:f + 1]).then_inc(s_hr, 1)
            hidden(0, 0, True)
            with act.Fori(1, NE) as e:
                hidden(e, 0, False)

        @block.vector
        def _(dve):
            dve.wait_ge(s_b1T, 1)
            nc.vector.tensor_copy(b1T[:, :], p_t[:, 0, 0:NE * F]).then_inc(s_b1T, 1)
            dve.wait_ge(s_b1T, 2)

            def expert(e, b, h, first):
                if not first:
                    dve.wait_ge(s_hr, GH * e)
                nc.vector.tensor_copy(b1c[:, :], b1T[:, bass.ds(F * e, F)]).then_inc(s_b1c, 1)
                for q in range(4):
                    dve.wait_ge(s_T, 4 * e + q + 1)
                    if q == 0 and not first:
                        dve.wait_ge(s_h, GH * e)
                    nc.vector.tensor_copy(tokT[:, q // 2, (q % 2) * 512:(q % 2 + 1) * 512], p_t[:, q % 2, :]
                                          ).then_inc(s_Tc, 1)
                if not first:
                    dve.wait_ge(s_st, 16 * e)
                dve.wait_ge(s_w[b], h)
                for j in range(J):
                    dve.wait_ge(s_y, J * e + j + 1)
                    nc.vector.tensor_tensor(y[:, j, :], p_y[:, j % 2, 0:D], b2[:, b, :], ALU.add).then_inc(s_yc, 1)
            expert(0, 0, 48, True)
            expert(1, 1, 48, False)
            with dve.Fori(1, NE // 2) as i:
                for b in range(2):
                    expert(2 * i + b, b, 48 * i + 48, False)

        @block.tensor
        def _(pe):
            pe.wait_ge(s_b1, 16)
            nc.tensor.transpose(p_t[:, 0, 0:NE * F], b1r[:, :], ident[0:NE * F, 0:NE * F]).then_inc(s_b1T, 1)
            pe.wait_ge(s_b1T, 2)

            def expert(e, b, h, first):
                pe.wait_ge(s_tok, 16 * e + 16)
                for q in range(4):
                    if q >= 2:
                        pe.wait_ge(s_Tc, 4 * e + q - 1)
                    elif not first:
                        pe.wait_ge(s_Tc, 4 * e + q - 1)
                    for r in range(4):
                        last = nc.tensor.transpose(p_t[:, q % 2, r * 128:(r + 1) * 128],
                                                   tok[:, (q % 2) * 4 + r, (q // 2) * 128:(q // 2 + 1) * 128],
                                                   ident[:, :])
                    last.then_inc(s_T, 1)
                pe.wait_ge(s_w[b], h)
                pe.wait_ge(s_Tc, 4 * e + 4)
                for g in range(GH):
                    f, half = g // 2, g % 2
                    if g >= 4:
                        pe.wait_ge(s_hr, GH * e + g - 3)
                    elif not first:
                        pe.wait_ge(s_hr, GH * e + g - 3)
                    for k in range(2):
                        last = nc.tensor.matmul(p_h[:, g % 4, :], w1[:, b, k, f * 128:(f + 1) * 128],
                                                tokT[:, k, half * 512:(half + 1) * 512],
                                                start=(k == 0), stop=(k == 1))
                    last.then_inc(s_h, 1)
                pe.wait_ge(s_hr, GH * e + GH)
                for j in range(J):
                    if j >= 2:
                        pe.wait_ge(s_yc, J * e + j - 1)
                    elif not first:
                        pe.wait_ge(s_yc, J * e + j - 1)
                    for f in range(F):
                        last = nc.tensor.matmul(p_y[:, j % 2, 0:D], hT[:, f, j * 128:(j + 1) * 128], w2[:, b, f, :],
                                                start=(f == 0), stop=(f == F - 1))
                    last.then_inc(s_y, 1)
            expert(0, 0, 48, True)
            expert(1, 1, 48, False)
            with pe.Fori(1, NE // 2) as i:
                for b in range(2):
                    expert(2 * i + b, b, 48 * i + 48, False)


def finish(nc, sem, sb, ybuf, x_sb, slot_g, gate_p, out):
    Q = 5
    BIG = 3.4028234e38
    with ExitStack() as st:
        islot = sb(st, "islot", [128, 2], I32)
        yg = sb(st, "yg", [128, 2, D])
        sc = sb(st, "sc", [128, 2, D])
        odd = sb(st, "odd", [128, 2, D])
        sub = sb(st, "sub", [128, 2, 2, D])
        s_i = sem("f_i")
        s_turn = sem("f_turn")
        s_g = [sem(f"f_g{b}") for b in range(2)]
        s_y = sem("f_y")
        s_odd = sem("f_odd")
        s_a = sem("f_a")
        s_sub = sem("f_sub")
        s_fix = sem("f_fix")
        s_x = sem("f_x")
        s_out = sem("f_out")
        rows = out.rearrange("(p t) d -> p t d", t=TT)
        block = st.enter_context(nc.Block())

        @block.gpsimd
        def _(pool):
            def gather(t, b):
                pool.wait_ge(s_i, t + 1)
                pool.sem_inc(s_turn)
                pool.indirect_dma_start(yg[0:P, b, :], None, ybuf,
                                        bass.IndirectOffsetOnAxis(islot[0:P, b:b + 1], 0)).then_inc(s_g[b], 16)

            def substitute(t, b):
                pool.wait_ge(s_y, t + 1)
                if again(t):
                    pool.wait_ge(s_fix, t - 1)
                pool.sem_inc(s_turn)
                pool.tensor_scalar(sub[0:P, b, 0, :], sc[0:P, b, :], BIG, 1e4, ALU.is_gt, ALU.mult).then_inc(s_a, 1)
                pool.tensor_scalar(sub[0:P, b, 1, :], sc[0:P, b, :], -BIG, -1e4, ALU.is_lt, ALU.mult).then_inc(s_a, 1)
                pool.wait_ge(s_a, 2 * t + 2)
                pool.tensor_tensor(sub[0:P, b, 0, :], sub[0:P, b, 0, :], sub[0:P, b, 1, :], ALU.add).then_inc(s_sub, 1)

            def step(s, b):
                if live(s + 1):
                    gather(s + 1, 1 - b)
                if live(s):
                    substitute(s, b)
            pipeline(pool, step)

        @block.scalar
        def _(act):
            def step(s, b):
                if live(s):
                    act.wait_ge(s_y, s + 1)
                    if again(s):
                        act.wait_ge(s_fix, s - 1)
                    nc.scalar.activation(odd[0:P, b, :], sc[0:P, b, :], ACT.Square, scale=0.0).then_inc(s_odd, 1)
            pipeline(act, step)

        @block.vector
        def _(dve):
            def step(s, b):
                t = s + 1
                if live(t):
                    if again(t):
                        dve.wait_ge(s_y, t - 1)
                    nc.vector.tensor_copy(islot[0:P, 1 - b:2 - b], slot_g[0:P, bass.ds(t, 1)]).then_inc(s_i, 1)
                if live(s):
                    dve.wait_ge(s_g[b], landed(s, b))
                    if again(s):
                        dve.wait_ge(s_x, s - 1)
                    nc.vector.tensor_scalar(sc[0:P, b, :], yg[0:P, b, :], gate_p[0:P, bass.ds(s, 1)], None, ALU.mult
                                            ).then_inc(s_y, 1)
                t = s - 1
                if live(t):
                    dve.wait_ge(s_odd, t + 1)
                    dve.wait_ge(s_sub, t + 1)
                    dve.sem_inc(s_turn)
                    nc.vector.copy_predicated(sc[0:P, 1 - b, :], odd[0:P, 1 - b, :].bitcast(I32), sub[0:P, 1 - b, 0, :]
                                              ).then_inc(s_fix, 1)
                    dve.wait_ge(s_fix, t + 1)
                    nc.vector.tensor_tensor(x_sb[0:P, bass.ds(t, 1), :], x_sb[0:P, bass.ds(t, 1), :],
                                            sc[0:P, 1 - b:2 - b, :], ALU.add).then_inc(s_x, 1)
            pipeline(dve, step)

        @block.sync
        def _(sp):
            with sp.Fori(0, TT // Q) as i:
                sp.wait_ge(s_x, Q * i + Q)
                sp.dma_start(rows[:, bass.ds(Q * i, Q), :], x_sb[0:P, bass.ds(Q * i, Q), :]).then_inc(s_out, 16)
            sp.wait_ge(s_out, 16 * (TT // Q))


_NAMES = ["x", "src", "dst", "L0_gnn_W1_1", "L0_gnn_b1_1", "L0_gnn_W2_1", "L0_gnn_b2_1", "L0_gnn_W1_2",
          "L0_gnn_b1_2", "L0_gnn_W2_2", "L0_gnn_b2_2", "L0_gnn_Wo", "L0_gnn_bo", "L0_gnn_Wr", "L0_gnn_br",
          "L0_mix_wq", "L0_mix_bo", "L0_mix_ln_k_g", "L0_mix_ln_k_b", "L0_mix_ln_v_g", "L0_mix_ln_v_b",
          "L0_ffn_gate_w", "L0_ffn_gate_b", "L0_ffn_w1", "L0_ffn_b1", "L0_ffn_w2", "L0_ffn_b2"]
_TRANSPOSED = {"wkT": "L0_mix_wk", "wvT": "L0_mix_wv", "woT": "L0_mix_wo"}


def kernel(**inputs):
    import numpy as np
    import concourse.bacc as bacc
    from concourse.bass_utils import run_bass_kernel_spmd

    nc = bacc.Bacc("TRN2", target_bir_lowering=False, num_devices=1)
    arrays = {n: np.ascontiguousarray(inputs[n]) for n in _NAMES}
    arrays |= {n: np.ascontiguousarray(np.asarray(inputs[m]).T) for n, m in _TRANSPOSED.items()}
    a = {n: nc.dram_tensor("in_" + n, v.shape, mybir.dt.from_np(v.dtype), kind="ExternalInput").ap()
         for n, v in arrays.items()}
    out = nc.dram_tensor("out", (N, D), F32, kind="ExternalOutput").ap()
    graph_moe_kernel(nc, a, out)
    r = run_bass_kernel_spmd(nc, [{"in_" + n: v for n, v in arrays.items()}], core_ids=[0])
    return r.results[0]["out"]
```

```python
import concourse.bass as bass
from concourse import mybir
from contextlib import ExitStack

F32 = mybir.dt.float32
I32 = mybir.dt.int32
BF16 = mybir.dt.bfloat16
ALU = mybir.AluOpType
ACT = mybir.ActivationFunctionType
AXX = mybir.AxisListType.X

N = 6250
D = 256
P = 125
TT = N // P
E = 206250
SPLIT = (slice(0, 112), slice(112, P))
NJ = N
TROWS = 6400
AROWS = 6400
U = 4
NT = 1616
NQ = NT // U
WT = 2 * U
NW = NT // WT
W = 42
NACC = U + 1
H, HD = 4, 64
NE, C = 8, 977
CP = 1024
BR = -(-(NE * CP + 4 * 128) // NW)
JUNK = BR * NW - NE * CP
NF = 1024
EPS = 1e-5


def graph_moe_kernel(nc, a, out):
    ctx = ExitStack()
    with ctx:
        def sem(name):
            return ctx.enter_context(nc.semaphore(name))

        def sb(scope, name, shape, dt=F32):
            return scope.enter_context(nc.sbuf_tensor(name, shape, dt))

        def ps(scope, name, shape):
            return scope.enter_context(nc.psum_tensor(name, shape, F32))

        def dram(name, shape):
            return nc.dram_tensor(name, shape, F32, kind="Internal").ap()

        tab_ad = dram("tab_ad", [TROWS, 2 * D])
        tab_bc = dram("tab_bc", [TROWS, 2 * D])
        acc = dram("acc", [NACC * AROWS, D])
        a["srow"] = nc.dram_tensor("srow", [NT, 2, 128], BF16, kind="Internal").ap()
        buf = dram("buf", [NE * CP + JUNK, D])
        ybuf = dram("ybuf", [NE * CP, D])

        ident = sb(ctx, "ident", [128, 128])
        upper = sb(ctx, "upper", [128, 128])
        pcol_i = sb(ctx, "pcol_i", [128, 1], I32)
        pcol = sb(ctx, "pcol", [128, 1])
        x_sb = sb(ctx, "x_sb", [128, TT, D])
        keep = sb(ctx, "keep", [128, TT, D])
        slot_g = sb(ctx, "slot_g", [128, TT], I32)
        gate_p = sb(ctx, "gate_p", [128, TT])

        with ExitStack() as scope:
            ix = Index()
            ix.ids = sb(scope, "ids", [128, NT, 2])
            ix.copy_row = sb(scope, "copy_row", [128, 2 * U])
            ix.junk = sb(scope, "junk", [128, 2 * U])
            ix.rel = sb(scope, "rel", [128, NW, WT])
            ix.base_i = sb(scope, "base_i", [128, NW], I32)
            ix.narrow_i = sb(scope, "narrow_i", [1, 1], I32)
            ix.iota3 = sb(scope, "iota3", [128, 3 * W])
            ix.part = sb(scope, "part", [128, 2])
            ix.sel = sb(scope, "sel", [2 * WT, WT, 128], BF16)
            ix.delta = sb(scope, "delta", [128, NW])
            ix.diff = sb(scope, "diff", [128, W])

            project(nc, a, sem, sb, ps, tab_ad, tab_bc, acc, ident, upper, pcol_i, pcol,
                    x_sb, keep, ix)
            edges(nc, a, sem, sb, ps, tab_ad, tab_bc, acc, buf, ident, upper, pcol, x_sb, keep, ix)

        logits = sb(ctx, "logits", [128, TT, NE])
        nodes(nc, a, sem, sb, ps, acc, ident, x_sb, keep, logits)
        ex = Expert(a, sem, sb, ctx)
        route(nc, a, ex, sem, sb, ps, buf, upper, pcol, keep, logits, slot_g, gate_p)
        experts(nc, ex, sem, sb, ps, buf, ybuf, ident)
        finish(nc, sem, sb, ybuf, x_sb, slot_g, gate_p, out)


class Index:
    pass


def chain(eng, s, base=0):
    done = [0]

    def link(ins):
        done[0] += 1
        ins.then_inc(s, 1)
        eng.wait_ge(s, base + done[0])
    return link


def chain_at(eng, s):
    def link(count, ins):
        ins.then_inc(s, 1)
        eng.wait_ge(s, count)
    return link


def project(nc, a, sem, sb, ps, tab_ad, tab_bc, acc, ident, upper, pcol_i, pcol, x_sb,
            keep, ix):
    ZR = NACC * AROWS // 128 // TT
    RG = (NT + 127) // 128
    full = E // 128
    whole = (RG - 1) * 128
    with ExitStack() as st:
        ids, rel, base_i = ix.ids, ix.rel, ix.base_i
        copy_row, junk, narrow_i, iota3 = ix.copy_row, ix.junk, ix.narrow_i, ix.iota3
        part, sel, delta, diff = ix.part, ix.sel, ix.delta, ix.diff
        base_f = sb(st, "base_f", [128, NW])
        store = keep[:, :, :].rearrange("p t d -> p (t d)")
        raw = store[:, 0:RG * 256].bitcast(I32).rearrange("p (g k e) -> p g k e", g=RG, k=2)
        rowb = store[:, RG * 256:RG * 384].bitcast(BF16).rearrange("p (g k e) -> p g k e", g=RG, k=2)
        rawf = sb(st, "rawf", [128, 2, 2, 128])
        rowi = sb(st, "rowi", [128, 2, 2, 128], I32)
        row0 = sb(st, "row0", [128, 128])
        worst = sb(st, "worst", [128, 2])
        narrow_f = sb(st, "narrow_f", [1, 1])
        iota_i = sb(st, "iota_i", [128, 3, W], I32)
        self32 = sb(st, "self32", [2 * WT, WT, 128])
        diff_i = sb(st, "diff_i", [128, W], I32)
        w = sb(st, "w", [128, 2, 4 * D])
        bias4 = sb(st, "bias4", [128, 2, 2 * D])
        zero = sb(st, "zero", [128, ZR * D])
        eps = sb(st, "eps", [128, 1])
        stats = sb(st, "stats", [128, 2, 6])
        mv = sb(st, "mv", [128, 2, 2])
        rstd = sb(st, "rstd", [128, 2])
        xn = sb(st, "xn", [128, 2, D])
        xT = sb(st, "xT", [128, 2, 2, P])
        ad = sb(st, "ad", [128, 2, 2 * D])
        bc = sb(st, "bc", [128, 2, 2 * D])
        p_T = ps(st, "p_T", [128, 512])
        p_ad = ps(st, "p_ad", [128, 2, 512])
        p_bc = ps(st, "p_bc", [128, 2, 512])

        s_x = sem("a_x")
        s_raw = sem("e_raw")
        s_rawm = sem("e_rawm")
        s_turn = sem("a_turn")
        s_rawf = sem("e_rawf")
        s_rawT = sem("e_rawT")
        s_ids = sem("e_ids")
        s_rowb = sem("e_rowb")
        s_rowd = sem("e_rowd")
        s_base = sem("e_base")
        s_prep = sem("e_prep")
        s_worst = sem("e_worst")
        s_wide = sem("e_wide")
        s_cst = sem("e_cst")
        s_sel = sem("e_sel")
        s_w = sem("a_w")
        s_w2 = sem("a_w2")
        s_zst = sem("a_zst")
        s_acc = sem("a_acc")
        s_const = sem("a_const")
        s_memset = sem("a_memset")
        s_dv = sem("a_dv")
        s_stats = sem("a_stats")
        s_std0 = sem("a_std0")
        s_norm = sem("a_norm")
        s_rstd0 = sem("a_rstd0")
        s_T = sem("a_T")
        s_xT = sem("a_xT")
        s_kept = sem("a_kept")
        s_mad = sem("a_mad")
        s_mbc = sem("a_mbc")
        s_adc = sem("a_adc")
        s_bcc = sem("a_bcc")
        s_stad = [sem(f"a_stad{b}") for b in range(2)]
        s_stbc = [sem(f"a_stbc{b}") for b in range(2)]

        rows_ad = tab_ad[0:N, :].rearrange("(p t) d -> p t d", t=TT)
        rows_bc = tab_bc[0:N, :].rearrange("(p t) d -> p t d", t=TT)
        acc_z = acc.rearrange("(p k r) d -> p k (r d)", p=128, r=ZR)
        parts = [("L0_gnn_W1_1", 0), ("L0_gnn_W2_2", 1), ("L0_gnn_W2_1", 2), ("L0_gnn_W1_2", 3)]

        block = st.enter_context(nc.Block())

        @block.sync
        def _(sp):
            sp.wait_ge(s_rawm, 1)
            for k, name in enumerate(("src", "dst")):
                sp.dma_start(raw[:, 0:RG - 1, k, :],
                             a[name][0:(RG - 1) * 16384].rearrange("(g r e) -> r g e", r=128, e=128)).then_inc(s_raw, 16)
                sp.dma_start(raw[0:full - whole, RG - 1, k, :],
                             a[name][whole * 128:full * 128].rearrange("(r e) -> r e", e=128)).then_inc(s_raw, 16)
                sp.dma_start(raw[full - whole:full - whole + 1, RG - 1, k, 0:E - full * 128],
                             a[name][full * 128:E].unsqueeze(0)).then_inc(s_raw, 16)
            for name, c in parts:
                sp.dma_start(w[:, :, c * D:(c + 1) * D],
                             a[name].rearrange("(k p) n -> p k n", p=128)).then_inc(s_w, 16)
            for k, name in enumerate(("L0_gnn_b2_1", "L0_gnn_b1_2", "L0_gnn_b1_1", "L0_gnn_b2_2")):
                sp.dma_start(bias4[:, k // 2, (k % 2) * D:(k % 2 + 1) * D],
                             a[name].unsqueeze(0).to_broadcast([128, D])).then_inc(s_w2, 16)
            for r in SPLIT:
                sp.dma_start(x_sb[r, :, :], a["x"].rearrange("(p t) d -> p t d", t=TT)[r, :, :]).then_inc(s_x, 16)
            sp.wait_ge(s_rowb, RG)
            sp.dma_start(a["srow"][0:whole, :, :].rearrange("(g r) k e -> r g k e", r=128), rowb[:, 0:RG - 1, :, :]
                         ).then_inc(s_rowd, 16)
            sp.dma_start(a["srow"][whole:NT, :, :], rowb[0:NT - whole, RG - 1, :, :]).then_inc(s_rowd, 16)
            sp.wait_ge(s_rowd, 32)
            sp.wait_ge(s_dv, 1)

            def store(t, b):
                sp.wait_ge(s_adc, t + 1)
                for r in SPLIT:
                    sp.dma_start(rows_ad[r, bass.ds(t, 1), :], ad[r, b:b + 1, :]).then_inc(s_stad[b], 16)
                sp.wait_ge(s_bcc, t + 1)
                for r in SPLIT:
                    sp.dma_start(rows_bc[r, bass.ds(t, 1), :], bc[r, b:b + 1, :]).then_inc(s_stbc[b], 16)
                sp.dma_start(acc_z[:, bass.ds(t, 1), :], zero[:, :].unsqueeze(1)).then_inc(s_acc, 16)
            pipeline(sp, store, TT, 0, TT - 1, 0)
            sp.wait_ge(s_acc, 16 * TT)
            for b in range(2):
                sp.wait_ge(s_stad[b], 32 * (TT // 2))
                sp.wait_ge(s_stbc[b], 32 * (TT // 2))

        @block.gpsimd
        def _(pool):
            pool.memset(ident[:, :], 1.0).then_inc(s_memset, 1)
            pool.memset(upper[:, :], 1.0).then_inc(s_memset, 1)
            pool.iota(pcol_i[:, :], pattern=[[0, 1]], base=0, channel_multiplier=1).then_inc(s_memset, 1)
            pool.wait_ge(s_memset, 3)
            pool.affine_select(out=ident[:, :], in_=ident[:, :], compare_op=ALU.is_equal, fill=0.0, base=0,
                               pattern=[[-1, 128]], channel_multiplier=1).then_inc(s_const, 1)
            pool.affine_select(out=upper[:, :], in_=upper[:, :], compare_op=ALU.is_gt, fill=0.0, base=0,
                               pattern=[[1, 128]], channel_multiplier=-1).then_inc(s_const, 1)
            pool.tensor_copy(pcol[:, :], pcol_i[:, :]).then_inc(s_const, 1)
            pool.iota(iota_i[:, :, :], pattern=[[0, 3], [1, W]], base=0, channel_multiplier=0
                      ).then_inc(s_wide, 1)
            pool.iota(diff_i[:, :], pattern=[[-1, W]], base=0, channel_multiplier=1).then_inc(s_wide, 1)
            pool.memset(self32[:, :, :], 0.0).then_inc(s_sel, 1)
            for k, v in ((0, 128.0), (1, 1.0)):
                pool.wait_ge(s_sel, k + 1)
                ins = pool.affine_select(out=self32[:, :, :], in_=self32[:, :, :], compare_op=ALU.not_equal,
                                         fill=v, base=-k, pattern=[[-2, WT], [0, 128]], channel_multiplier=1)
                ins.then_inc(s_wide if k else s_sel, 1 + k)
            pool.wait_ge(s_rowd, 32)
            def step(s, b):
                if live(s):
                    pool.wait_ge(s_xT, s + 1)
                    pool.tensor_copy(keep[:, bass.ds(s, 1), 0:2 * P],
                                     xT[:, b, :, :].rearrange("p k n -> p (k n)").unsqueeze(1)).then_inc(s_kept, 1)
            pipeline(pool, step, TT, 0, TT - 1, 0)

        @block.scalar
        def _(act):
            act.wait_ge(s_dv, 1)
            for t in (tab_ad, tab_bc):
                act.dma_start(t[N:N + 75, :], zero[0:75, 0:2 * D]).then_inc(s_zst, 16)
                act.dma_start(t[N + 75:TROWS, :], zero[0:75, 0:2 * D]).then_inc(s_zst, 16)

            def step(s, b):
                t = s + 3
                if live(t):
                    act.wait_ge(s_stats, 2 * t + 2)
                    if again(t):
                        act.wait_ge(s_norm, t - 1)
                    nc.scalar.activation(rstd[0:P, 1 - b:2 - b], mv[0:P, 1 - b, 1:2], ACT.Sqrt, bias=eps[0:P, :]
                                         ).then_inc(s_std0, 1)
                if live(s):
                    act.wait_ge(s_mad, s + 1)
                    if again(s):
                        act.wait_ge(s_stad[b], 16 * (s - b))
                    nc.scalar.copy(ad[0:P, b, :], p_ad[0:P, b, :]).then_inc(s_adc, 1)
                t = s + 2
                if live(t):
                    act.wait_ge(s_T, t + 1)
                    if again(t):
                        act.wait_ge(s_mbc, t - 1)
                        act.wait_ge(s_kept, t - 1)
                    nc.scalar.copy(xT[:, b, :, :].rearrange("p k n -> p (k n)"), p_T[:, 0:2 * P]).then_inc(s_xT, 1)
            pipeline(act, step, TT, -3, TT - 1, 0)
            act.wait_ge(s_zst, 16 * 4)

        @block.vector
        def _(dve):
            nc.vector.memset(zero[:, :], 0.0).then_inc(s_dv, 1)
            nc.vector.memset(eps[:, :], EPS).then_inc(s_dv, 1)

            def split_rows(g):
                s = g % 2
                if g >= 2:
                    dve.wait_ge(s_rawT, g - 1)
                nc.vector.tensor_copy(rawf[:, s, :, :], raw[:, g, :, :]).then_inc(s_rawf, 1)
                if g >= 2:
                    dve.wait_ge(s_rowb, g - 1)
                nc.vector.tensor_single_scalar(rowi[:, s, 0, :], raw[:, g, 0, :], 7, ALU.logical_shift_right
                                               ).then_inc(s_prep, 1)
                nc.vector.tensor_single_scalar(rowi[:, s, 1, :], raw[:, g, 0, :], 127, ALU.bitwise_and
                                               ).then_inc(s_prep, 1)
                dve.wait_ge(s_prep, 2 * g + 2)
                nc.vector.tensor_copy(rowb[:, g, :, :], rowi[:, s, :, :]).then_inc(s_rowb, 1)

            def columns(g):
                wd = min(128, NT - g * 128)
                dve.wait_ge(s_rawT, g + 1)
                nc.vector.tensor_copy(ids[:, g * 128:g * 128 + wd, :].rearrange("p t k -> p k t"),
                                      p_ad[:, g % 2, 0:256].rearrange("p (k t) -> p k t", k=2)[:, :, 0:wd]
                                      ).then_inc(s_ids, 1)
            nc.vector.memset(raw[:, RG - 1, :, :], NJ).then_inc(s_rawm, 1)
            dve.wait_ge(s_raw, 16 * 6)
            for g in range(RG):
                split_rows(g)
                if g:
                    columns(g - 1)
            columns(RG - 1)
            dve.wait_ge(s_const, 3)
            nc.vector.memset(row0[:, :], 0.0).then_inc(s_cst, 1)
            dve.wait_ge(s_cst, 1)
            nc.vector.memset(row0[0:1, :], 1.0).then_inc(s_cst, 1)
            for c in range(2 * U):
                nc.vector.memset(copy_row[:, c:c + 1], float((U if c % 2 else c // 2) * AROWS)).then_inc(s_cst, 1)
            dve.wait_ge(s_cst, 2 + 2 * U)
            dve.wait_ge(s_ids, RG)
            done = 2 * RG
            link = chain(dve, s_prep, done)
            link(nc.vector.tensor_scalar(junk[:, :], copy_row[:, :], pcol[:, :], float(N + 22), ALU.add, ALU.add))
            link(nc.vector.tensor_scalar(part[:, 0:1], pcol[:, :], float(W), -1.0, ALU.is_ge, ALU.mult))
            link(nc.vector.tensor_scalar(part[:, 1:2], pcol[:, :], float(2 * W), -1.0, ALU.is_ge, ALU.mult))
            dve.wait_ge(s_base, 1)
            link(nc.vector.tensor_copy(base_f[:, :], p_bc[:, 0, 0:NW]))
            link(nc.vector.tensor_copy(base_i[:, :], base_f[:, :]))
            link(nc.vector.tensor_tensor(rel[:, :, :], ids[:, :, 1].rearrange("p (w t) -> p w t", t=WT),
                                 base_f[:, :].unsqueeze(2).to_broadcast([128, NW, WT]), ALU.subtract))
            flat = rel[:, :, :].rearrange("p w t -> p (w t)")
            link(nc.vector.tensor_reduce(worst[:, 0:1], flat, AXX, ALU.max))
            link(nc.vector.tensor_reduce(worst[:, 1:2], flat, AXX, ALU.min))
            link(nc.vector.tensor_scalar_add(worst[:, 0:1], worst[:, 0:1], float(1 - W)))
            link(nc.vector.scalar_tensor_tensor(worst[:, 0:1], worst[:, 1:2], -1.0, worst[:, 0:1], ALU.mult, ALU.max))
            link(nc.vector.tensor_tensor(delta[:, 1:NW], base_f[:, 1:NW], base_f[:, 0:NW - 1], ALU.subtract))
            link(nc.vector.tensor_reduce(worst[:, 1:2], delta[:, 1:NW], AXX, ALU.min))
            link(nc.vector.scalar_tensor_tensor(worst[:, 0:1], worst[:, 1:2], -1.0, worst[:, 0:1], ALU.mult, ALU.max))
            dve.sem_inc(s_worst)
            dve.wait_ge(s_worst, 2)
            link(nc.vector.tensor_reduce(narrow_f[:, :], p_bc[0:1, 0, 256:384], AXX, ALU.max))
            link(nc.vector.tensor_scalar(narrow_i[:, :], narrow_f[:, :], 0.0, None, ALU.is_le))
            dve.wait_ge(s_wide, 4)
            nc.vector.tensor_copy(iota3[:, :], iota_i[:, :, :].rearrange("p c w -> p (c w)")).then_inc(s_cst, 1)
            nc.vector.tensor_copy(sel[:, :, :], self32[:, :, :]).then_inc(s_cst, 1)
            nc.vector.tensor_copy(diff[:, :], diff_i[:, :]).then_inc(s_cst, 1)
            dve.wait_ge(s_cst, 5 + 2 * U)

            dve.wait_ge(s_x, 32)
            dve.wait_ge(s_w2, 16 * 4)
            nc.vector.tensor_tensor(bias4[:, 0, :], bias4[:, 0, :], bias4[:, 1, :], ALU.add).then_inc(s_rstd0, 1)
            dve.wait_ge(s_rstd0, 1)

            def step(s, b):
                t = s + 2
                if live(t):
                    dve.wait_ge(s_std0, t + 1)
                    nc.vector.reciprocal(rstd[0:P, b:b + 1], rstd[0:P, b:b + 1]).then_inc(s_rstd0, 1)
                    dve.wait_ge(s_rstd0, t + 2)
                    if again(t):
                        dve.wait_ge(s_T, t - 1)
                    nc.vector.tensor_scalar(xn[0:P, b:b + 1, :], x_sb[0:P, bass.ds(t, 1), :],
                                            mv[0:P, b, 0:1], rstd[0:P, b:b + 1],
                                            ALU.subtract, ALU.mult).then_inc(s_norm, 1)
                t = s + 3
                if live(t):
                    nc.vector.bn_stats(stats[0:P, 1 - b:2 - b, :], x_sb[0:P, bass.ds(t, 1), :]).then_inc(s_stats, 1)
                    dve.wait_ge(s_stats, 2 * t + 1)
                    if again(t):
                        dve.wait_ge(s_norm, t - 1)
                    dve.sem_inc(s_turn)
                    nc.vector.bn_aggr(mv[0:P, 1 - b, :], stats[0:P, 1 - b, :]).then_inc(s_stats, 1)
                if live(s):
                    dve.wait_ge(s_mbc, s + 1)
                    if again(s):
                        dve.wait_ge(s_stbc[b], 16 * (s - b))
                    nc.vector.tensor_tensor(bc[0:P, b, :], p_bc[0:P, b, :], bias4[0:P, 0, :], ALU.add).then_inc(s_bcc, 1)
            pipeline(dve, step, TT, -3, TT - 1, 0)

        @block.tensor
        def _(pe):
            pe.wait_ge(s_const, 3)
            for g in range(RG):
                pe.wait_ge(s_rawf, g + 1)
                if g >= 2:
                    pe.wait_ge(s_ids, g - 1)
                for k in range(2):
                    last = nc.tensor.transpose(p_ad[:, g % 2, k * 128:(k + 1) * 128], rawf[:, g % 2, k, :], ident[:, :])
                last.then_inc(s_rawT, 1)
            pe.wait_ge(s_ids, RG)
            pe.wait_ge(s_cst, 2)
            nc.tensor.matmul(p_bc[:, 0, 0:NW], row0[:, :], ids[:, ::WT, 1], start=True, stop=True
                             ).then_inc(s_base, 1)
            pe.wait_ge(s_worst, 1)
            nc.tensor.transpose(p_bc[0:1, 0, 256:384], worst[:, 0:1], ident[:, :]).then_inc(s_worst, 1)
            pe.wait_ge(s_prep, 2 * RG + 14)
            pe.wait_ge(s_w, 16 * 4)
            def step(s, b):
                if live(s):
                    pe.wait_ge(s_xT, s + 1)
                    for pt, c, done, free in ((p_ad, 0, s_mad, s_adc), (p_bc, 2, s_mbc, s_bcc)):
                        if again(s):
                            pe.wait_ge(free, s - 1)
                        for k in range(2):
                            last = nc.tensor.matmul(pt[0:P, b, :], xT[:, b, k, :], w[:, k, c * D:(c + 2) * D],
                                                    start=(k == 0), stop=(k == 1))
                        last.then_inc(done, 1)
                t = s + 2
                if live(t):
                    pe.wait_ge(s_norm, t + 1)
                    if again(t, 1):
                        pe.wait_ge(s_xT, t)
                    for k in range(2):
                        last = nc.tensor.transpose(p_T[:, k * P:(k + 1) * P], xn[0:P, b, k * 128:(k + 1) * 128],
                                                   ident[0:P, 0:P])
                    last.then_inc(s_T, 1)
            pipeline(pe, step, TT, -2, TT - 1, 0)


def edges(nc, a, sem, sb, ps, tab_ad, tab_bc, acc, buf, ident, upper, pcol, x_sb,
          keep, ix):
    with ExitStack() as st:
        ids, rel, base_i = ix.ids, ix.rel, ix.base_i
        copy_row, junk, narrow_i, iota3 = ix.copy_row, ix.junk, ix.narrow_i, ix.iota3
        part, sel, delta, diff = ix.part, ix.sel, ix.delta, ix.diff
        small = sb(st, "small", [128, 4, 2, 2 * U])
        gidx = sb(st, "gidx", [128, 2, 2 * U], I32)
        sidx = sb(st, "sidx", [128, 2, 2 * U], I32)
        g_ad = sb(st, "g_ad", [128, 2, U, 2 * D])
        later = sb(st, "later", [128, U, 128], BF16)

        s_nil = sem("e_nil")
        s_buf = sem("e_buf")
        s_idx = sem("e_idx")
        s_turn = sem("e_turn")
        s_turn_pe = sem("e_turn_pe")
        s_row = sem("e_row")
        s_same = sem("e_same")
        s_small = sem("e_small")
        s_sidx = sem("e_sidx")
        s_gad = [sem(f"e_gad{b}") for b in range(2)]
        s_gbc = [sem(f"e_gbc{b}") for b in range(2)]
        s_add = sem("e_add")
        s_relu = sem("e_relu")
        s_sum = sem("e_sum")
        s_res = sem("e_res")
        s_scat = [sem(f"e_scat{b}") for b in range(2)]
        s_dst = sem("e_dst")
        s_srow = sem("e_srow")
        s_win = sem("e_win")
        s_h = sem("e_h")
        s_t1 = sem("e_t1")
        s_m1 = sem("e_m1")
        s_wout = sem("e_wout")
        s_hot = sem("e_hot")
        s_T = sem("e_T")
        s_hotT = sem("e_hotT")
        s_exp = sem("e_exp")
        s_dd = sem("e_dd")
        s_wev = sem("e_wev")
        s_shift = sem("e_shift")
        s_rank = sem("e_rank")
        s_pre = sem("e_pre")
        s_kc0 = sem("k_const")
        s_kw = sem("k_w")
        s_kw2 = sem("k_w2")
        s_xcp = sem("k_xc")
        s_kp = sem("k_prod")
        s_kc = sem("k_chain")
        s_ksq = sem("k_sq")
        s_kstd = sem("k_std")
        s_ks = sem("k_sum")
        s_free = sem("k_free")
        s_kT = sem("k_T")
        s_fold = sem("k_fold")

        with ExitStack() as s2:
            same = sb(s2, "same", [128, 4, U, 128])
            hot = sb(s2, "edge_hot", [128, 4, U, 3 * W])
            hotT = sb(s2, "hotT", [3 * W, U, 128], BF16)
            win = sb(s2, "win", [3 * W, 2 * D])
            hi = sb(s2, "hi", [3 * W, 2 * D], BF16)
            t1 = sb(s2, "rest1", [3 * W, 2 * D])
            m1 = sb(s2, "rest1b", [3 * W, 2 * D], BF16)
            winb = sb(s2, "winb", [3 * W, 2 * D], BF16)
            srow = sb(s2, "srow_sb", [2 * WT, 128], BF16)
            res = sb(s2, "res", [128, 2, 2, 2 * D])
            msg = sb(s2, "msg", [128, 2, U, 2 * D])
            wres = sb(s2, "wres", [W, D])
            shift = sb(s2, "shift", [W, W])
            p_x = ps(s2, "p_x", [128, U, 128])
            p_bc = ps(s2, "p_bc2", [128, U, 512])
            p_res = ps(s2, "p_res", [128, 512])
            p_kv = ps(s2, "p_kv", [128, 512])
            wkv = sb(s2, "wkv", [128, 2, 2 * D])
            lng = sb(s2, "lng", [128, 2, HD])
            lnb = sb(s2, "lnb", [128, 2, HD])
            xc = sb(s2, "edge_xc", [128, 2, P])
            cen = sb(s2, "cen", [128, 2 * D])
            sq = sb(s2, "sq", [128, 2 * D])
            kvg = sb(s2, "kvg", [128, 2 * D])
            hs = sb(s2, "hs", [128, 3, 8])
            kacc = sb(s2, "kacc", [128, D])
            kvT = sb(s2, "kvT", [128, 2, 128])
            eps = sb(s2, "eps3", [128, 1])
            p_win = ps(s2, "p_win", [128, 512])
            nil = sb(s2, "nil", [2 * BR, D // 2])
            idf = sb(s2, "idf", [128, 2 * U])
            sG = same[:, 0:2, :, :].rearrange("p b u e -> p (b u) e")
            gres = res[:, :, :, :].rearrange("p b r n -> p (b r) n")
            g_bc = g_ad[:, 1, :, :]
            twins = msg[:, 0, 0:2, :].rearrange("p u (c e) -> p (u c) e", e=128)
            PER = 16 * U
            LAST = NQ // 2

            block = s2.enter_context(nc.Block())

            def past(q, n):
                return not isinstance(q, int) or q >= n

            def ok(q, n=NQ):
                return not isinstance(q, int) or 0 <= q < n

            STAGES = (0, 1, 2, 2.5, 3)

            def pipe(eng, step, gather_kv, fold, use_kv):
                for s in range(-2, 0):
                    step(s // 2, s % 2, s % 4, None, None)
                for c in range(4):
                    step(c // 2, c % 2, c, 0, gather_kv)
                for c in range(4):
                    step(2 + c // 2, c % 2, c, 1, gather_kv)
                with eng.Fori(2, TT) as j:
                    for c in range(4):
                        step(2 * j + c // 2, c % 2, c, j, gather_kv)
                fold()
                with eng.Fori(TT, 2 * TT) as j:
                    for c in range(4):
                        step(2 * j + c // 2, c % 2, c, j, use_kv)
                for s in range(8 * TT, NQ + 2):
                    step(s // 2, s % 2, s % 4, None, None)

            def beside(eng, gather_kv, fold, use_kv):
                for j in range(2):
                    for c in STAGES:
                        gather_kv(j, c)
                with eng.Fori(2, TT) as j:
                    for c in STAGES:
                        gather_kv(j, c)
                fold()
                with eng.Fori(TT, 2 * TT) as j:
                    for c in STAGES:
                        use_kv(j, c)

            @block.sync
            def _(sp):
                def load_kv():
                    for name, c in (("wkT", 0), ("wvT", 1)):
                        sp.dma_start(wkv[:, :, c * D:(c + 1) * D], a[name].rearrange("(k p) n -> p k n", p=128)
                                     ).then_inc(s_kw, 16)
                    for k, name in enumerate(("L0_mix_ln_k", "L0_mix_ln_v")):
                        sp.dma_start(lng[:, k, :], a[name + "_g"].unsqueeze(0).to_broadcast([128, HD])).then_inc(s_kw, 16)
                        sp.dma_start(lnb[:, k, :], a[name + "_b"].unsqueeze(0).to_broadcast([128, HD])).then_inc(s_kw, 16)

                def blank(w):
                    sp.dma_start(buf[bass.ds(BR * w, BR), :].rearrange("r (h d) -> (r h) d", h=2), nil[:, :]
                                 ).then_inc(s_buf, 16)
                sp.wait_ge(s_nil, 1)
                narrow = sp.value_load(narrow_i[0:1, 0:1], min_val=0, max_val=1)
                with sp.If(narrow):
                    def load(w):
                        if past(w, 1):
                            sp.wait_ge(s_row, 2 * w)
                        sp.dma_start(srow[:, :], a["srow"][bass.ds(WT * w, WT), :, :].rearrange("t k e -> (t k) e")
                                     ).then_inc(s_srow, 16)
                        first = sp.value_load(base_i[0:1, bass.ds(w, 1)], min_val=0, max_val=NJ)
                        if past(w, 1):
                            sp.wait_ge(s_t1, w)
                            sp.wait_ge(s_h, w)
                        for c in range(3):
                            sp.dma_start(win[c * W:(c + 1) * W, :], tab_bc[bass.ds(first, W), :]).then_inc(s_win, 16)

                    def store(w):
                        first = sp.value_load(base_i[0:1, bass.ds(w, 1)], min_val=0, max_val=NJ)
                        sp.wait_ge(s_wev, w + 1)
                        sp.dma_start(acc[bass.ds(U * AROWS + first, W), :], wres[:, :]).then_inc(s_dst, 16)
                    load(0)
                    load_kv()
                    load(1)
                    with sp.Fori(2, NW) as w:
                        load(w)
                        blank(w)
                        store(w - 2)
                    blank(0)
                    blank(1)
                    store(NW - 2)
                    store(NW - 1)
                    sp.wait_ge(s_dst, 16 * NW)
                with sp.Else():
                    load_kv()
                    with sp.Fori(0, NW) as w:
                        blank(w)
                sp.wait_ge(s_buf, 16 * NW)

            @block.gpsimd
            def _(pool):
                def gather(q, b):
                    pool.wait_ge(s_idx, q + 1)
                    if past(q, 2):
                        pool.wait_ge(s_add, 2 * q - 2)
                    pool.sem_inc(s_turn)
                    for u in range(U):
                        pool.indirect_dma_start(g_ad[:, b, u, :], None, tab_ad,
                                                bass.IndirectOffsetOnAxis(gidx[:, b, u:u + 1], 0)
                                                ).then_inc(s_gad[b], 16)

                def scatter(q, b, w):
                    pool.wait_ge(s_sidx, q + 1)
                    pool.wait_ge(s_res, 2 * q + 2)
                    if past(q, 1):
                        pool.wait_ge(s_scat[1 - b], PER * (w + b))
                    pool.sem_inc(s_turn)
                    for u in range(U):
                        pool.indirect_dma_start(acc, bass.IndirectOffsetOnAxis(sidx[:, b, u:u + 1], 0),
                                                res[:, b, u // 2, (u % 2) * D:(u % 2 + 1) * D], None,
                                                compute_op=ALU.add).then_inc(s_scat[b], 16)

                def nothing(*_):
                    pass

                def step(i, b, c, j, piece):
                    s = 2 * i + b
                    if ok(s):
                        gather(s, b)
                    if ok(s - 2):
                        scatter(s - 2, b, i - 1)
                narrow = pool.value_load(narrow_i[0:1, 0:1], min_val=0, max_val=1)
                with pool.If(narrow):
                    pipe(pool, step, nothing, nothing, nothing)
                    for b in range(2):
                        pool.wait_ge(s_scat[b], PER * (NQ // 2))
                with pool.Else():
                    def tiles(q, first):
                        pool.wait_ge(s_idx, q + 1)
                        pool.sem_inc(s_turn)
                        for u in range(U):
                            pool.indirect_dma_start(g_ad[:, 0, u, :], None, tab_ad,
                                                    bass.IndirectOffsetOnAxis(gidx[:, 0, 2 * u:2 * u + 1], 0)
                                                    ).then_inc(s_gad[0], 16)
                            pool.indirect_dma_start(g_bc[:, u, :], None, tab_bc,
                                                    bass.IndirectOffsetOnAxis(gidx[:, 0, 2 * u + 1:2 * u + 2], 0)
                                                    ).then_inc(s_gbc[0], 16)
                        pool.wait_ge(s_sidx, q + 1)
                        pool.wait_ge(s_res, U * (q + 1))
                        pool.sem_inc(s_turn)
                        for u in range(U):
                            pool.indirect_dma_start(acc, bass.IndirectOffsetOnAxis(sidx[:, 0, 2 * u:2 * u + 1], 0),
                                                    gres[:, u, 0:D], None, compute_op=ALU.add
                                                    ).then_inc(s_scat[0], 16)
                            if u or not first:
                                pool.wait_ge(s_dst, 16 * U * q + 16 * u)
                                pool.sem_inc(s_turn)
                            pool.indirect_dma_start(acc, bass.IndirectOffsetOnAxis(sidx[:, 0, 2 * u + 1:2 * u + 2], 0),
                                                    gres[:, u, D:2 * D], None, compute_op=ALU.add
                                                    ).then_inc(s_dst, 16)
                    tiles(0, True)
                    with pool.Fori(1, NQ) as q:
                        tiles(q, False)
                    pool.wait_ge(s_scat[0], PER * NQ)
                    pool.wait_ge(s_dst, PER * NQ)

            @block.vector
            def _(dve):
                V = nc.vector
                V.memset(nil[:, :], 0.0).then_inc(s_nil, 1)
                V.memset(eps[:, :], EPS).then_inc(s_kc0, 1)
                V.memset(kacc[:, :], 0.0).then_inc(s_kc0, 1)
                V.memset(kvT[:, :, :], 0.0).then_inc(s_kc0, 1)
                dve.wait_ge(s_kc0, 3)

                def indices(q, b, c):
                    src = ids[:, bass.ds(U * q, U), 0]
                    if past(q, 4):
                        dve.wait_ge(s_sidx, q - 3)
                    V.tensor_scalar(small[:, c, 0, U:2 * U], src, -1.0, junk[:, 0:1], ALU.mult, ALU.add
                                    ).then_inc(s_pre, 1)
                    V.tensor_tensor(small[:, c, 1, U:2 * U], src, copy_row[:, ::2], ALU.add).then_inc(s_pre, 1)
                    V.tensor_copy(gidx[:, b, 0:U], ids[:, bass.ds(U * q, U), 0]).then_inc(s_idx, 1)

                def onehot(q, c):
                    if past(q, 4):
                        dve.wait_ge(s_sum, q - 3)
                        dve.wait_ge(s_dd, 2 * q - 6)
                    r = rel[:, :, :].rearrange("p w t -> p (w t)")[:, bass.ds(U * q, U)]
                    V.tensor_tensor(hot[:, c, :, :], iota3[:, :].unsqueeze(1).to_broadcast([128, U, 3 * W]),
                                    r.unsqueeze(2).to_broadcast([128, U, 3 * W]), ALU.is_equal).then_inc(s_hot, 1)

                def duplicates(q, c):
                    dve.wait_ge(s_row, q + 1)
                    V.tensor_tensor(same[:, c, :, :], p_x[:, :, :],
                                    ids[:, bass.ds(U * q, U), 0].unsqueeze(2).to_broadcast([128, U, 128]),
                                    ALU.is_equal).then_inc(s_same, 1)

                def ranks(q, c):
                    dve.wait_ge(s_same, q + 1)
                    if past(q, 1):
                        dve.wait_ge(s_rank, 3 * q)
                    V.tensor_tensor(later[:, :, :], same[:, c, :, :],
                                    upper[:, :].unsqueeze(1).to_broadcast([128, U, 128]), ALU.mult
                                    ).then_inc(s_rank, 1)
                    dve.wait_ge(s_rank, 3 * q + 1)
                    V.tensor_reduce(small[:, c, 0, 0:U], later[:, :, :], AXX, ALU.add).then_inc(s_rank, 1)
                    if past(q, 4):
                        dve.wait_ge(s_sidx, q - 3)
                    dve.wait_ge(s_rank, 3 * q + 2)
                    dve.wait_ge(s_pre, 2 * q + 1)
                    V.scalar_tensor_tensor(small[:, c, 1, 0:U], small[:, c, 0, 0:U], 0.0,
                                           small[:, c, 0, U:2 * U], ALU.is_gt, ALU.mult).then_inc(s_rank, 1)

                def targets(q, b, c, w):
                    dve.wait_ge(s_rank, 3 * q + 3)
                    if past(q, 2):
                        dve.wait_ge(s_scat[b], PER * w)
                    dve.wait_ge(s_pre, 2 * q + 2)
                    V.tensor_tensor(sidx[:, b, 0:U], small[:, c, 1, 0:U], small[:, c, 1, U:2 * U], ALU.add
                                    ).then_inc(s_sidx, 1)

                def add(q, b, w):
                    dve.wait_ge(s_gad[b], PER * (w + 1))
                    dve.wait_ge(s_exp, q + 1)
                    if past(q, 2):
                        dve.wait_ge(s_sum, q - 1)
                        dve.wait_ge(s_dd, 2 * q - 2)
                    for r in range(2):
                        u = slice(2 * r, 2 * r + 2)
                        V.tensor_tensor(msg[:, b, u, :], g_ad[:, b, u, :], p_bc[:, u, :], ALU.add).then_inc(s_add, 1)

                def rest(w):
                    dve.wait_ge(s_win, 48 * (w + 1))
                    dve.wait_ge(s_h, w + 1)
                    if past(w, 1):
                        dve.wait_ge(s_m1, w)
                        dve.wait_ge(s_wout, w)
                    V.scalar_tensor_tensor(t1[:, :], hi[:, :], part[0:3 * W, 0:1], win[:, :], ALU.mult, ALU.add
                                           ).then_inc(s_t1, 1)

                def thirds(w):
                    dve.wait_ge(s_m1, w + 1)
                    dve.wait_ge(s_t1, w + 1)
                    if past(w, 1):
                        dve.wait_ge(s_exp, 2 * w)
                    V.scalar_tensor_tensor(winb[:, :], m1[:, :], part[0:3 * W, 1:2], t1[:, :], ALU.mult, ALU.add
                                           ).then_inc(s_wout, 1)

                def carry(w):
                    if past(w, 2):
                        dve.wait_ge(s_sum, 2 * w - 1)
                    V.tensor_scalar(shift[:, :], diff[0:W, :], delta[0:W, bass.ds(w, 1)], None, ALU.is_equal
                                    ).then_inc(s_shift, 1)

                link = chain_at(dve, s_kc)

                def gather_kv(t, c):
                    kv8 = p_kv[0:P, :].rearrange("p (g d) -> p g d", d=HD)
                    cen8 = cen[0:P, :].rearrange("p (g d) -> p g d", d=HD)
                    kv4 = kvg[0:P, :].rearrange("p (w h d) -> p w h d", w=2, h=H)

                    def wide(v):
                        return v.unsqueeze(2).to_broadcast([P, 8, HD])
                    if c == 1:
                        dve.wait_ge(s_kp, t + 1)
                        link(8 * t + 1, V.tensor_reduce(hs[0:P, 0, :], kv8, AXX, ALU.add))
                        link(8 * t + 2, V.tensor_scalar_mul(hs[0:P, 0, :], hs[0:P, 0, :], 1.0 / HD))
                        V.tensor_tensor(cen8, kv8, wide(hs[0:P, 0, :]), ALU.subtract).then_inc(s_kc, 1)
                    if c == 2:
                        dve.wait_ge(s_ksq, t + 1)
                        link(8 * t + 4, V.tensor_reduce(hs[0:P, 1, :], sq[0:P, :].rearrange("p (g d) -> p g d", d=HD),
                                                        AXX, ALU.add))
                    if c == 2.5:
                        dve.wait_ge(s_kstd, t + 1)
                        link(8 * t + 5, V.reciprocal(hs[0:P, 2, :], hs[0:P, 2, :]))
                        link(8 * t + 6, V.tensor_tensor(kvg[0:P, :].rearrange("p (g d) -> p g d", d=HD), cen8,
                                                        wide(hs[0:P, 2, :]), ALU.mult))
                    if c == 3:
                        if not past(t, 1):
                            dve.wait_ge(s_kw, 16 * 6)
                        link(8 * t + 7, V.tensor_tensor(kv4, kv4, lng[0:P, :, :].unsqueeze(2).to_broadcast([P, 2, H, HD]),
                                                        ALU.mult))
                        V.tensor_tensor(kv4, kv4, lnb[0:P, :, :].unsqueeze(2).to_broadcast([P, 2, H, HD]),
                                        ALU.add).then_inc(s_kc, 1)
                    if c == 0 and past(t, 1):
                        dve.wait_ge(s_ks, t)
                        if past(t, 2):
                            dve.wait_ge(s_free, t - 1)
                        V.tensor_tensor(kacc[:, :], kacc[:, :], p_kv[:, 0:D], ALU.add).then_inc(s_free, 1)

                def fold():
                    gather_kv(TT, 0)
                    dve.wait_ge(s_free, TT)
                    for hp in range(2):
                        for h in range(2):
                            r = slice(h * HD, (h + 1) * HD)
                            V.tensor_scalar_mul(kvT[r, hp, r], kacc[r, hp * 128 + h * HD:hp * 128 + (h + 1) * HD],
                                                1.0 / N).then_inc(s_kT, 1)
                    dve.wait_ge(s_fold, 1)
                    V.tensor_copy(cen[:, :], p_kv[:, :]).then_inc(s_free, 1)
                    dve.wait_ge(s_fold, 2)
                    V.tensor_copy(wkv[:, :, D:2 * D], p_kv[:, :].rearrange("p (k n) -> p k n", k=2)).then_inc(s_free, 1)

                def use_kv(j, c):
                    if c == 1:
                        t = j - TT
                        dve.wait_ge(s_kp, j + 1)
                        V.tensor_scalar_mul(keep[0:P, bass.ds(t, 1), :], p_kv[0:P, 0:D].unsqueeze(1), 1.0
                                            ).then_inc(s_free, 1)
                        V.tensor_tensor(x_sb[0:P, bass.ds(t, 1), :], x_sb[0:P, bass.ds(t, 1), :],
                                        p_kv[0:P, D:2 * D].unsqueeze(1), ALU.add).then_inc(s_free, 1)

                def step(i, b, c, j, piece):
                    s = 2 * i + b
                    if ok(s + 1):
                        onehot(s + 1, (c + 1) % 4)
                        duplicates(s + 1, (c + 1) % 4)
                    if piece:
                        piece(j, c)
                    if ok(s):
                        add(s, b, i)
                    if ok(s + 2):
                        indices(s + 2, b, (c + 2) % 4)
                    if b == 1 and ok(i + 1, NW):
                        thirds(i + 1)
                    if b == 0 and past(i, 1) and ok(i, NW):
                        carry(i)
                    if ok(s + 1):
                        ranks(s + 1, (c + 1) % 4)
                    if ok(s - 1):
                        targets(s - 1, 1 - b, (c - 1) % 4, i - 1 + b)
                    if b == 0 and ok(i + 1, NW):
                        rest(i + 1)
                    if piece and c == 2:
                        piece(j, 2.5)
                narrow = dve.value_load(narrow_i[0:1, 0:1], min_val=0, max_val=1)
                with dve.If(narrow):
                    pipe(dve, step, gather_kv, fold, use_kv)
                with dve.Else():
                    beside(dve, gather_kv, fold, use_kv)

                    def group(q, first):
                        def wide(v):
                            return v.unsqueeze(2).to_broadcast([128, 2 * U, 128])
                        src = ids[:, bass.ds(U * q, U), :].rearrange("p t k -> p (t k)")
                        if not first:
                            dve.wait_ge(s_scat[0], PER * q)
                            dve.wait_ge(s_dst, PER * q)
                        V.tensor_copy(idf[:, :], src).then_inc(s_small, 1)
                        V.tensor_copy(gidx[:, 0, :], src).then_inc(s_idx, 1)
                        dve.wait_ge(s_small, 6 * q + 1)
                        for half in range(2):
                            dve.wait_ge(s_row, 2 * q + half + 1)
                            V.tensor_tensor(sG[:, half * U:(half + 1) * U, :], p_x[:, :, :],
                                            idf[:, half * U:(half + 1) * U].unsqueeze(2).to_broadcast([128, U, 128]),
                                            ALU.is_equal).then_inc(s_same, 1)
                        dve.wait_ge(s_same, 2 * q + 2)
                        link = chain(dve, s_small, 6 * q + 1)
                        link(V.tensor_tensor(twins, sG[:, :, :],
                                             upper[:, :].unsqueeze(1).to_broadcast([128, 2 * U, 128]), ALU.mult))
                        link(V.tensor_reduce(small[:, 0, 0, :], twins, AXX, ALU.add))
                        link(V.tensor_tensor(idf[:, :], idf[:, :], copy_row[:, :], ALU.add))
                        link(V.tensor_tensor(small[:, 0, 1, :], junk[:, :], idf[:, :], ALU.subtract))
                        link(V.scalar_tensor_tensor(small[:, 0, 1, :], small[:, 0, 0, :], 0.0, small[:, 0, 1, :],
                                                    ALU.is_gt, ALU.mult))
                        V.tensor_tensor(sidx[:, 0, :], small[:, 0, 1, :], idf[:, :], ALU.add).then_inc(s_sidx, 1)
                        dve.wait_ge(s_sidx, q + 1)
                        dve.wait_ge(s_gad[0], PER * (q + 1))
                        dve.wait_ge(s_gbc[0], PER * (q + 1))
                        V.tensor_tensor(g_ad[:, 0, :, :], g_ad[:, 0, :, :], g_bc[:, :, :], ALU.add).then_inc(s_add, 1)
                    group(0, True)
                    with dve.Fori(1, NQ) as q:
                        group(q, False)

            @block.scalar
            def _(act):
                S = nc.scalar
                act.wait_ge(s_kc0, 3)

                def results(q, r, b, w):
                    if r == 0 and past(q, 2):
                        act.wait_ge(s_scat[b], PER * w)
                    act.wait_ge(s_dd, 2 * q + r + 1)
                    S.copy(res[:, b, r, :], p_res[:, :]).then_inc(s_res, 1)

                def relu(q, b):
                    for r in range(2):
                        u = slice(2 * r, 2 * r + 2)
                        act.wait_ge(s_add, 2 * q + r + 1)
                        S.activation(msg[:, b, u, :], msg[:, b, u, :], ACT.Relu).then_inc(s_relu, 1)

                def window_sums(w):
                    act.wait_ge(s_sum, 2 * w + 2)
                    if past(w, 1):
                        act.wait_ge(s_dst, 16 * w)
                    S.copy(wres[:, :], p_win[0:W, 0:D]).then_inc(s_wev, 1)

                def transposed(q):
                    act.wait_ge(s_T, q + 1)
                    S.copy(hotT[:, :, :], p_x[0:3 * W, :, :]).then_inc(s_hotT, 1)

                def high(w):
                    act.wait_ge(s_win, 48 * (w + 1))
                    if past(w, 1):
                        act.wait_ge(s_t1, w)
                    S.copy(hi[:, :], win[:, :]).then_inc(s_h, 1)

                def middle(w):
                    act.wait_ge(s_t1, w + 1)
                    if past(w, 1):
                        act.wait_ge(s_wout, w)
                    S.copy(m1[:, :], t1[:, :]).then_inc(s_m1, 1)

                def copy_xn(j, t):
                    if past(j, 1):
                        act.wait_ge(s_kp, j)
                    S.copy(xc[:, :, :].rearrange("p k n -> p (k n)").unsqueeze(1), keep[:, bass.ds(t, 1), 0:2 * P]
                           ).then_inc(s_xcp, 1)

                def gather_kv(t, c):
                    if c == 0:
                        copy_xn(t, t)
                    if c == 1:
                        act.wait_ge(s_kc, 8 * t + 3)
                        S.activation(sq[0:P, :], cen[0:P, :], ACT.Square).then_inc(s_ksq, 1)
                    if c == 2:
                        act.wait_ge(s_kc, 8 * t + 4)
                        S.activation(hs[0:P, 2, :], hs[0:P, 1, :], ACT.Sqrt, bias=eps[0:P, :],
                                     scale=1.0 / HD).then_inc(s_kstd, 1)

                def fold():
                    act.wait_ge(s_free, TT)
                    act.dma_start(kvg[:, :].rearrange("p (k n) -> p k n", k=2),
                                  a["L0_mix_wq"].rearrange("(k p) n -> p k n", p=128)).then_inc(s_kw2, 16)
                    act.dma_start(sq[:, :].rearrange("p (k n) -> p k n", k=2),
                                  a["woT"].rearrange("(k p) n -> p k n", p=128)).then_inc(s_kw2, 16)
                    act.dma_start(wkv[:, :, 0:D], a["L0_gnn_Wr"].rearrange("(k p) n -> p k n", p=128)
                                  ).then_inc(s_kw2, 16)

                def use_kv(j, c):
                    if c == 0:
                        copy_xn(j, j - TT)

                def step(i, b, c, j, piece):
                    s = 2 * i + b
                    if piece and c == 0:
                        piece(j, c)
                    if b == 1 and ok(i + 1, NW):
                        middle(i + 1)
                    if b == 1 and ok(i - 1, NW):
                        window_sums(i - 1)
                    if ok(s - 1):
                        results(s - 1, 0, 1 - b, i - 1 + b)
                    if ok(s + 1):
                        transposed(s + 1)
                    if ok(s - 1):
                        results(s - 1, 1, 1 - b, i - 1 + b)
                    if ok(s):
                        relu(s, b)
                    if b == 0 and ok(i + 1, NW):
                        high(i + 1)
                    if piece and c:
                        piece(j, c)
                narrow = act.value_load(narrow_i[0:1, 0:1], min_val=0, max_val=1)
                with act.If(narrow):
                    pipe(act, step, gather_kv, fold, use_kv)
                with act.Else():
                    beside(act, gather_kv, fold, use_kv)
                    with act.Fori(0, NQ) as q:
                        act.wait_ge(s_add, q + 1)
                        S.activation(g_ad[:, 0, :, :], g_ad[:, 0, :, :], ACT.Relu).then_inc(s_relu, 1)
                        for u in range(U):
                            act.wait_ge(s_sum, U * q + u + 1)
                            S.copy(gres[:, u, :], p_bc[:, u, :]).then_inc(s_res, 1)

            @block.tensor
            def _(pe):
                T = nc.tensor

                def rows(q, b, w):
                    pe.wait_ge(s_srow, 16 * (w + 1))
                    if past(q, 1):
                        pe.wait_ge(s_hotT, q)
                    for u in range(U):
                        last = T.matmul(p_x[:, u, :], sel[:, U * b + u, :], srow[:, :], start=True, stop=True)
                    last.then_inc(s_row, 1)

                def spread(q, b, w):
                    pe.wait_ge(s_hotT, q + 1)
                    pe.wait_ge(s_wout, w + 1)
                    if past(q, 1):
                        pe.wait_ge(s_add, 2 * q)
                    for u in range(U):
                        last = T.matmul(p_bc[:, u, :], hotT[:, u, :], winb[:, :], start=True, stop=True)
                    last.then_inc(s_exp, 1)

                def dedupe(q, b, r, c):
                    pe.wait_ge(s_relu, 2 * q + r + 1)
                    if r or past(q, 1):
                        pe.wait_ge(s_res, 2 * q + r)
                    for u in (2 * r, 2 * r + 1):
                        last = T.matmul(p_res[:, (u % 2) * D:(u % 2 + 1) * D], same[:, c, u, :],
                                        msg[:, b, u, 0:D], start=True, stop=True)
                    last.then_inc(s_dd, 1)

                def sums(q, b, c, w):
                    pe.wait_ge(s_relu, 2 * q + 2)
                    if b == 0 and past(w, 1):
                        pe.wait_ge(s_wev, w)
                        pe.wait_ge(s_shift, w)
                        pe.sem_inc(s_turn_pe)
                        T.matmul(p_win[0:W, 0:D], shift[:, :], wres[:, :], start=True, stop=False)
                    for u in range(U):
                        first = b == 0 and u == 0 and not past(w, 1)
                        last = T.matmul(p_win[0:W, 0:D], hot[:, c, u, 0:W], msg[:, b, u, D:2 * D],
                                        start=first, stop=(b == 1 and u == U - 1))
                    last.then_inc(s_sum, 1)

                def transposes(q, c):
                    pe.wait_ge(s_hot, q + 1)
                    pe.wait_ge(s_same, q + 1)
                    for u in range(U):
                        last = T.transpose(p_x[0:3 * W, u, :], hot[:, c, u, :], ident[:, :])
                    last.then_inc(s_T, 1)

                def gather_kv(t, c):
                    if c == 0:
                        if not past(t, 1):
                            pe.wait_ge(s_kw, 16 * 6)
                        pe.wait_ge(s_xcp, t + 1)
                        if past(t, 1):
                            pe.wait_ge(s_free, t)
                        for k in range(2):
                            last = T.matmul(p_kv[0:P, :], xc[:, k, :], wkv[:, k, :], start=(k == 0), stop=(k == 1))
                        last.then_inc(s_kp, 1)
                    if c == 3:
                        pe.wait_ge(s_kc, 8 * t + 8)
                        for hp in range(2):
                            last = T.matmul(p_kv[:, hp * 128:(hp + 1) * 128], kvg[0:P, D + hp * 128:D + (hp + 1) * 128],
                                            kvg[0:P, hp * 128:(hp + 1) * 128], start=True, stop=True)
                        last.then_inc(s_ks, 1)

                def fold():
                    pe.wait_ge(s_kT, 4)
                    pe.wait_ge(s_kw2, 16 * 3)
                    for hp in range(2):
                        last = T.matmul(p_kv[:, hp * D:(hp + 1) * D], kvT[:, hp, :], sq[:, hp * D:(hp + 1) * D],
                                        start=True, stop=True)
                    last.then_inc(s_fold, 1)
                    pe.wait_ge(s_free, TT + 1)
                    for m in range(2):
                        for k in range(2):
                            last = T.matmul(p_kv[:, m * D:(m + 1) * D], kvg[:, k * D + m * 128:k * D + (m + 1) * 128],
                                            cen[:, k * D:(k + 1) * D], start=(k == 0), stop=(k == 1))
                    last.then_inc(s_fold, 1)

                def use_kv(j, c):
                    if c == 0:
                        pe.wait_ge(s_xcp, j + 1)
                        pe.wait_ge(s_free, 2 * j + 2 - TT)
                        for k in range(2):
                            last = T.matmul(p_kv[0:P, :], xc[:, k, :], wkv[:, k, :], start=(k == 0), stop=(k == 1))
                        last.then_inc(s_kp, 1)

                def step(i, b, c, j, piece):
                    s = 2 * i + b
                    if ok(s + 1):
                        rows(s + 1, 1 - b, i + b)
                    if ok(s):
                        spread(s, b, i)
                    if ok(s - 1):
                        dedupe(s - 1, 1 - b, 0, (c - 1) % 4)
                    if ok(s + 1):
                        transposes(s + 1, (c + 1) % 4)
                    if ok(s - 1):
                        dedupe(s - 1, 1 - b, 1, (c - 1) % 4)
                    if ok(s - 1):
                        sums(s - 1, 1 - b, (c - 1) % 4, i - 1 + b)
                    if piece:
                        piece(j, c)
                narrow = pe.value_load(narrow_i[0:1, 0:1], min_val=0, max_val=1)
                with pe.If(narrow):
                    pipe(pe, step, gather_kv, fold, use_kv)
                with pe.Else():
                    beside(pe, gather_kv, fold, use_kv)

                    def group(q, first):
                        pe.wait_ge(s_small, 6 * q + 1)
                        for half in range(2):
                            if half or not first:
                                pe.wait_ge(s_same, 2 * q + half)
                            for c in range(U):
                                last = T.transpose(p_x[:, c, :],
                                                   idf[:, half * U + c:half * U + c + 1].to_broadcast([128, 128]),
                                                   ident[:, :])
                            last.then_inc(s_row, 1)
                        pe.wait_ge(s_same, 2 * q + 2)
                        pe.wait_ge(s_relu, q + 1)
                        for u in range(U):
                            if not first:
                                pe.wait_ge(s_res, U * (q - 1) + u + 1)
                            for k in range(2):
                                last = T.matmul(p_bc[:, u, k * D:(k + 1) * D], sG[:, 2 * u + k, :],
                                                g_ad[:, 0, u, k * D:(k + 1) * D], start=True, stop=True)
                            last.then_inc(s_sum, 1)
                    group(0, True)
                    with pe.Fori(1, NQ) as q:
                        group(q, False)


def live(t, n=TT):
    return not isinstance(t, int) or 0 <= t < n


def again(t, slots=2):
    return not isinstance(t, int) or t >= slots


def pipeline(eng, step, n, first, last, lag, slots=2):
    start = -(-(lag + slots) // slots) * slots
    stop = (n + first) // slots * slots
    for s in range(first, start):
        step(s, s % slots)
    with eng.Fori(start // slots, stop // slots) as i:
        for c in range(slots):
            step(slots * i + c, c)
    for s in range(stop, last + 1):
        step(s, s % slots)


def nodes(nc, a, sem, sb, ps, acc, ident, x_sb, keep, logits):
    with ExitStack() as st:
        wo = sb(st, "wo", [128, 4, D])
        gw = sb(st, "gw", [128, 2, NE])
        bh = sb(st, "bh", [128, 2, D])
        bm = sb(st, "bm", [128, D])
        bg = sb(st, "bg", [128, NE])
        eps = sb(st, "eps2", [128, 1])
        part = sb(st, "nparts", [128, 4, NACC, D])
        xw = sb(st, "xw", [128, 2, D])
        xb = sb(st, "xb", [128, 2, D])
        mT = sb(st, "mT", [128, 2, 4, P])
        hb = sb(st, "hb", [128, 2, D])
        x2 = sb(st, "x2", [128, 2, D])
        xn2 = sb(st, "xn2", [128, 2, D])
        stats = sb(st, "stats2", [128, 2, 6])
        mv = sb(st, "mv2", [128, 2, 2])
        std = sb(st, "std2", [128, 2])
        x2T = sb(st, "x2T", [128, 2, 2, P])
        p_mT = ps(st, "p_mT", [128, 2, 512])
        p_h = ps(st, "p_h", [128, 2, 512])
        p_xT = ps(st, "p_xT", [128, 2, 512])
        p_g = ps(st, "p_g", [128, 2, 512])

        s_w = sem("n_w")
        s_ld = [sem(f"n_ld{c}") for c in range(4)]
        s_const = sem("n_const")
        s_half = sem("n_half")
        s_turn = sem("n_turn")
        s_msg = sem("n_msg")
        s_xc = sem("n_xc")
        s_xb = sem("n_xb")
        s_mT = sem("n_mT")
        s_mTc = sem("n_mTc")
        s_h = sem("n_h")
        s_hb = sem("n_hb")
        s_ln = sem("n_ln")
        s_var = sem("n_var")
        s_std = sem("n_std")
        s_x2 = sem("n_x2")
        s_xn2 = sem("n_xn2")
        s_xT = sem("n_xT")
        s_xTc = sem("n_xTc")
        s_gate = sem("n_gate")
        s_lg = sem("n_lg")
        rows = acc.rearrange("(c r) d -> r c d", r=AROWS)[0:N, :, :].rearrange("(p t) c d -> p t c d", t=TT)

        block = st.enter_context(nc.Block())

        @block.sync
        def _(sp):
            sp.dma_start(wo[:, :, :], a["L0_gnn_Wo"].rearrange("(k p) n -> p k n", p=128)).then_inc(s_w, 16)
            sp.dma_start(gw[:, :, :], a["L0_ffn_gate_w"].rearrange("(k p) n -> p k n", p=128)).then_inc(s_w, 16)
            for dst, name, n in ((bh[:, 0, :], "L0_gnn_bo", D), (bh[:, 1, :], "L0_gnn_br", D),
                                 (bm[:, :], "L0_mix_bo", D), (bg[:, :], "L0_ffn_gate_b", NE)):
                sp.dma_start(dst, a[name].unsqueeze(0).to_broadcast([128, n])).then_inc(s_w, 16)

            def load(t, c):
                if again(t, 4):
                    sp.wait_ge(s_mT, t - 3)
                for r in SPLIT:
                    sp.dma_start(part[r, c, :, :],
                                 rows[r, bass.ds(t, 1), :, :].rearrange("p t c d -> p (t c) d")
                                 ).then_inc(s_ld[c], 16)
            pipeline(sp, load, TT, 0, TT - 1, 0, 4)

        @block.gpsimd
        def _(pool):
            pool.wait_ge(s_w, 16 * 6)
            pool.wait_ge(s_const, 2)

            def step(s, c):
                b = c % 2
                t, d = s + 2, (c + 2) % 4
                if live(t):
                    pool.wait_ge(s_ld[d], 8 * (t - d) + 32)
                    pool.tensor_tensor(part[0:P, d, 0:2, :], part[0:P, d, 0:2, :], part[0:P, d, 2:4, :],
                                       ALU.add).then_inc(s_half, 1)
                if live(s):
                    if again(s):
                        pool.wait_ge(s_hb, s - 1)
                        pool.wait_ge(s_ln, 4 * s - 7)
                    pool.tensor_tensor(xw[0:P, b:b + 1, :], keep[0:P, bass.ds(s, 1), :], bh[0:P, 0:1, :],
                                       ALU.add).then_inc(s_xc, 1)
                    pool.tensor_tensor(xb[0:P, b:b + 1, :], x_sb[0:P, bass.ds(s, 1), :], bm[0:P, :].unsqueeze(1),
                                       ALU.add).then_inc(s_xb, 1)
            pipeline(pool, step, TT, -2, TT - 1, 0, 4)

        @block.vector
        def _(dve):
            nc.vector.memset(eps[:, :], EPS).then_inc(s_const, 1)
            dve.wait_ge(s_w, 16 * 6)
            nc.vector.tensor_tensor(bh[:, 0, :], bh[:, 0, :], bh[:, 1, :], ALU.add).then_inc(s_const, 1)
            dve.wait_ge(s_const, 2)

            def message_sums(t, c):
                dve.wait_ge(s_half, t + 1)
                nc.vector.tensor_tensor(part[0:P, c, 3, :], part[0:P, c, 0, :], part[0:P, c, 1, :],
                                        ALU.add).then_inc(s_msg, 1)

            def residual(t, b):
                dve.wait_ge(s_h, t + 1)
                dve.wait_ge(s_xc, t + 1)
                nc.vector.tensor_tensor(hb[0:P, b, :], p_h[0:P, b, 0:D], xw[0:P, b, :], ALU.add).then_inc(s_hb, 1)
                dve.wait_ge(s_xb, t + 1)
                if again(t):
                    dve.wait_ge(s_x2, t - 1)
                link = chain(dve, s_ln, 4 * t)
                dve.wait_ge(s_hb, t + 1)
                link(nc.vector.scalar_tensor_tensor(x2[0:P, b, :], hb[0:P, b, :], 0.0, xb[0:P, b, :],
                                                    ALU.max, ALU.add))
                link(nc.vector.bn_stats(stats[0:P, b, :], x2[0:P, b, :]))
                dve.sem_inc(s_turn)
                nc.vector.bn_aggr(mv[0:P, b, :], stats[0:P, b, :]).then_inc(s_var, 1)
                return link

            def normalise(t, b, link):
                dve.wait_ge(s_std, t + 1)
                link(nc.vector.reciprocal(std[0:P, b:b + 1], std[0:P, b:b + 1]))
                if again(t):
                    dve.wait_ge(s_xT, t - 1)
                    dve.wait_ge(s_xn2, t - 1)
                link(nc.vector.tensor_scalar(xn2[0:P, b, :], x2[0:P, b, :], mv[0:P, b, 0:1], std[0:P, b:b + 1],
                                             ALU.subtract, ALU.mult))

            def step(s, c):
                b = c % 2
                if live(s - 1):
                    link = residual(s - 1, 1 - b)
                if live(s + 1):
                    message_sums(s + 1, (c + 1) % 4)
                if live(s - 1):
                    normalise(s - 1, 1 - b, link)
                if live(s - 3):
                    dve.wait_ge(s_gate, s - 2)
                    nc.vector.tensor_tensor(logits[0:P, bass.ds(s - 3, 1), :], p_g[0:P, 1 - b:2 - b, 0:NE],
                                            bg[0:P, :].unsqueeze(1), ALU.add).then_inc(s_lg, 1)
            pipeline(dve, step, TT, -1, TT + 2, 3, 4)

        @block.scalar
        def _(act):
            def step(s, b):
                t = s - 1
                if live(t):
                    act.wait_ge(s_var, t + 1)
                    if again(t):
                        act.wait_ge(s_ln, 4 * t - 4)
                    nc.scalar.activation(std[0:P, 1 - b:2 - b], mv[0:P, 1 - b, 1:2], ACT.Sqrt, bias=eps[0:P, :]
                                         ).then_inc(s_std, 1)
                t = s + 1
                if live(t):
                    act.wait_ge(s_mT, t + 1)
                    if again(t):
                        act.wait_ge(s_h, t - 1)
                    nc.scalar.copy(mT[:, 1 - b, :, :].rearrange("p k n -> p (k n)"), p_mT[:, 1 - b, 0:4 * P]
                                   ).then_inc(s_mTc, 1)
                t = s - 1
                if live(t):
                    act.wait_ge(s_xT, t + 1)
                    if again(t):
                        act.wait_ge(s_gate, t - 1)
                    nc.scalar.copy(x2T[:, 1 - b, :, :].rearrange("p k n -> p (k n)"), p_xT[:, 1 - b, 0:2 * P]
                                   ).then_inc(s_xTc, 1)
                    act.wait_ge(s_ln, 4 * t + 4)
                    act.wait_ge(s_xc, t + 1)
                    act.wait_ge(s_xb, t + 1)
                    nc.scalar.copy(x_sb[0:P, bass.ds(t, 1), :], x2[0:P, 1 - b:2 - b, :]).then_inc(s_x2, 1)
                    nc.scalar.copy(keep[0:P, bass.ds(t, 1), :], xn2[0:P, 1 - b:2 - b, :]).then_inc(s_xn2, 1)
            act.wait_ge(s_const, 2)
            pipeline(act, step, TT, -1, TT, 1)

        @block.tensor
        def _(pe):
            pe.wait_ge(s_w, 16 * 6)

            def step(s, c):
                b = c % 2
                if live(s):
                    pe.wait_ge(s_mTc, s + 1)
                    if again(s):
                        pe.wait_ge(s_hb, s - 1)
                    for k in range(4):
                        last = nc.tensor.matmul(p_h[0:P, b, 0:D], mT[:, b, k, :], wo[:, k, :],
                                                start=(k == 0), stop=(k == 3))
                    last.then_inc(s_h, 1)
                t = s + 1
                if live(t):
                    pe.wait_ge(s_msg, t + 1)
                    if again(t):
                        pe.wait_ge(s_mTc, t - 1)
                    for k in range(4):
                        last = nc.tensor.transpose(p_mT[:, 1 - b, k * P:(k + 1) * P],
                                                   part[0:P, (c + 1) % 4, 3 + k // 2, (k % 2) * 128:(k % 2 + 1) * 128],
                                                   ident[0:P, 0:P])
                    last.then_inc(s_mT, 1)
                t = s - 1
                if live(t):
                    pe.wait_ge(s_ln, 4 * t + 4)
                    if again(t):
                        pe.wait_ge(s_xTc, t - 1)
                    for k in range(2):
                        last = nc.tensor.transpose(p_xT[:, 1 - b, k * P:(k + 1) * P],
                                                   xn2[0:P, 1 - b, k * 128:(k + 1) * 128], ident[0:P, 0:P])
                    last.then_inc(s_xT, 1)
                t = s - 2
                if live(t):
                    pe.wait_ge(s_xTc, t + 1)
                    if again(t):
                        pe.wait_ge(s_lg, t - 1)
                    for k in range(2):
                        last = nc.tensor.matmul(p_g[0:P, b, 0:NE], x2T[:, b, k, :], gw[:, k, :],
                                                start=(k == 0), stop=(k == 1))
                    last.then_inc(s_gate, 1)
            pipeline(pe, step, TT, -1, TT + 1, 2, 4)


def route(nc, a, ex, sem, sb, ps, buf, upper, pcol, keep, logits, slot_g, gate_p):
    with ExitStack() as st:
        probs = sb(st, "probs", [128, TT, NE])
        hot = sb(st, "hot", [128, TT, NE])
        before = sb(st, "before", [128, TT, NE])
        tmp = sb(st, "tmp", [128, TT, NE])
        ones = sb(st, "ones", [128, TT])
        rank = sb(st, "rank", [128, 2, NE])
        col = sb(st, "col", [128, 5, TT])
        junk = sb(st, "junk2", [128, TT])
        offs = sb(st, "offs", [128, NE])
        dest = sb(st, "dest", [128, TT])
        dslot = sb(st, "dslot", [128, 4], I32)
        rowst = sb(st, "rowst", [128, 4, D])
        p_off = ps(st, "p_off", [128, 512])
        s_c = sem("r_chain")
        s_shift = sem("r_shift")
        s_exp = sem("r_exp")
        s_tot = sem("r_tot")
        s_off = sem("r_off")
        s_stage = sem("r_stage")
        s_slot = sem("r_slot")
        s_turn = sem("r_turn")
        s_sc = [sem(f"r_sc{c}") for c in range(4)]

        block = st.enter_context(nc.Block())

        @block.scalar
        def _(act):
            act.wait_ge(s_shift, 1)
            nc.scalar.activation(probs[0:P, :, :], tmp[0:P, :, :], ACT.Exp).then_inc(s_exp, 1)

        @block.tensor
        def _(pe):
            pe.wait_ge(s_tot, 1)
            nc.tensor.matmul(p_off[0:P, 0:NE], upper[0:P, 0:P], before[0:P, TT - 1, :], start=True, stop=True
                             ).then_inc(s_off, 1)

        @block.vector
        def _(dve):
            link = chain(dve, s_c)
            V = nc.vector
            top, total, pos, base, kept = (col[0:P, k, :] for k in range(5))
            lg, pr, ht, bf, tm = (x[0:P, :, :] for x in (logits, probs, hot, before, tmp))

            def wide(v):
                return v.unsqueeze(2).to_broadcast([P, TT, NE])
            for e in range(NE):
                link(V.memset(rank[:, 0, e:e + 1], float(NE - e)))
                link(V.memset(rank[:, 1, e:e + 1], float(e * CP)))
            link(V.memset(ones[:, :], 1.0))
            for c in range(4):
                link(V.memset(junk[:, c::4], float(NE * CP + 128 * c)))
            link(V.tensor_scalar_add(junk[:, :], junk[:, :], pcol[:, :]))
            link(V.tensor_reduce(top, lg, AXX, ALU.max))
            V.tensor_tensor(tm, lg, wide(top), ALU.subtract).then_inc(s_shift, 1)
            dve.wait_ge(s_exp, 1)
            link(V.tensor_reduce(total, pr, AXX, ALU.add))
            link(V.reciprocal(total, total))
            link(V.tensor_tensor(pr, pr, wide(total), ALU.mult))
            link(V.tensor_reduce(top, pr, AXX, ALU.max))
            link(V.tensor_tensor(tm, pr, wide(top), ALU.is_equal))
            link(V.tensor_tensor(tm, tm, rank[0:P, 0:1, :].to_broadcast([P, TT, NE]), ALU.mult))
            link(V.tensor_reduce(pos, tm, AXX, ALU.max))
            link(V.tensor_tensor(ht, tm, wide(pos), ALU.is_equal))
            for e in range(NE):
                last = V.tensor_tensor_scan(before[0:P, :, e], ones[0:P, :], hot[0:P, :, e], 0.0, ALU.mult, ALU.add)
            last.then_inc(s_tot, 1)
            dve.wait_ge(s_off, 1)
            link(V.tensor_copy(offs[0:P, :], p_off[0:P, 0:NE]))
            link(V.tensor_tensor(tm, bf, offs[0:P, :].unsqueeze(1).to_broadcast([P, TT, NE]), ALU.add))
            link(V.tensor_tensor(tm, tm, ht, ALU.mult))
            link(V.tensor_reduce(pos, tm, AXX, ALU.add))
            link(V.tensor_tensor(tm, ht, rank[0:P, 1:2, :].to_broadcast([P, TT, NE]), ALU.mult))
            link(V.tensor_reduce(base, tm, AXX, ALU.add))
            link(V.tensor_scalar(kept, pos, float(C), None, ALU.is_le))
            link(V.tensor_tensor(gate_p[0:P, :], top, kept, ALU.mult))
            link(V.tensor_tensor(dest[0:P, :], base, pos, ALU.add))
            link(V.scalar_tensor_tensor(dest[0:P, :], dest[0:P, :], -1.0, junk[0:P, :], ALU.add, ALU.subtract))
            link(V.tensor_tensor(dest[0:P, :], dest[0:P, :], kept, ALU.mult))
            link(V.tensor_tensor(dest[0:P, :], dest[0:P, :], junk[0:P, :], ALU.add))
            link(V.tensor_scalar(pos, pos, float(C), -1.0, ALU.min, ALU.add))
            link(V.tensor_tensor(slot_g[0:P, :], base, pos, ALU.add))

            def stage(t, c):
                if again(t, 4):
                    dve.wait_ge(s_sc[c], 4 * (t - c))
                V.tensor_copy(dslot[0:P, c:c + 1], dest[0:P, bass.ds(t, 1)]).then_inc(s_slot, 1)
                V.tensor_copy(rowst[0:P, c:c + 1, :], keep[0:P, bass.ds(t, 1), :]).then_inc(s_stage, 1)
            pipeline(dve, stage, TT, 0, TT - 1, 0, 4)

        @block.gpsimd
        def _(pool):
            def scatter(t, c):
                pool.wait_ge(s_slot, t + 1)
                pool.wait_ge(s_stage, t + 1)
                pool.sem_inc(s_turn)
                pool.indirect_dma_start(buf, bass.IndirectOffsetOnAxis(dslot[0:P, c:c + 1], 0),
                                        rowst[0:P, c, :], None).then_inc(s_sc[c], 16)
            pipeline(pool, scatter, TT, 0, TT - 1, 0, 4)
            for c in range(4):
                pool.wait_ge(s_sc[c], 16 * ((TT - c + 3) // 4))

        @block.sync
        def _(sp):
            sp.dma_start(ex.b1r[:, :], a["L0_ffn_b1"].rearrange("e (f p) -> (e f) p", p=128)).then_inc(ex.s_b1, 16)
            for e in range(2):
                ex.load(sp, e, e)


class Expert:

    def __init__(self, a, sem, sb, scope):
        self.a = a
        self.w1 = sb(scope, "w1", [128, 2, 2, NF])
        self.w2 = sb(scope, "w2", [128, 2, NF // 128, D])
        self.b2 = sb(scope, "b2", [128, 2, D])
        self.b1r = sb(scope, "b1r", [NE * NF // 128, 128])
        self.s_b1 = sem("x_b1")
        self.s_w = [sem(f"x_w{b}") for b in range(2)]

    def load(self, sp, e, b):
        w1_d = self.a["L0_ffn_w1"].rearrange("e (k p) f -> p e k f", p=128)
        w2_d = self.a["L0_ffn_w2"].rearrange("e (f p) d -> p e f d", p=128)
        sp.dma_start(self.w1[:, b:b + 1, :, :], w1_d[:, bass.ds(e, 1), :, :]).then_inc(self.s_w[b], 16)
        sp.dma_start(self.w2[:, b:b + 1, :, :], w2_d[:, bass.ds(e, 1), :, :]).then_inc(self.s_w[b], 16)
        sp.dma_start(self.b2[:, b:b + 1, :], self.a["L0_ffn_b2"][bass.ds(e, 1), :].unsqueeze(0).to_broadcast([128, 1, D])
                     ).then_inc(self.s_w[b], 16)


def experts(nc, ex, sem, sb, ps, buf, ybuf, ident):
    J = CP // 128
    F = NF // 128
    with ExitStack() as st:
        w1, w2, b2, b1r, s_b1, s_w = ex.w1, ex.w2, ex.b2, ex.b1r, ex.s_b1, ex.s_w
        tok = sb(st, "tok", [128, J, D])
        tokT = sb(st, "tokT", [128, 2, CP])
        hT = sb(st, "hT", [128, F, CP])
        y = sb(st, "y", [128, J, D])
        b1T = sb(st, "b1T", [128, NE * F])
        b1c = sb(st, "b1c", [128, F])
        p_t = ps(st, "p_t", [128, 2, 512])
        p_h = ps(st, "p_hid", [128, 4, 512])
        p_y = ps(st, "p_y", [128, 2, 512])

        s_b1T = sem("x_b1T")
        s_b1c = sem("x_b1c")
        s_tok = sem("x_tok")
        s_T = sem("x_T")
        s_Tc = sem("x_Tc")
        s_h = sem("x_h")
        s_hr = sem("x_hr")
        s_y = sem("x_y")
        s_yc = sem("x_yc")
        s_st = sem("x_st")
        tok_d = buf[0:NE * CP, :].rearrange("(e p j) d -> p e j d", p=128, j=J)
        y_d = ybuf.rearrange("(e p j) d -> p e j d", p=128, j=J)
        GH = 2 * F

        def past(e):
            return not isinstance(e, int) or e >= 0

        block = st.enter_context(nc.Block())

        @block.sync
        def _(sp):
            def load(e, b):
                if not isinstance(e, int) or e:
                    sp.wait_ge(s_T, 4 * e)
                sp.dma_start(tok[:, :, :].unsqueeze(1), tok_d[:, bass.ds(e, 1), :, :]).then_inc(s_tok, 16)
                if again(e):
                    sp.wait_ge(s_yc, J * (e - 1))
                    ex.load(sp, e, b)
            pipeline(sp, load, NE, 0, NE - 1, 0)

        @block.gpsimd
        def _(pool):
            with pool.Fori(0, NE) as e:
                pool.wait_ge(s_yc, J * e + J)
                pool.dma_start(y_d[:, bass.ds(e, 1), :, :], y[:, :, :].unsqueeze(1)).then_inc(s_st, 16)
            pool.wait_ge(s_st, 16 * NE)

        @block.scalar
        def _(act):
            act.wait_ge(s_b1T, 2)

            def hidden(e, b, first):
                act.wait_ge(s_b1c, e + 1)
                if not first:
                    act.wait_ge(s_y, J * e)
                for g in range(GH):
                    f, half = g // 2, g % 2
                    act.wait_ge(s_h, GH * e + g + 1)
                    nc.scalar.activation(hT[:, f, half * 512:(half + 1) * 512], p_h[:, g % 4, :], ACT.Relu,
                                         bias=b1c[:, f:f + 1]).then_inc(s_hr, 1)
            hidden(0, 0, True)
            with act.Fori(1, NE) as e:
                hidden(e, 0, False)

        @block.vector
        def _(dve):
            dve.wait_ge(s_b1T, 1)
            nc.vector.tensor_copy(b1T[:, :], p_t[:, 0, 0:NE * F]).then_inc(s_b1T, 1)
            dve.wait_ge(s_b1T, 2)

            def step(s, b):
                e = s + 1
                if live(e, NE):
                    if past(s):
                        dve.wait_ge(s_hr, GH * e)
                    nc.vector.tensor_copy(b1c[:, :], b1T[:, bass.ds(F * e, F)]).then_inc(s_b1c, 1)
                    for q in range(4):
                        dve.wait_ge(s_T, 4 * e + q + 1)
                        if q == 0 and past(s):
                            dve.wait_ge(s_h, GH * e)
                        nc.vector.tensor_copy(tokT[:, q // 2, (q % 2) * 512:(q % 2 + 1) * 512], p_t[:, q % 2, :]
                                              ).then_inc(s_Tc, 1)
                if live(s, NE):
                    if past(s - 1):
                        dve.wait_ge(s_st, 16 * s)
                    dve.wait_ge(s_w[b], 24 * (s - b) + 48)
                    for j in range(J):
                        dve.wait_ge(s_y, J * s + j + 1)
                        nc.vector.tensor_tensor(y[:, j, :], p_y[:, j % 2, 0:D], b2[:, b, :], ALU.add).then_inc(s_yc, 1)
            pipeline(dve, step, NE, -1, NE - 1, 0)

        @block.tensor
        def _(pe):
            pe.wait_ge(s_b1, 16)
            nc.tensor.transpose(p_t[:, 0, 0:NE * F], b1r[:, :], ident[0:NE * F, 0:NE * F]).then_inc(s_b1T, 1)
            pe.wait_ge(s_b1T, 2)

            def transposes(e):
                pe.wait_ge(s_tok, 16 * e + 16)
                for q in range(4):
                    if q >= 2 or past(e - 1):
                        pe.wait_ge(s_Tc, 4 * e + q - 1)
                    for r in range(4):
                        last = nc.tensor.transpose(p_t[:, q % 2, r * 128:(r + 1) * 128],
                                                   tok[:, (q % 2) * 4 + r, (q // 2) * 128:(q // 2 + 1) * 128],
                                                   ident[:, :])
                    last.then_inc(s_T, 1)

            def step(s, b):
                if live(s, NE):
                    pe.wait_ge(s_w[b], 24 * (s - b) + 48)
                    pe.wait_ge(s_Tc, 4 * s + 4)
                    for g in range(GH):
                        f, half = g // 2, g % 2
                        if g >= 4 or past(s - 1):
                            pe.wait_ge(s_hr, GH * s + g - 3)
                        for k in range(2):
                            last = nc.tensor.matmul(p_h[:, g % 4, :], w1[:, b, k, f * 128:(f + 1) * 128],
                                                    tokT[:, k, half * 512:(half + 1) * 512],
                                                    start=(k == 0), stop=(k == 1))
                        last.then_inc(s_h, 1)
                if live(s + 1, NE):
                    transposes(s + 1)
                if live(s, NE):
                    pe.wait_ge(s_hr, GH * s + GH)
                    for j in range(J):
                        if j >= 2 or past(s - 1):
                            pe.wait_ge(s_yc, J * s + j - 1)
                        for f in range(F):
                            last = nc.tensor.matmul(p_y[:, j % 2, 0:D], hT[:, f, j * 128:(j + 1) * 128],
                                                    w2[:, b, f, :], start=(f == 0), stop=(f == F - 1))
                        last.then_inc(s_y, 1)
            pipeline(pe, step, NE, -1, NE - 1, 0)


def finish(nc, sem, sb, ybuf, x_sb, slot_g, gate_p, out):
    NP = TT // 2
    BIG = 3.4028234e38
    with ExitStack() as st:
        islot = sb(st, "islot", [128, 4, 2], I32)
        yg = sb(st, "yg", [128, 4, 2, D])
        sc = sb(st, "sc", [128, 4, 2, D])
        above = sb(st, "above", [128, 2, 2, D])
        inf = sb(st, "inf", [128, 2, 2, D])
        odd = sb(st, "odd", [128, 2, 2, D])
        sub = sb(st, "sub", [128, 2, 2, D])
        s_i = sem("f_i")
        s_turn = sem("f_turn")
        s_g = [sem(f"f_g{c}") for c in range(4)]
        s_y = sem("f_y")
        s_above = sem("f_above")
        s_inf = sem("f_inf")
        s_odd = sem("f_odd")
        s_sub = sem("f_sub")
        s_fix = sem("f_fix")
        s_x = sem("f_x")
        s_out = sem("f_out")
        rows = out.rearrange("(p t) d -> p t d", t=TT)
        block = st.enter_context(nc.Block())

        @block.gpsimd
        def _(pool):
            def gather(t, c):
                pool.wait_ge(s_i, t + 1)
                pool.sem_inc(s_turn)
                for k in range(2):
                    pool.indirect_dma_start(yg[0:P, c, k, :], None, ybuf,
                                            bass.IndirectOffsetOnAxis(islot[0:P, c, k:k + 1], 0)
                                            ).then_inc(s_g[c], 16)
            pipeline(pool, gather, NP, 0, NP - 1, 0, 4)

        @block.scalar
        def _(act):
            def step(s, c):
                b = c % 2
                if live(s, NP):
                    act.wait_ge(s_g[c], 8 * (s - c) + 32)
                    if again(s, 4):
                        act.wait_ge(s_x, s - 3)
                    for k in range(2):
                        nc.scalar.activation(sc[0:P, c, k:k + 1, :], yg[0:P, c, k:k + 1, :], ACT.Copy,
                                             scale=gate_p[0:P, bass.ds(2 * s + k, 1)]).then_inc(s_y, 1)
                t = s - 1
                if live(t, NP):
                    act.wait_ge(s_inf, t + 1)
                    if again(t):
                        act.wait_ge(s_fix, t - 1)
                    nc.scalar.mul(sub[0:P, 1 - b, :, :], inf[0:P, 1 - b, :, :], -1e4).then_inc(s_sub, 1)
                if live(s, NP):
                    act.wait_ge(s_y, 2 * s + 2)
                    if again(s):
                        act.wait_ge(s_fix, s - 1)
                    nc.scalar.activation(odd[0:P, b, :, :], sc[0:P, c, :, :], ACT.Square, scale=0.0).then_inc(s_odd, 1)
            pipeline(act, step, NP, 0, NP, 1, 4)

        @block.vector
        def _(dve):
            def step(s, c):
                b = c % 2
                t = s + 3
                if live(t, NP):
                    if again(t, 4):
                        dve.wait_ge(s_y, 2 * t - 6)
                    nc.vector.tensor_copy(islot[0:P, (c + 3) % 4, :], slot_g[0:P, bass.ds(2 * t, 2)]).then_inc(s_i, 1)
                if live(s, NP):
                    dve.wait_ge(s_y, 2 * s + 2)
                    if again(s):
                        dve.wait_ge(s_inf, s - 1)
                        dve.wait_ge(s_sub, s - 1)
                    nc.vector.tensor_single_scalar(above[0:P, b, :, :], sc[0:P, c, :, :], BIG, ALU.is_gt
                                                   ).then_inc(s_above, 1)
                    dve.wait_ge(s_above, s + 1)
                    nc.vector.scalar_tensor_tensor(inf[0:P, b, :, :], sc[0:P, c, :, :], -BIG, above[0:P, b, :, :],
                                                   ALU.is_lt, ALU.subtract).then_inc(s_inf, 1)
                t = s - 1
                if live(t, NP):
                    dve.wait_ge(s_odd, t + 1)
                    dve.wait_ge(s_sub, t + 1)
                    dve.sem_inc(s_turn)
                    nc.vector.copy_predicated(sc[0:P, (c - 1) % 4, :, :].rearrange("p k d -> p (k d)"),
                                              odd[0:P, 1 - b, :, :].rearrange("p k d -> p (k d)").bitcast(I32),
                                              sub[0:P, 1 - b, :, :].rearrange("p k d -> p (k d)")).then_inc(s_fix, 1)
                    dve.wait_ge(s_fix, t + 1)
                    nc.vector.tensor_tensor(x_sb[0:P, bass.ds(2 * t, 2), :], x_sb[0:P, bass.ds(2 * t, 2), :],
                                            sc[0:P, (c - 1) % 4, :, :], ALU.add).then_inc(s_x, 1)
            pipeline(dve, step, NP, -3, NP, 1, 4)

        @block.sync
        def _(sp):
            with sp.Fori(0, NP) as i:
                sp.wait_ge(s_x, i + 1)
                for r in SPLIT:
                    sp.dma_start(rows[r, bass.ds(2 * i, 2), :], x_sb[r, bass.ds(2 * i, 2), :]).then_inc(s_out, 16)
            sp.wait_ge(s_out, 32 * NP)


_NAMES = ["x", "src", "dst", "L0_gnn_W1_1", "L0_gnn_b1_1", "L0_gnn_W2_1", "L0_gnn_b2_1", "L0_gnn_W1_2",
          "L0_gnn_b1_2", "L0_gnn_W2_2", "L0_gnn_b2_2", "L0_gnn_Wo", "L0_gnn_bo", "L0_gnn_Wr", "L0_gnn_br",
          "L0_mix_wq", "L0_mix_bo", "L0_mix_ln_k_g", "L0_mix_ln_k_b", "L0_mix_ln_v_g", "L0_mix_ln_v_b",
          "L0_ffn_gate_w", "L0_ffn_gate_b", "L0_ffn_w1", "L0_ffn_b1", "L0_ffn_w2", "L0_ffn_b2"]
_TRANSPOSED = {"wkT": "L0_mix_wk", "wvT": "L0_mix_wv", "woT": "L0_mix_wo"}


def kernel(**inputs):
    import numpy as np
    import concourse.bacc as bacc
    from concourse.bass_utils import run_bass_kernel_spmd

    nc = bacc.Bacc("TRN2", target_bir_lowering=False, num_devices=1)
    arrays = {n: np.ascontiguousarray(inputs[n]) for n in _NAMES}
    arrays |= {n: np.ascontiguousarray(np.asarray(inputs[m]).T) for n, m in _TRANSPOSED.items()}
    a = {n: nc.dram_tensor("in_" + n, v.shape, mybir.dt.from_np(v.dtype), kind="ExternalInput").ap()
         for n, v in arrays.items()}
    out = nc.dram_tensor("out", (N, D), F32, kind="ExternalOutput").ap()
    graph_moe_kernel(nc, a, out)
    r = run_bass_kernel_spmd(nc, [{"in_" + n: v for n, v in arrays.items()}], core_ids=[0])
    return r.results[0]["out"]
```
